# Optimizing a Trainium2 kernel written in Bass

```python
import numpy as np
import jax
import jax.numpy as jnp

def _softmax(x, axis=-1):
    return jax.nn.softmax(x, axis=axis)

def _gelu(x):
    return jax.nn.gelu(x, approximate=True)

def _silu(x):
    return jax.nn.silu(x)

def _sigmoid(x):
    return jax.nn.sigmoid(x)

def _layernorm(x, axis=-1, eps=1e-05):
    m = jnp.mean(x, axis=axis, keepdims=True)
    v = jnp.var(x, axis=axis, keepdims=True)
    return (x - m) / jnp.sqrt(v + eps)

def _scatter_add(tgt, idx, src, axis=0):
    return tgt.at[idx].add(src)

def _segment_sum(src, seg, n):
    return jax.ops.segment_sum(src, seg, n)
kernel_name = 'mk_xattn_ffn_d1_seqx_r4_bb3585'

def setup_inputs(seed: int=0):
    np.random.seed(seed)
    _w = jnp.asarray

    def _rec_inputs():
        import jax
        import jax.numpy as jnp
        _rk = jax.random.key(seed)
        x = 0.0003765 + 1 * jax.random.normal(jax.random.fold_in(_rk, 1), (8, 256, 512), jnp.float32)
        _lenS = 256 - jax.random.randint(jax.random.fold_in(_rk, 7), (8,), 0, max(1, 256 // 4) + 1, jnp.int32)
        _lenS2 = 256 - jax.random.randint(jax.random.fold_in(_rk, 8), (8,), 0, max(1, 256 // 4) + 1, jnp.int32)
        _ctx_2048P = jax.random.normal(jax.random.fold_in(_rk, 11), (8, 16, 512), jnp.float32)
        _ctx_2048c = jax.random.dirichlet(jax.random.fold_in(_rk, 511), 0.3 * jnp.ones((16,), jnp.float32), (8, 256))
        _ctx_2048t = jnp.einsum('bsk,bkd->bsd', _ctx_2048c, _ctx_2048P)
        _ctx_2048t = _ctx_2048t * jax.lax.rsqrt(jnp.mean(jnp.square(_ctx_2048t)) + 1e-12) * 0.953939
        ctx_2048 = -0.000292821 + 1.00034 * (_ctx_2048t + 0.3 * jax.random.normal(jax.random.fold_in(_rk, 611), (8, 256, 512), jnp.float32))
        return (x, ctx_2048)
    x, ctx_2048 = _rec_inputs()

    def _L0_xattn_setup():
        import jax, jax.numpy as jnp
        import numpy as np
        key = jax.random.key(seed)
        k1, k2, k3, k4, k5 = jax.random.split(key, 5)
        B, D_MODEL, L = (2, 256, 512)
        HEAD_DIM = 8
        H = D_MODEL // HEAD_DIM
        return {'k': jax.random.normal(k1, (B, D_MODEL, L), dtype=jnp.float32), 'v': jax.random.normal(k2, (B, D_MODEL, L), dtype=jnp.float32), 'q': jax.random.normal(k3, (B, D_MODEL, L), dtype=jnp.float32), 'ssm_kernel': jax.random.normal(k4, (H, L), dtype=jnp.float32), 'D': jax.random.normal(k5, (H,), dtype=jnp.float32), 'head_dim': HEAD_DIM}
    _L0_xattn_all = _L0_xattn_setup()
    _L0_xattn_in = {k: v for k, v in _L0_xattn_all.items() if k in ('ssm_kernel', 'D')}
    del _L0_xattn_all

    def _L0_ffn_setup():
        import jax, jax.numpy as jnp
        import numpy as np
        B, S, H = (1, 512, 512)
        E, K, I = (16, 4, 352)
        IS = 704
        CAP = 256
        key = jax.random.key(seed)
        ks = jax.random.split(key, 8)
        sc = 0.02
        return {'hidden_states': jax.random.normal(ks[0], (B, S, H), jnp.float32), 'gate_w': jax.random.normal(ks[1], (E, H), jnp.float32) * sc, 'w_gate': jax.random.normal(ks[2], (E, H, I), jnp.float32) * sc, 'w_up': jax.random.normal(ks[3], (E, H, I), jnp.float32) * sc, 'w_down': jax.random.normal(ks[4], (E, I, H), jnp.float32) * sc, 'sw_gate': jax.random.normal(ks[5], (H, IS), jnp.float32) * sc, 'sw_up': jax.random.normal(ks[6], (H, IS), jnp.float32) * sc, 'sw_down': jax.random.normal(ks[7], (IS, H), jnp.float32) * sc}
    _L0_ffn_all = _L0_ffn_setup()
    _L0_ffn_in = {k: v for k, v in _L0_ffn_all.items() if k in ('gate_w', 'w_gate', 'w_up', 'w_down', 'sw_gate', 'sw_up', 'sw_down')}
    del _L0_ffn_all
    return {'x': x, 'ctx_2048': ctx_2048, 'L0_xattn_ssm_kernel': _L0_xattn_in['ssm_kernel'], 'L0_xattn_D': _L0_xattn_in['D'], 'L0_ffn_gate_w': _L0_ffn_in['gate_w'], 'L0_ffn_w_gate': _L0_ffn_in['w_gate'], 'L0_ffn_w_up': _L0_ffn_in['w_up'], 'L0_ffn_w_down': _L0_ffn_in['w_down'], 'L0_ffn_sw_gate': _L0_ffn_in['sw_gate'], 'L0_ffn_sw_up': _L0_ffn_in['sw_up'], 'L0_ffn_sw_down': _L0_ffn_in['sw_down']}

def reference(x, ctx_2048, L0_xattn_ssm_kernel, L0_xattn_D, L0_ffn_gate_w, L0_ffn_w_gate, L0_ffn_w_up, L0_ffn_w_down, L0_ffn_sw_gate, L0_ffn_sw_up, L0_ffn_sw_down):
    import jax
    import jax.numpy as jnp

    def _L0_xattn_ref(k, v, q, ssm_kernel, D, head_dim):
        import jax, jax.numpy as jnp
        import numpy as np
        B, HD, L = k.shape
        H = HD // head_dim
        fft_size = 2 * L
        k_ = k.reshape(B, H, head_dim, L)
        v_ = v.reshape(B, H, head_dim, L)
        q_ = q.reshape(B, H, head_dim, L)
        kv = jnp.einsum('bhil,bhjl->bijhl', k_, v_)
        kv_f = jnp.fft.rfft(kv, n=fft_size)
        kernel_f = jnp.fft.rfft(ssm_kernel, n=fft_size)
        y = jnp.fft.irfft(kv_f * kernel_f, n=fft_size)[..., :L]
        out = y + kv * D[None, None, None, :, None]
        out = jnp.einsum('bijhl,bhil->bjhl', out, q_)
        out = jnp.transpose(out, (0, 2, 1, 3)).reshape(B, H * head_dim, L)
        return out.astype(k.dtype)

    def _L0_ffn_ref(hidden_states, gate_w, w_gate, w_up, w_down, sw_gate, sw_up, sw_down):
        import jax, jax.numpy as jnp
        import numpy as np
        B, S, H = (1, 512, 512)
        E, K, I = (16, 4, 352)
        IS = 704
        CAP = 256
        b, s, h = hidden_states.shape
        x = hidden_states.reshape(-1, h)
        T = x.shape[0]
        scores = jax.nn.softmax(x @ gate_w.T, axis=-1)
        topk_w, topk_i = jax.lax.top_k(scores, K)
        topk_w = topk_w / (topk_w.sum(-1, keepdims=True) + 1e-20)
        flat_i = topk_i.reshape(-1)
        flat_w = topk_w.reshape(-1)
        order = jnp.argsort(flat_i)
        se = flat_i[order]
        counts = jax.ops.segment_sum(jnp.ones_like(flat_i), flat_i, num_segments=E)
        starts = jnp.cumsum(counts) - counts
        rank = jnp.arange(T * K) - starts[se]
        tok = order // K
        slot = jnp.where(rank < CAP, rank, CAP)
        buf = jnp.full((E, CAP + 1), T, dtype=jnp.int32).at[se, slot].set(tok)[:, :CAP]
        wbuf = jnp.zeros((E, CAP + 1), x.dtype).at[se, slot].set(flat_w[order])[:, :CAP]
        xpad = jnp.concatenate([x, jnp.zeros((1, h), x.dtype)], axis=0)
        xg = xpad[buf]
        gact = jax.nn.silu(jnp.einsum('ech,ehi->eci', xg, w_gate))
        mid = gact * jnp.einsum('ech,ehi->eci', xg, w_up)
        eout = jnp.einsum('eci,eih->ech', mid, w_down) * wbuf[..., None]
        y = jnp.zeros((T + 1, h), x.dtype).at[buf.reshape(-1)].add(eout.reshape(-1, h))[:T]
        shared = jax.nn.silu(x @ sw_gate) * (x @ sw_up) @ sw_down
        return (y + shared).reshape(b, s, h)
    x = x + _L0_xattn_ref(ctx_2048, ctx_2048, _layernorm(x, axis=-1), L0_xattn_ssm_kernel, L0_xattn_D, 8)
    x = x + _L0_ffn_ref(_layernorm(x, axis=-1), L0_ffn_gate_w, L0_ffn_w_gate, L0_ffn_w_up, L0_ffn_w_down, L0_ffn_sw_gate, L0_ffn_sw_up, L0_ffn_sw_down)
    return x

_drawn_inputs = setup_inputs


def setup_inputs(seed=0):
    import zlib

    import numpy as np

    out = dict(_drawn_inputs(seed))
    spreads = {}
    factors = {'L0_ffn_gate_w': 8.0,
     'L0_ffn_w_gate': 8.0,
     'L0_ffn_w_up': 8.0,
     'L0_ffn_w_down': 8.0,
     'L0_ffn_sw_gate': 8.0,
     'L0_ffn_sw_up': 8.0,
     'L0_ffn_sw_down': 8.0}
    for name, (base, spread) in spreads.items():
        noise = np.random.default_rng([zlib.crc32(name.encode()), seed]).standard_normal(out[name].shape)
        drawn = base * np.exp(spread * noise) if base else spread * noise
        out[name] = jnp.asarray(drawn.astype(out[name].dtype))
    for name, factor in factors.items():
        out[name] = (out[name] * factor).astype(out[name].dtype)
    return out
```

```python
import concourse.bass as bass
from concourse import mybir
from contextlib import ExitStack

fp32 = mybir.dt.float32
fp32r = mybir.dt.float32r
bf16 = mybir.dt.bfloat16
int32 = mybir.dt.int32
ALU = mybir.AluOpType
ACT = mybir.ActivationFunctionType
AX = mybir.AxisListType

P = 128
PASSES = ((0, 0), (0, 1), (1, 0))


def wait(eng, sem, value):
    if not (isinstance(value, int) and value <= 0):
        eng.wait_ge(sem, value)


def xattn_moe_kernel(nc, x, ctx, taps, skip, gate_w, w_gate, w_up, w_down, sw_gate, sw_up, sw_down, out):
    B, ROWS, L = x.shape
    H = taps.shape[0]
    HD = ROWS // H
    E, _, I = w_gate.shape
    IS = sw_gate.shape[1]
    CAP, TOPK, EPS = 256, 4, 1e-5
    T = B * ROWS
    LB = L // P
    GH = 4
    GR = GH * HD
    NG = H // GH
    TR = P // B
    TT = GR // TR
    GT = TT * P
    PAIRS = HD * (HD + 1) // 2
    PW = PAIRS * B
    POFF = [B * sum(HD - d for d in range(s)) for s in range(HD + 1)]
    TW = P + L
    SJ = -(-IS // P)
    SK = [min(P, IS - j * P) for j in range(SJ)]
    EJ = -(-I // P)
    EK = [min(P, I - j * P) for j in range(EJ)]
    HALVES = CAP // P
    NT = NG * TT
    TE = NT * E
    FAR = float(1 << 20)

    toep_dram = nc.dram_tensor("toeplitz_taps", [H, 2, TW], fp32).ap()
    xn_dram = nc.dram_tensor("normalised_tokens", [T, L], fp32).ap()
    x_g = x.rearrange("b (g t r) l -> g t r b l", t=TT, r=TR)
    c_g = ctx.rearrange("b (g t r) l -> g t r b l", t=TT, r=TR)
    xn_g = xn_dram.rearrange("(b g t r) l -> g t r b l", b=B, t=TT, r=TR)
    out_g = out.rearrange("b (g t r) l -> g t r b l", t=TT, r=TR)
    out_rows = out.rearrange("b r l -> (b r) l")
    wg_e = w_gate.rearrange("e (c p) i -> e p c i", p=P)
    wu_e = w_up.rearrange("e (c p) i -> e p c i", p=P)

    es = ExitStack()
    with es:
        def sem(name):
            return es.enter_context(nc.semaphore(name))

        arena_bytes = (nc.sbuf_bytes_remaining - 256) // 32 * 32
        arena = es.enter_context(nc.sbuf_tensor("arena", [P, arena_bytes // 4], fp32))
        arena_base = nc.sbuf_base - arena_bytes
        cursor = [arena_base]

        def place(name, shape, dt):
            size = 1
            for n in shape[1:]:
                size *= n
            size = -(-size * (2 if dt == bf16 else 4) // 32) * 32
            t = nc.alloc_sbuf_tensor_at(name, shape, dt, offset=cursor[0])
            cursor[0] += size
            assert cursor[0] <= arena_base + arena_bytes, (name, cursor[0])
            return t

        ident = place("ident", [P, P], fp32)
        same_b = place("same_b", [P, P], bf16)
        before_in_b = place("before_in_b", [P, P], bf16)
        earlier_b = place("earlier_b", [P, P], bf16)
        later_row = place("later_row", [P, P], bf16)
        col_i = place("col_i", [P, P], int32)
        colmod_i = place("colmod_i", [P, P], int32)
        row_i = place("row_i", [P, 3], int32)
        row_f = place("row_f", [P, 3], fp32)
        iota_i = place("iota_i", [P, CAP], int32)
        iota_c = place("iota_c", [P, CAP], bf16)
        tok_i = place("tok_i", [P, TE], int32)
        carrier = place("carrier", [P, 3], fp32)
        carrier_d = place("carrier_d", [P, 2], fp32)
        half_neg = place("half_neg", [P, TT], fp32)
        gwT = place("gwT", [P, LB, 2, E], fp32r)
        logits = place("logits", [P, NG, TT * E], fp32)
        xstat = place("xstat", [P, TT, 6], fp32)
        xmv = place("xmv", [P, TT, 2], fp32)
        xve = place("xve", [P, TT], fp32)
        xrs = place("xrs", [P, TT], fp32)
        tstat = place("tstat", [P, TT, 6], fp32)
        tmv = place("tmv", [P, TT, 2], fp32)
        tve = place("tve", [P, TT], fp32)
        trs = place("trs", [P, TT], fp32)
        shared_at = cursor[0]
        sw = place("sw", [P, LB, 2, 2 * IS], fp32r)
        sd = place("sd", [P, SJ, 2, L], fp32r)
        xT = place("xT", [P, LB, 2, GT], fp32r)
        sil = place("sil", [P, 2, CAP], fp32)
        mid = place("mid", [P, 2, CAP], fp32)
        stage_at = cursor[0]
        midh = place("midh", [P, SJ, CAP], fp32r)
        midl = place("midl", [P, SJ, CAP], fp32r)
        ffn_end = cursor[0]
        cursor[0] = stage_at
        sw_raw = place("sw_raw", [P, 2, 2 * IS], fp32)
        cursor[0] = ffn_end
        yo = place("yo", [P, TT, L], fp32)
        x1 = place("x1", [P, 2, TT, L], fp32)
        xn = place("xn", [P, TT, L], fp32)
        zone = cursor[0]
        x_t = place("x_t", [P, 3, TT, L], fp32)
        c_t = place("c_t", [P, TT, L], fp32)
        xq = place("xq", [P, TT, L], fp32)
        kT = place("kT", [P, 2, LB, GR * B], fp32)
        qT = place("qT", [P, 2, LB, GR * B], fp32)
        kv = place("kv", [P, 2, LB, PW], fp32)
        kvh = place("kvh", [P, 2, LB, PW], fp32r)
        kvl = place("kvl", [P, 2, LB, PW], fp32r)
        toep = [place(f"toep{n}", [P, 2, L], fp32r) for n in range(2)]
        oT = place("oT", [P, LB, GR * B], fp32)
        prod_at = cursor[0]
        prod = place("prod", [P, 2, LB, HD, HD * B], fp32)
        cursor[0] = prod_at
        tap_rows = place("tap_rows", [H, L], fp32)
        pad = place("pad", [H, TW], fp32)
        padhl = place("padhl", [H, 2, TW], fp32r)
        skip_t = place("skip_t", [H, 1], fp32)
        gate_rows = place("gate_rows", [E, L], fp32)
        cursor[0] = zone
        ew0 = place("ew0", [P, LB, 2, 2 * I], fp32r)
        ed0 = place("ed0", [P, EJ, 2, L], fp32r)
        raw_w0 = place("raw_w0", [P, LB, 2 * I], fp32)
        raw_d0 = place("raw_d0", [P, EJ, L], fp32)
        xg = [place(f"xg{k}", [P, HALVES, L], fp32) for k in range(2)]
        onehot = place("onehot", [P, NT, CAP], bf16)
        routing_at = cursor[0]
        cursor[0] = shared_at
        raw_w = [raw_w0, place("raw_w1", [P, LB, 2 * I], fp32)]
        raw_d = [raw_d0, place("raw_d1", [P, EJ, L], fp32)]
        ew = [ew0, place("ew1", [P, LB, 2, 2 * I], fp32r)]
        assert raw_w[1] is not None and cursor[0] <= shared_at + LB * 4 * IS * 4
        ed = [ed0, place("ed1", [P, EJ, 2, L], fp32r)]
        xgT = [xT, place("xgT1", [P, LB, 2, CAP], fp32r)]
        cursor[0] = routing_at
        PADW = E + 8
        scp = place("scp", [P, NT, PADW], fp32)
        rep = place("rep", [P, NT, PADW], fp32)
        top8 = place("top8", [P, NT, 8], fp32)
        r_max = place("r_max", [P, NT], fp32)
        r_sum = place("r_sum", [P, NT], fp32)
        r_rec = place("r_rec", [P, NT], fp32)
        chosen = place("chosen", [P, TE], fp32)
        chosen_b = place("chosen_b", [P, TE], bf16)
        run = place("run", [P, TE], fp32)
        excl_b = place("excl_b", [P, TE], bf16)
        tot_b = place("tot_b", [P, TE], bf16)
        reset = place("reset", [P, TE], fp32)
        rank = place("rank", [P, TE], fp32)
        wt = place("wt", [P, TE], fp32)
        wtmp = place("wtmp", [P, TE], fp32)
        V = place("V", [P, TE, 6], bf16)
        slot_f = place("slot_f", [P, HALVES, 6], fp32)
        slot_a = place("slot_a", [P, HALVES], fp32)
        slot_b = place("slot_b", [P, HALVES], fp32)
        idx_g = [place(f"idx_g{k}", [P, HALVES], int32) for k in range(2)]
        idx_s = [place(f"idx_s{k}", [P, HALVES], int32) for k in range(2)]
        wts_g = [place(f"wts_g{k}", [P, HALVES], fp32) for k in range(2)]
        wts_s = [place(f"wts_s{k}", [P, HALVES], fp32) for k in range(2)]

        yb = es.enter_context(nc.psum_tensor("yb", [P, LB, 512], fp32))
        gu = es.enter_context(nc.psum_tensor("gu", [P, 2, 512], fp32))
        mb = es.enter_context(nc.psum_tensor("mb", [P, 2, 512], fp32))

        taps_in, taps_out = sem("taps_in"), sem("taps_out")
        gate_in = sem("gate_in")
        swraw_in = [sem("swraw_in0"), sem("swraw_in1")]
        group_in = sem("group_in")
        toep_in = [sem("toep_in0"), sem("toep_in1")]
        xn_out, out_out = sem("xn_out"), sem("out_out")
        raw_in = [sem("raw_in0"), sem("raw_in1")]
        rows_in = [sem("rows_in0"), sem("rows_in1")]
        added = sem("added")
        consts = sem("consts")
        pad_ok, skip_ok, taps_hl = sem("pad_ok"), sem("skip_ok"), sem("taps_hl")
        gate_t, gate_h, gate_l = sem("gate_t"), sem("gate_h"), sem("gate_l")
        sw_h, sw_l = sem("sw_h"), sem("sw_l")
        x_stat, x_rs, x_nrm = sem("x_stat"), sem("x_rs"), sem("x_nrm")
        c_tr, q_tr = sem("c_tr"), sem("q_tr")
        k_ev, q_ev = sem("k_ev"), sem("q_ev")
        kv_m, kv_h, kv_l = sem("kv_m"), sem("kv_h"), sem("kv_l")
        conv = sem("conv")
        d_mul, d_sum = sem("d_mul"), sem("d_sum")
        o_tr = sem("o_tr")
        x1_ok, t_stat, t_rs, t_nrm = sem("x1_ok"), sem("t_stat"), sem("t_rs"), sem("t_nrm")
        n_tr, n_h, n_l = sem("n_tr"), sem("n_h"), sem("n_l")
        lg_mm, lg_ok = sem("lg_mm"), sem("lg_ok")
        gu_mm, sil_ok, mid_ok, mid_h, mid_l = sem("gu_mm"), sem("sil_ok"), sem("mid_ok"), sem("mid_h"), sem("mid_l")
        dn_mm, dn_ok = sem("dn_mm"), sem("dn_ok")
        rt, rt_exp, rt_mm = sem("rt"), sem("rt_exp"), sem("rt_mm")
        rt_c = sem("rt_c")
        ew_h, ew_l, ed_h, ed_l = sem("ew_h"), sem("ew_l"), sem("ed_h"), sem("ed_l")
        oh_ok, sl_mm, sl_ok, sl_cp = sem("oh_ok"), sem("sl_mm"), sem("sl_ok"), sem("sl_cp")
        chain = sem("chain")
        g_tr, g_h, g_l = sem("g_tr"), sem("g_h"), sem("g_l")
        e_mm, e_sil, e_mid, e_midh, e_midl = sem("e_mm"), sem("e_sil"), sem("e_mid"), sem("e_midh"), sem("e_midl")
        e_dn, e_ok = sem("e_dn"), sem("e_ok")
        xg_zero = sem("xg_zero")
        dec = [sem("dec0"), sem("dec1"), sem("dec2")]
        kept = sem("kept")

        carried = [sem("carried0"), sem("carried1")]
        N_CONST = 10
        SW_PIECES = LB + SJ // 2

        block = es.enter_context(nc.Block())

        @block.sync
        def _(sp):
            def load_group(g):
                for t in range(TT):
                    sp.dma_start(x_t[:, bass.ds(g % 3, 1), t, :].rearrange("p s l -> p (s l)"),
                                 x_g[g, t]).then_inc(group_in, 16)
                    sp.dma_start(c_t[:, t, :], c_g[g, t]).then_inc(group_in, 16)

            def load_toep(n, k):
                h = toep_dram[n]
                src = bass.AP(h.tensor, h.offset, [[1, P], [TW, 2], [1, L]])
                sp.dma_start(toep[k][:].bitcast(fp32), src).then_inc(toep_in[k], 16)

            def load_shared(piece):
                if piece < LB:
                    rows = slice(piece * P, (piece + 1) * P)
                    sp.dma_start(sw_raw[:, piece % 2, 0:IS], sw_gate[rows, :]).then_inc(swraw_in[piece % 2], 16)
                    sp.dma_start(sw_raw[:, piece % 2, IS:2 * IS], sw_up[rows, :]).then_inc(swraw_in[piece % 2], 16)
                else:
                    for h in range(2):
                        j = 2 * (piece - LB) + h
                        sp.dma_start(sw_raw[0:SK[j], piece % 2, h * L:(h + 1) * L],
                                     sw_down[j * P:j * P + SK[j], :]).then_inc(swraw_in[piece % 2], 16)

            def store(dst_g, src, g, done, signal, count):
                for t in range(TT):
                    wait(sp, done, count + t + 1)
                    sp.dma_start(dst_g[g, t], src[:, t, :]).then_inc(signal, 16)

            def steps(g, heads, more, post, store_out, ahead):
                if store_out:
                    store(out_g, yo, g - 3, dn_ok, out_out, TT * (g - 3))
                for hl in range(GH):
                    if heads:
                        n = GH * g + hl
                        if not (isinstance(n, int) and n + 2 >= H):
                            sp.wait_ge(conv, n + 1)
                            load_toep(n + 2, hl % 2)
                    if hl == 1 and post:
                        store(xn_g, xn, g - 1, t_nrm, xn_out, TT * (g - 1))
                    if hl == 1 and ahead:
                        wait(sp, x1_ok, TT * g)
                        wait(sp, c_tr, TT * (g + 2))
                        load_group(g + 2)

            sp.dma_start(tap_rows[:], taps).then_inc(taps_in, 16)
            sp.dma_start(skip_t[:], skip.rearrange("(h a) -> h a", a=1)).then_inc(taps_in, 16)
            load_group(0)
            sp.wait_ge(taps_hl, 1)
            sp.dma_start(toep_dram, padhl[:].bitcast(fp32)).then_inc(taps_out, 16)
            sp.dma_start(gate_rows[:], gate_w).then_inc(gate_in, 16)
            sp.wait_ge(taps_out, 16)
            load_toep(0, 0)
            load_toep(1, 1)
            load_shared(0)
            load_shared(1)
            sp.wait_ge(c_tr, TT)
            load_group(1)
            for piece in range(2, SW_PIECES):
                sp.wait_ge(sw_h, piece - 1)
                sp.wait_ge(sw_l, piece - 1)
                load_shared(piece)
            steps(0, True, True, False, False, True)
            steps(1, True, True, True, False, True)
            steps(2, True, True, True, False, True)
            with sp.Fori(3, NG - 2) as g:
                steps(g, True, True, True, True, True)
            steps(NG - 2, True, True, True, True, False)
            steps(NG - 1, True, False, True, True, False)
            steps(NG, False, False, True, True, False)

            def load_raw(e, k):
                sp.dma_start(raw_w[k][:, :, 0:I], wg_e[e]).then_inc(raw_in[k], 16)
                sp.dma_start(raw_w[k][:, :, I:2 * I], wu_e[e]).then_inc(raw_in[k], 16)
                sp.dma_start(raw_d[k][:, 0:2, :], w_down[e, 0:2 * P, :].rearrange("(j p) l -> p j l", p=P))\
                    .then_inc(raw_in[k], 16)
                sp.dma_start(raw_d[k][0:EK[2], 2, :], w_down[e, 2 * P:I, :]).then_inc(raw_in[k], 16)

            sp.wait_ge(conv, H)
            sp.wait_ge(d_sum, H)
            sp.wait_ge(n_l, TT * NG)
            sp.wait_ge(o_tr, TT * NG)
            sp.wait_ge(x1_ok, TT * NG)
            load_raw(0, 0)
            store(out_g, yo, NG - 2, dn_ok, out_out, TT * (NG - 2))
            sp.wait_ge(gu_mm, SJ * NG)
            load_raw(1, 1)
            store(out_g, yo, NG - 1, dn_ok, out_out, TT * (NG - 1))

            def next_raw(e, k):
                sp.wait_ge(ew_h, LB * (e + 1))
                sp.wait_ge(ew_l, LB * (e + 1))
                sp.wait_ge(ed_h, e + 1)
                sp.wait_ge(ed_l, e + 1)
                load_raw(e + 2, k)

            with sp.Fori(0, E // 2 - 1) as i:
                for k in range(2):
                    next_raw(2 * i + k, k)
            sp.wait_ge(out_out, 16 * TT * NG)
            sp.wait_ge(xn_out, 16 * TT * NG)

        @block.tensor
        def _(pe):
            def transposes(dst, src):
                for c in range(LB):
                    last = pe.transpose(dst[:, c * P:(c + 1) * P], src(c), ident[:])
                return last

            def convolve(n, hl):
                s = hl % 2
                pe.wait_ge(kv_h, n + 1)
                pe.wait_ge(kv_l, n + 1)
                pe.wait_ge(toep_in[s], 16 * ((n - s) // 2 + 1) if isinstance(n, int) else n * 8 + (16 - 8 * s))
                wait(pe, d_mul, n)
                for lb in range(LB):
                    steps = [(m, a, b) for m in range(lb + 1) for a, b in PASSES]
                    for i, (m, a, b) in enumerate(steps):
                        d = (LB - 1 - lb + m) * P
                        rhs = (kvh, kvl)[b]
                        last = pe.matmul(yb[:, lb, 0:PW], toep[s][:, a, d:d + P], rhs[:, s, m, :],
                                         start=(i == 0), stop=(i == len(steps) - 1))
                last.then_inc(conv, 1)

            def prep_ctx(g):
                pe.wait_ge(group_in, 64 * g + 64)
                for t in range(TT):
                    if t == 1:
                        wait(pe, lg_ok, g - 2)
                    wait(pe, dn_ok, TT * (g - 3))
                    wait(pe, n_l, TT * (g - 2))
                    wait(pe, q_ev, TT * (g - 1) + t + 1)
                    transposes(mb[:, t, :], lambda c: c_t[:, t, c * P:(c + 1) * P]).then_inc(c_tr, 1)

            def prep_q(g):
                for t in range(TT):
                    pe.wait_ge(x_nrm, TT * g + t + 1)
                    wait(pe, x1_ok, TT * (g - 2) + t + 1)
                    pe.wait_ge(k_ev, TT * g + t + 1)
                    transposes(mb[:, t, :], lambda c: xq[:, t, (LB - 1 - c) * P:(LB - c) * P]).then_inc(q_tr, 1)

            def mixed_out(g, ev):
                pe.wait_ge(d_sum, GH * (g + 1))
                for t in range(TT):
                    wait(pe, k_ev, TT * ev + t + 1)
                    wait(pe, q_ev, TT * ev - TT + t + 1)
                    wait(pe, dn_ok, TT * (g - 1))
                    wait(pe, n_l, TT * g)
                    wait(pe, lg_ok, g)
                    last = transposes(mb[:, t, :], lambda c: oT[:, LB - 1 - c, t * P:(t + 1) * P])
                    last.then_inc(o_tr, 1)

            def normalised(g, nq):
                for t in range(TT):
                    pe.wait_ge(t_nrm, TT * g + t + 1)
                    wait(pe, q_ev, TT * nq + t + 1)
                    pe.wait_ge(x1_ok, TT * g + t + 1)
                    transposes(mb[:, t, :], lambda c: xn[:, t, c * P:(c + 1) * P]).then_inc(n_tr, 1)

            def router(g):
                pe.wait_ge(n_h, TT * g + TT)
                pe.wait_ge(n_l, TT * g + TT)
                for t in range(TT):
                    for c in range(LB):
                        for a, b in PASSES:
                            last = pe.matmul(mb[:, 1, t * E:(t + 1) * E], xT[:, c, a, t * P:(t + 1) * P],
                                             gwT[:, c, b, :], start=(c == 0 and (a, b) == PASSES[0]),
                                             stop=(c == LB - 1 and (a, b) == PASSES[-1]))
                last.then_inc(lg_mm, 1)

            def gate_up(g, j):
                m = SK[j]
                pe.wait_ge(n_h, TT * g + TT)
                pe.wait_ge(n_l, TT * g + TT)
                wait(pe, mid_ok, SJ * g + max(j - 1, 0))
                for u in range(2):
                    for c in range(LB):
                        for a, b in PASSES:
                            col = u * IS + j * P
                            last = pe.matmul(gu[0:m, j % 2, u * GT:(u + 1) * GT], sw[:, c, a, col:col + m],
                                             xT[:, c, b, :], start=(c == 0 and (a, b) == PASSES[0]),
                                             stop=(c == LB - 1 and (a, b) == PASSES[-1]))
                last.then_inc(gu_mm, 1)

            def down(g, lg):
                pe.wait_ge(mid_h, SJ * g + SJ)
                pe.wait_ge(mid_l, SJ * g + SJ)
                wait(pe, n_l, TT * lg)
                wait(pe, lg_ok, lg)
                for t in range(TT):
                    for j in range(SJ):
                        for a, b in PASSES:
                            lhs = (midh, midl)[a]
                            last = pe.matmul(mb[:, t, :], lhs[0:SK[j], j, t * P:(t + 1) * P], sd[0:SK[j], j, b, :],
                                             start=(j == 0 and (a, b) == PASSES[0]),
                                             stop=(j == SJ - 1 and (a, b) == PASSES[-1]))
                    last.then_inc(dn_mm, 1)

            def steps(g, heads, prep, post, chunk):
                nq = g + 1 if prep else NG - 1
                if heads:
                    convolve(GH * g, 0)
                if prep:
                    prep_ctx(g + 1)
                if chunk:
                    gate_up(g - 2, 0)
                if post:
                    mixed_out(g - 1, nq)
                if chunk:
                    gate_up(g - 2, 1)
                if heads:
                    convolve(GH * g + 1, 1)
                if prep:
                    prep_q(g + 1)
                if chunk:
                    gate_up(g - 2, 2)
                    gate_up(g - 2, 3)
                if heads:
                    convolve(GH * g + 2, 2)
                if chunk:
                    gate_up(g - 2, 4)
                    gate_up(g - 2, 5)
                if post:
                    normalised(g - 1, nq)
                if heads:
                    convolve(GH * g + 3, 3)
                if post:
                    router(g - 1)
                if chunk:
                    down(g - 2, g if post else g - 1)

            pe.wait_ge(consts, N_CONST)
            prep_ctx(0)
            prep_q(0)
            pe.wait_ge(gate_in, 16)
            pe.wait_ge(q_ev, TT)
            for c in range(LB):
                last = pe.transpose(mb[:, 0, c * E:(c + 1) * E], gate_rows[:, c * P:(c + 1) * P], ident[0:E, 0:E])
            last.then_inc(gate_t, 1)
            pe.wait_ge(gate_h, 1)
            pe.wait_ge(gate_l, 1)
            steps(0, True, True, False, False)
            steps(1, True, True, True, False)
            pe.wait_ge(sw_h, SW_PIECES)
            pe.wait_ge(sw_l, SW_PIECES)
            steps(2, True, True, True, True)
            with pe.Fori(3, NG - 1) as g:
                steps(g, True, True, True, True)
            steps(NG - 1, True, False, True, True)
            steps(NG, False, False, True, True)
            for j in range(SJ - 2):
                gate_up(NG - 1, j)
            pe.wait_ge(rt_c, 1)
            for lhs, rhs in ((before_in_b, chosen_b), (same_b, excl_b), (earlier_b, tot_b)):
                last = pe.matmul(yb[:, 0, 0:TE], lhs[:], rhs[:], start=(lhs is before_in_b),
                                 stop=(lhs is earlier_b))
            last.then_inc(rt_mm, 1)
            for j in range(SJ - 2, SJ):
                gate_up(NG - 1, j)
            down(NG - 1, NG)

            def slots(e):
                pe.wait_ge(oh_ok, e + 1)
                wait(pe, sl_cp, e)
                for h in range(HALVES):
                    for t in range(NT):
                        col = e * NT + t
                        last = pe.matmul(yb[:, 2, h * 8:h * 8 + 6], onehot[:, t, h * P:(h + 1) * P],
                                         V[:, bass.ds(col, 1), :].rearrange("p a c -> p (a c)"),
                                         start=(t == 0), stop=(t == NT - 1))
                last.then_inc(sl_mm, 1)

            def rows_t(e, k):
                pe.wait_ge(rows_in[k], 16 * HALVES * ((e - k) // 2) + 16 * HALVES if isinstance(e, int)
                           else e * (8 * HALVES) + (16 - 8 * k) * HALVES)
                for h in range(HALVES):
                    wait(pe, g_l, HALVES * e - HALVES + h + 1)
                    transposes(yb[:, h, :], lambda c: xg[k][:, h, c * P:(c + 1) * P]).then_inc(g_tr, 1)

            def expert_gu(e, k, j):
                m, s = EK[j], (EJ * k + j) % 2
                if j == 0:
                    pe.wait_ge(ew_h, LB * e + LB)
                    pe.wait_ge(ew_l, LB * e + LB)
                    pe.wait_ge(g_h, HALVES * e + HALVES)
                    pe.wait_ge(g_l, HALVES * e + HALVES)
                wait(pe, e_mid, EJ * e + j - 1)
                for u in range(2):
                    for c in range(LB):
                        for a, b in PASSES:
                            col = u * I + j * P
                            last = pe.matmul(gu[0:m, s, u * CAP:(u + 1) * CAP], ew[k][:, c, a, col:col + m],
                                             xgT[k][:, c, b, :], start=(c == 0 and (a, b) == PASSES[0]),
                                             stop=(c == LB - 1 and (a, b) == PASSES[-1]))
                last.then_inc(e_mm, 1)

            def expert_down(e, k):
                pe.wait_ge(e_midh, EJ * e + EJ)
                pe.wait_ge(e_midl, EJ * e + EJ)
                pe.wait_ge(ed_h, e + 1)
                pe.wait_ge(ed_l, e + 1)
                for h in range(HALVES):
                    wait(pe, e_ok, HALVES * e - HALVES + h + 1)
                    for j in range(EJ):
                        for a, b in PASSES:
                            lhs = (midh, midl)[a]
                            last = pe.matmul(mb[:, h, :], lhs[0:EK[j], EJ * k + j, h * P:(h + 1) * P],
                                             ed[k][0:EK[j], j, b, :], start=(j == 0 and (a, b) == PASSES[0]),
                                             stop=(j == EJ - 1 and (a, b) == PASSES[-1]))
                    last.then_inc(e_dn, 1)

            def unit(e, k, before, next1, next2):
                expert_gu(e, k, 0)
                if before:
                    expert_down(e - 1, 1 - k)
                expert_gu(e, k, 1)
                if next1:
                    rows_t(e + 1, 1 - k)
                if next2:
                    slots(e + 2)
                expert_gu(e, k, 2)

            slots(0)
            slots(1)
            rows_t(0, 0)
            pe.wait_ge(dn_ok, TT * NG)
            unit(0, 0, False, True, True)
            unit(1, 1, True, True, True)
            with pe.Fori(1, E // 2 - 1) as i:
                unit(2 * i, 0, True, True, True)
                unit(2 * i + 1, 1, True, True, True)
            unit(E - 2, 0, True, True, False)
            unit(E - 1, 1, True, False, False)
            expert_down(E - 1, 1)

        @block.scalar
        def _(act):
            def split_shared(piece):
                s = piece % 2
                act.wait_ge(swraw_in[s], 32 * (piece // 2 + 1))
                if piece < LB:
                    act.activation(sw[:, piece, 0, :], sw_raw[:, s, :], ACT.Copy).then_inc(sw_h, 1)
                else:
                    for h in range(2):
                        j = 2 * (piece - LB) + h
                        last = act.activation(sd[0:SK[j], j, 0, :], sw_raw[0:SK[j], s, h * L:(h + 1) * L], ACT.Copy)
                    last.then_inc(sw_h, 1)

            def evacuate(dst, g, arrived, signal, free, free_at):
                for t in range(TT):
                    act.wait_ge(arrived, TT * g + t + 1)
                    wait(act, free, free_at)
                    tile = dst[:, bass.ds(g % 2, 1), :, t * P:(t + 1) * P].rearrange("p s c w -> p (s c) w")
                    act.activation(tile, mb[:, t, :].rearrange("p (c w) -> p c w", c=LB), ACT.Copy).then_inc(signal, 1)

            def round_kv(n, s):
                act.wait_ge(kv_m, n + 1)
                wait(act, conv, n - 1)
                act.activation(kvh[:, s, :, :], kv[:, s, :, :], ACT.Copy).then_inc(kv_h, 1)

            def silu(g, j):
                m = SK[j]
                act.wait_ge(gu_mm, SJ * g + j + 1)
                wait(act, mid_ok, SJ * g + max(j - 1, 0))
                act.activation(sil[0:m, j % 2, :], gu[0:m, j % 2, 0:GT], ACT.Silu).then_inc(sil_ok, 1)

            def round_mid(g, j):
                m = SK[j]
                act.wait_ge(mid_ok, SJ * g + j + 1)
                wait(act, dn_mm, TT * g)
                act.activation(midh[0:m, j, :], mid[0:m, j % 2, :], ACT.Copy).then_inc(mid_h, 1)

            def round_tokens(g):
                for t in range(TT):
                    act.wait_ge(n_tr, TT * g + t + 1)
                    wait(act, gu_mm, SJ * g)
                    wait(act, lg_mm, g)
                    act.activation(xT[:, :, 0, t * P:(t + 1) * P], mb[:, t, :].rearrange("p (c k) -> p c k", c=LB),
                                   ACT.Copy).then_inc(n_h, 1)

            def keep_scores(g):
                act.wait_ge(lg_mm, g + 1)
                act.activation(logits[:, bass.ds(g, 1), :].rearrange("p a e -> p (a e)"), mb[:, 1, 0:TT * E],
                               ACT.Copy).then_inc(lg_ok, 1)

            def steps(g, heads, prep, post, chunk):
                if heads:
                    round_kv(GH * g + 2, 0)
                if prep:
                    evacuate(kT, g + 1, c_tr, k_ev, kv_m, GH * g)
                if chunk:
                    silu(g - 2, 0)
                    silu(g - 2, 1)
                    round_mid(g - 2, 0)
                if heads:
                    round_kv(GH * g + 3, 1)
                if prep:
                    evacuate(qT, g + 1, q_tr, q_ev, d_mul, GH * g)
                if chunk:
                    round_mid(g - 2, 1)
                    silu(g - 2, 2)
                    silu(g - 2, 3)
                    round_mid(g - 2, 2)
                if heads and prep:
                    round_kv(GH * g + 4, 0)
                if chunk:
                    round_mid(g - 2, 3)
                    silu(g - 2, 4)
                    silu(g - 2, 5)
                    round_mid(g - 2, 4)
                if post:
                    round_tokens(g - 1)
                if chunk:
                    round_mid(g - 2, 5)
                if heads and prep:
                    round_kv(GH * g + 5, 1)
                if post:
                    keep_scores(g - 1)

            evacuate(kT, 0, c_tr, k_ev, c_tr, 0)
            evacuate(qT, 0, q_tr, q_ev, q_tr, 0)
            round_kv(0, 0)
            round_kv(1, 1)
            act.wait_ge(gate_t, 1)
            act.activation(gwT[:, :, 0, :], mb[:, 0, 0:LB * E].rearrange("p (c e) -> p c e", c=LB), ACT.Copy)\
                .then_inc(gate_h, 1)
            for piece in range(SW_PIECES):
                split_shared(piece)
            steps(0, True, True, False, False)
            steps(1, True, True, True, False)
            steps(2, True, True, True, True)
            with act.Fori(3, NG - 1) as g:
                steps(g, True, True, True, True)
            steps(NG - 1, True, False, True, True)
            steps(NG, False, False, True, True)
            act.wait_ge(rt, 1)
            act.activation(scp[:, :, 0:E], rep[:, :, 0:E], ACT.Exp).then_inc(rt_exp, 1)

            def split_w(e, k, c):
                act.wait_ge(raw_in[k], 64 * ((e - k) // 2) + 64 if isinstance(e, int) else e * 32 + (64 - 32 * k))
                wait(act, e_mm, EJ * e - EJ)
                act.activation(ew[k][:, c, 0, :], raw_w[k][:, c, :], ACT.Copy).then_inc(ew_h, 1)

            def split_d(e, k):
                act.wait_ge(raw_in[k], 64 * ((e - k) // 2) + 64 if isinstance(e, int) else e * 32 + (64 - 32 * k))
                wait(act, e_dn, HALVES * e - HALVES)
                act.activation(ed[k][:, 0:2, 0, :], raw_d[k][:, 0:2, :], ACT.Copy)
                act.activation(ed[k][0:EK[2], 2, 0, :], raw_d[k][0:EK[2], 2, :], ACT.Copy).then_inc(ed_h, 1)

            def round_rows(e, k):
                for h in range(HALVES):
                    act.wait_ge(g_tr, HALVES * e + h + 1)
                    wait(act, e_mm, EJ * e - EJ)
                    act.activation(xgT[k][:, :, 0, h * P:(h + 1) * P],
                                   yb[:, h, :].rearrange("p (c n) -> p c n", c=LB), ACT.Copy).then_inc(g_h, 1)

            def e_silu(e, k, j):
                m, s = EK[j], (EJ * k + j) % 2
                act.wait_ge(e_mm, EJ * e + j + 1)
                wait(act, e_mid, EJ * e + j - 1)
                act.activation(sil[0:m, s, :], gu[0:m, s, 0:CAP], ACT.Silu).then_inc(e_sil, 1)

            def e_round(e, k, j):
                m, s = EK[j], (EJ * k + j) % 2
                act.wait_ge(e_mid, EJ * e + j + 1)
                wait(act, e_dn, HALVES * e - HALVES)
                act.activation(midh[0:m, EJ * k + j, :], mid[0:m, s, :], ACT.Copy).then_inc(e_midh, 1)

            def unit(e, k, next1):
                if next1:
                    split_w(e + 1, 1 - k, 0)
                    split_w(e + 1, 1 - k, 1)
                e_silu(e, k, 0)
                if next1:
                    split_w(e + 1, 1 - k, 2)
                e_round(e, k, 0)
                if next1:
                    split_w(e + 1, 1 - k, 3)
                e_silu(e, k, 1)
                e_round(e, k, 1)
                if next1:
                    round_rows(e + 1, 1 - k)
                    split_d(e + 1, 1 - k)
                e_silu(e, k, 2)
                e_round(e, k, 2)

            def shared_tail():
                for j in range(0, SJ, 2):
                    silu(NG - 1, j)
                    silu(NG - 1, j + 1)
                    round_mid(NG - 1, j)
                    round_mid(NG - 1, j + 1)

            act.wait_ge(n_l, TT * NG)
            shared_tail()
            for c in range(LB):
                split_w(0, 0, c)
            split_d(0, 0)
            act.wait_ge(dn_mm, TT * NG)
            round_rows(0, 0)
            unit(0, 0, True)
            unit(1, 1, True)
            with act.Fori(1, E // 2 - 1) as i:
                unit(2 * i, 0, True)
                unit(2 * i + 1, 1, True)
            unit(E - 2, 0, True)
            unit(E - 1, 1, False)

        @block.gpsimd
        def _(pool):
            made = [0]

            def const(ins, after=True):
                ins.then_inc(consts, 1)
                made[0] += 1
                pool.wait_ge(consts, made[0])

            pool.memset(pad[:], 0.0).then_inc(pad_ok, 1)
            const(pool.memset(ident[:], 0.0))
            const(pool.affine_select(out=ident[:], in_=ident[:], compare_op=ALU.not_equal, fill=1.0, base=0,
                                     pattern=[[-1, P]], channel_multiplier=1))
            const(pool.memset(half_neg[:], -0.5))
            const(pool.iota(col_i[:], [[1, P]], base=0, channel_multiplier=0))
            const(pool.iota(colmod_i[:], [[0, TR], [1, B]], base=0, channel_multiplier=0))
            const(pool.iota(row_i[:, 0:1], [[0, 1]], base=0, channel_multiplier=1))
            const(pool.iota(iota_i[:], [[1, CAP]], base=0, channel_multiplier=0))
            const(pool.tensor_copy(iota_c[:], iota_i[:]))
            const(pool.iota(tok_i[:], [[0, E], [TR, NT]], base=0, channel_multiplier=0))
            const(pool.memset(carrier[:], 0.0))
            assert made[0] == N_CONST

            def pow_half(rs, ve, ready, count, signal):
                pool.wait_ge(ready, count)
                pool.tensor_tensor(rs[:], ve[:], half_neg[:], ALU.pow).then_inc(signal, 1)

            def pairs(n, g, hl):
                s = hl % 2
                pool.wait_ge(k_ev, TT * g + TT)
                wait(pool, kv_h, n - 1)
                wait(pool, kv_l, n - 1)
                src = kT[:, bass.ds(g % 2, 1), :, hl * HD * B:(hl + 1) * HD * B].rearrange("p s c w -> p (s c) w")
                for d in range(HD):
                    w = (HD - d) * B
                    last = pool.tensor_tensor(kv[:, s, :, POFF[d]:POFF[d] + w], src[:, :, 0:w],
                                              src[:, :, d * B:HD * B], ALU.mult)
                last.then_inc(kv_m, 1)

            def low_kv(n, s):
                pool.wait_ge(kv_h, n + 1)
                wait(pool, conv, n - 1)
                pool.wait_ge(kv_m, n + 1)
                pool.tensor_tensor(kvl[:, s, :, :], kv[:, s, :, :], kvh[:, s, :, :].bitcast(fp32), ALU.subtract)\
                    .then_inc(kv_l, 1)

            def low_mid(g, j):
                m = SK[j]
                pool.wait_ge(mid_h, SJ * g + j + 1)
                wait(pool, dn_mm, TT * g)
                pool.tensor_tensor(midl[0:m, j, :], mid[0:m, j % 2, :], midh[0:m, j, :].bitcast(fp32), ALU.subtract)\
                    .then_inc(mid_l, 1)

            def steps(g, heads, prep, post, chunk):
                if prep:
                    pow_half(xrs, xve, x_stat, g + 2, x_rs)
                if heads:
                    pairs(GH * g + 2, g, 2)
                    low_kv(GH * g + 1, 1)
                if chunk:
                    low_mid(g - 2, 0)
                if post:
                    pow_half(trs, tve, t_stat, g, t_rs)
                if heads:
                    pairs(GH * g + 3, g, 3)
                    low_kv(GH * g + 2, 0)
                if chunk:
                    low_mid(g - 2, 1)
                    low_mid(g - 2, 2)
                if heads and prep:
                    pairs(GH * g + 4, g + 1, 0)
                if heads:
                    low_kv(GH * g + 3, 1)
                if chunk:
                    low_mid(g - 2, 3)
                    low_mid(g - 2, 4)
                    low_mid(g - 2, 5)
                if heads and prep:
                    pairs(GH * g + 5, g + 1, 1)
                    low_kv(GH * g + 4, 0)

            pow_half(xrs, xve, x_stat, 1, x_rs)
            pairs(0, 0, 0)
            pairs(1, 0, 1)
            low_kv(0, 0)
            steps(0, True, True, False, False)
            steps(1, True, True, True, False)
            steps(2, True, True, True, True)
            with pool.Fori(3, NG - 1) as g:
                steps(g, True, True, True, True)
            steps(NG - 1, True, False, True, True)
            steps(NG, False, False, True, True)
            pool.wait_ge(conv, H)
            pool.wait_ge(d_sum, H)
            pool.wait_ge(o_tr, TT * NG)
            pool.wait_ge(n_l, TT * NG)
            for k in range(2):
                pool.memset(xg[k][:], 0.0).then_inc(xg_zero, 1)
            pool.wait_ge(xg_zero, 2)

            def gather(e, k):
                pool.wait_ge(sl_ok, e + 1)
                wait(pool, g_tr, HALVES * e - HALVES)
                wait(pool, carried[0], e)
                pool.tensor_tensor(carrier[:, 0:1], carrier[:, 2:3], carrier[:, 2:3], ALU.mult)\
                    .then_inc(carried[0], 1)
                for h in range(HALVES):
                    pool.indirect_dma_start(xg[k][:, h, :], None, xn_dram,
                                            bass.IndirectOffsetOnAxis(idx_g[k][:, h:h + 1], 0),
                                            bounds_check=T - 1, oob_is_err=False).then_inc(rows_in[k], 16)

            def scatter(e, k):
                wait(pool, added, 16 * HALVES * e)
                for h in range(HALVES):
                    if h == 0:
                        pool.wait_ge(e_ok, HALVES * e + HALVES)
                        wait(pool, carried[1], e)
                        pool.tensor_tensor(carrier[:, 1:2], carrier[:, 2:3], carrier[:, 2:3], ALU.mult)\
                            .then_inc(carried[1], 1)
                    pool.indirect_dma_start(out_rows, bass.IndirectOffsetOnAxis(idx_s[k][:, h:h + 1], 0),
                                            yo[:, h, :], None, bounds_check=T - 1, oob_is_err=False,
                                            compute_op=ALU.add).then_inc(added, 16)

            def low_d(e, k):
                pool.wait_ge(ed_h, e + 1)
                wait(pool, e_dn, HALVES * e - HALVES)
                pool.tensor_tensor(ed[k][:, 0:2, 1, :], raw_d[k][:, 0:2, :], ed[k][:, 0:2, 0, :].bitcast(fp32),
                                   ALU.subtract)
                pool.tensor_tensor(ed[k][0:EK[2], 2, 1, :], raw_d[k][0:EK[2], 2, :],
                                   ed[k][0:EK[2], 2, 0, :].bitcast(fp32), ALU.subtract).then_inc(ed_l, 1)

            def e_low(e, k, j):
                m, s = EK[j], (EJ * k + j) % 2
                pool.wait_ge(e_midh, EJ * e + j + 1)
                wait(pool, e_dn, HALVES * e - HALVES)
                pool.tensor_tensor(midl[0:m, EJ * k + j, :], mid[0:m, s, :],
                                   midh[0:m, EJ * k + j, :].bitcast(fp32), ALU.subtract).then_inc(e_midl, 1)

            def unit(e, k, before, next1, next2):
                e_low(e, k, 0)
                if before:
                    scatter(e - 1, 1 - k)
                e_low(e, k, 1)
                if next1:
                    low_d(e + 1, 1 - k)
                if next2:
                    gather(e + 2, k)
                e_low(e, k, 2)

            for j in range(SJ):
                low_mid(NG - 1, j)
            pool.wait_ge(xn_out, 16 * TT * NG)
            gather(0, 0)
            gather(1, 1)
            low_d(0, 0)
            pool.wait_ge(out_out, 16 * TT * NG)
            unit(0, 0, False, True, True)
            unit(1, 1, True, True, True)
            with pool.Fori(1, E // 2 - 1) as i:
                unit(2 * i, 0, True, True, True)
                unit(2 * i + 1, 1, True, True, True)
            unit(E - 2, 0, True, True, False)
            unit(E - 1, 1, True, False, False)
            scatter(E - 1, 1)
            pool.wait_ge(added, 16 * HALVES * E)

        @block.vector
        def _(dve):
            links = [0]

            def link(ins):
                links[0] += 1
                ins.then_inc(chain, 1)
                dve.wait_ge(chain, links[0])

            def split_shared(piece):
                s = piece % 2
                dve.wait_ge(sw_h, piece + 1)
                if piece < LB:
                    dve.tensor_tensor(sw[:, piece, 1, :], sw_raw[:, s, :], sw[:, piece, 0, :].bitcast(fp32),
                                      ALU.subtract).then_inc(sw_l, 1)
                else:
                    for h in range(2):
                        j = 2 * (piece - LB) + h
                        last = dve.tensor_tensor(sd[0:SK[j], j, 1, :], sw_raw[0:SK[j], s, h * L:(h + 1) * L],
                                                 sd[0:SK[j], j, 0, :].bitcast(fp32), ALU.subtract)
                    last.then_inc(sw_l, 1)

            def stats(tile, st, mv, ve, signal):
                for t in range(TT):
                    dve.bn_stats(st[:, t, :], tile(t))
                dve.drain()
                for t in range(TT):
                    dve.bn_aggr(mv[:, t, :], st[:, t, :])
                dve.drain()
                dve.tensor_scalar(ve[:], mv[:, :, 1:2].rearrange("p t a -> p (t a)"), EPS, None, ALU.add)\
                    .then_inc(signal, 1)

            def x_tile(g, t):
                return x_t[:, bass.ds(g % 3, 1), t, :].rearrange("p s l -> p (s l)")

            def x1_tile(g, t):
                return x1[:, bass.ds(g % 2, 1), t, :].rearrange("p s l -> p (s l)")

            def prep_stats(g):
                dve.wait_ge(group_in, 64 * g + 64)
                wait(dve, x_nrm, TT * g)
                dve.tensor_copy(carrier_d[:, 0:1], carrier_d[:, 1:2])
                stats(lambda t: x_tile(g, t), xstat, xmv, xve, x_stat)

            def prep_norm(g):
                dve.wait_ge(x_rs, g + 1)
                for t in range(TT):
                    wait(dve, q_tr, TT * g - TT + t + 1)
                    dve.tensor_scalar(xq[:, t, ::-1], x_tile(g, t), xmv[:, t, 0:1], xrs[:, t:t + 1],
                                      ALU.subtract, ALU.mult).then_inc(x_nrm, 1)

            def multiply(n, g, hl):
                s = hl % 2
                dve.wait_ge(conv, n + 1)
                dve.wait_ge(q_ev, TT * g + TT)
                wait(dve, d_sum, n - 1)
                q = qT[:, bass.ds(g % 2, 1), :, hl * HD * B:(hl + 1) * HD * B].rearrange("p s c w -> p (s c) w")
                for d in range(HD):
                    w = (HD - d) * B
                    last = dve.tensor_tensor(prod[:, s, :, d, d * B:HD * B], yb[:, :, POFF[d]:POFF[d] + w],
                                             q[:, :, 0:w], ALU.mult)
                    if d:
                        last = dve.tensor_tensor(prod[:, s, :, HD - d, 0:w], yb[:, :, POFF[d]:POFF[d] + w],
                                                 q[:, :, d * B:HD * B], ALU.mult)
                last.then_inc(d_mul, 1)

            def add_up(n, g, hl):
                s = hl % 2
                dve.wait_ge(d_mul, n + 1)
                wait(dve, o_tr, TT * g)
                dve.tensor_reduce(oT[:, :, hl * HD * B:(hl + 1) * HD * B],
                                  prod[:, s, :, :, :].rearrange("p c i w -> p c w i"), AX.X, ALU.add)\
                    .then_inc(d_sum, 1)

            def add_x(g):
                for t in range(TT):
                    dve.wait_ge(o_tr, TT * g + t + 1)
                    wait(dve, dn_ok, TT * (g - 1))
                    dve.tensor_tensor(x1_tile(g, t), mb[:, t, ::-1], x_tile(g, t), ALU.add).then_inc(x1_ok, 1)
                dve.wait_ge(x1_ok, TT * g + TT)
                wait(dve, t_nrm, TT * g)
                dve.tensor_copy(carrier_d[:, 0:1], carrier_d[:, 1:2])
                stats(lambda t: x1_tile(g, t), tstat, tmv, tve, t_stat)

            def token_norm(g):
                dve.wait_ge(t_rs, g + 1)
                wait(dve, n_tr, TT * g)
                wait(dve, xn_out, 16 * TT * g)
                for t in range(TT):
                    dve.tensor_scalar(xn[:, t, :], x1_tile(g, t), tmv[:, t, 0:1], trs[:, t:t + 1],
                                      ALU.subtract, ALU.mult).then_inc(t_nrm, 1)

            def low_tokens(g):
                for t in range(TT):
                    dve.wait_ge(n_h, TT * g + t + 1)
                    wait(dve, gu_mm, SJ * g)
                    cols = slice(t * P, (t + 1) * P)
                    dve.tensor_tensor(xT[:, :, 1, cols], mb[:, t, :].rearrange("p (c n) -> p c n", c=LB),
                                      xT[:, :, 0, cols].bitcast(fp32), ALU.subtract).then_inc(n_l, 1)

            def middle(g, j):
                m = SK[j]
                dve.wait_ge(sil_ok, SJ * g + j + 1)
                wait(dve, mid_h, SJ * g + max(j - 1, 0))
                wait(dve, mid_l, SJ * g + max(j - 1, 0))
                dve.tensor_tensor(mid[0:m, j % 2, :], sil[0:m, j % 2, :], gu[0:m, j % 2, GT:2 * GT], ALU.mult)\
                    .then_inc(mid_ok, 1)

            def chunk_sum(g):
                for t in range(TT):
                    dve.wait_ge(dn_mm, TT * g + t + 1)
                    wait(dve, out_out, 16 * TT * g)
                    dve.tensor_tensor(yo[:, t, :], mb[:, t, :], x1_tile(g, t), ALU.add).then_inc(dn_ok, 1)

            def steps(g, heads, prep, post, chunk):
                if prep:
                    prep_stats(g + 1)
                if heads:
                    multiply(GH * g, g, 0)
                    add_up(GH * g, g, 0)
                if prep:
                    prep_norm(g + 1)
                if chunk:
                    middle(g - 2, 0)
                if post:
                    add_x(g - 1)
                if chunk:
                    middle(g - 2, 1)
                if heads:
                    multiply(GH * g + 1, g, 1)
                    add_up(GH * g + 1, g, 1)
                if post:
                    token_norm(g - 1)
                if chunk:
                    middle(g - 2, 2)
                    middle(g - 2, 3)
                if heads:
                    multiply(GH * g + 2, g, 2)
                    add_up(GH * g + 2, g, 2)
                if chunk:
                    middle(g - 2, 4)
                    middle(g - 2, 5)
                if post:
                    low_tokens(g - 1)
                if heads:
                    multiply(GH * g + 3, g, 3)
                    add_up(GH * g + 3, g, 3)
                if chunk:
                    chunk_sum(g - 2)

            dve.wait_ge(consts, N_CONST)
            dve.memset(carrier_d[:], 0.0)
            dve.tensor_scalar(row_i[:, 1:2], row_i[:, 0:1], B - 1, None, ALU.bitwise_and)
            link(dve.tensor_scalar(row_i[:, 2:3], row_i[:, 0:1], B.bit_length() - 1, None, ALU.logical_shift_right))
            link(dve.tensor_copy(row_f[:], row_i[:]))
            dve.tensor_scalar(later_row[:], col_i[:], row_f[:, 0:1], None, ALU.is_gt)
            dve.tensor_scalar(earlier_b[:], colmod_i[:], row_f[:, 1:2], None, ALU.is_gt)
            link(dve.tensor_scalar(same_b[:], colmod_i[:], row_f[:, 1:2], None, ALU.is_equal))
            link(dve.tensor_tensor(before_in_b[:], same_b[:], later_row[:], ALU.mult))
            dve.wait_ge(taps_in, 32)
            dve.wait_ge(pad_ok, 1)
            link(dve.tensor_copy(pad[:, 0:L], tap_rows[:, ::-1]))
            link(dve.tensor_tensor(pad[:, L - 1:L], pad[:, L - 1:L], skip_t[:], ALU.add))
            link(dve.tensor_copy(padhl[:, 0, :], pad[:]))
            dve.tensor_tensor(padhl[:, 1, :], pad[:], padhl[:, 0, :].bitcast(fp32), ALU.subtract).then_inc(taps_hl, 1)
            prep_stats(0)
            prep_norm(0)
            dve.wait_ge(gate_h, 1)
            dve.tensor_tensor(gwT[:, :, 1, :], mb[:, 0, 0:LB * E].rearrange("p (c e) -> p c e", c=LB),
                              gwT[:, :, 0, :].bitcast(fp32), ALU.subtract).then_inc(gate_l, 1)
            for piece in range(SW_PIECES):
                split_shared(piece)
            steps(0, True, True, False, False)
            steps(1, True, True, True, False)
            steps(2, True, True, True, True)
            with dve.Fori(3, NG - 1) as g:
                steps(g, True, True, True, True)
            steps(NG - 1, True, False, True, True)
            steps(NG, False, False, True, True)

            tiles = logits[:].rearrange("p g (t e) -> p (g t) e", e=E)

            def scores():
                dve.wait_ge(lg_ok, NG)
                dve.wait_ge(taps_out, 16)
                link(dve.tensor_reduce(r_max[:], tiles, AX.X, ALU.max))
                dve.memset(scp[:, :, E:PADW], -1.0)
                dve.memset(reset[:], 1.0)
                dve.tensor_tensor(rep[:, :, 0:E], tiles, r_max[:].unsqueeze(2).broadcast_to([P, NT, E]),
                                  ALU.subtract).then_inc(rt, 1)

            def softmax():
                dve.wait_ge(rt_exp, 1)
                link(dve.tensor_reduce(r_sum[:], scp[:, :, 0:E], AX.X, ALU.add))
                link(dve.reciprocal(r_rec[:], r_sum[:]))
                link(dve.tensor_tensor(rep[:, :, 0:E], scp[:, :, 0:E],
                                       r_rec[:].unsqueeze(2).broadcast_to([P, NT, E]), ALU.mult))
                link(dve.tensor_copy(scp[:, :, 0:E], rep[:, :, 0:E]))

            def top():
                for t in range(NT):
                    last = dve.max(top8[:, t, :], scp[:, t, :])
                link(last)
                link(dve.tensor_reduce(r_sum[:], top8[:, :, 0:TOPK], AX.X, ALU.add))
                dve.memset(top8[:, :, TOPK:8], -1.0)
                link(dve.tensor_scalar(r_sum[:], r_sum[:], 1e-20, None, ALU.add))
                for t in range(NT):
                    last = dve.match_replace(rep[:, t, :], top8[:, t, :], scp[:, t, :], -2.0)
                link(dve.reciprocal(r_rec[:], r_sum[:]))

            def ranks():
                link(dve.tensor_tensor(chosen[:].rearrange("p (e n) -> p n e", n=NT), rep[:, :, 0:E],
                                       scp[:, :, 0:E], ALU.not_equal))
                link(dve.memset(reset[:].rearrange("p (e n) -> p e n", n=NT)[:, :, 0:1], 0.0))
                dve.tensor_copy(chosen_b[:], chosen[:])
                link(dve.tensor_tensor_scan(run[:], reset[:], chosen[:], 0.0, ALU.mult, ALU.add))
                dve.tensor_tensor(excl_b[:], run[:], chosen[:], ALU.subtract)
                dve.tensor_copy(tot_b[:].rearrange("p (e n) -> p e n", n=NT),
                                run[:].rearrange("p (e n) -> p e n", n=NT)[:, :, NT - 1:NT]
                                .broadcast_to([P, E, NT])).then_inc(rt_c, 1)

            def weights():
                col = lambda i: V[:, :, i:i + 1].rearrange("p c a -> p (c a)")
                link(dve.tensor_tensor(wt[:].rearrange("p (e n) -> p n e", n=NT), scp[:, :, 0:E],
                                       r_rec[:].unsqueeze(2).broadcast_to([P, NT, E]), ALU.mult))
                dve.tensor_scalar(col(0), reset[:], 0.0, row_f[:, 1:2], ALU.mult, ALU.add)
                dve.tensor_scalar(col(1), tok_i[:], row_f[:, 2:3], None, ALU.add)
                dve.memset(col(2), 1.0)
                for part in range(3):
                    link(dve.tensor_copy(col(3 + part), wt[:]))
                    if part < 2:
                        link(dve.tensor_tensor(wtmp[:], wt[:], col(3 + part), ALU.subtract))
                        link(dve.tensor_copy(wt[:], wtmp[:]))
                dve.wait_ge(rt_mm, 1)
                link(dve.scalar_tensor_tensor(out=rank[:], in0=yb[:, 0, 0:TE], scalar=1.0, in1=chosen[:],
                                              op0=ALU.add, op1=ALU.mult))
                link(dve.tensor_scalar(rank[:], rank[:], -1.0, None, ALU.add))

            def one_hot(e):
                wait(dve, sl_mm, e)
                for t in range(NT):
                    col = e * NT + t
                    last = dve.tensor_scalar(onehot[:, t, :], iota_c[:], rank[:, bass.ds(col, 1)], None,
                                             ALU.is_equal)
                last.then_inc(oh_ok, 1)

            def decode(e, k):
                dve.wait_ge(sl_mm, e + 1)
                wait(dve, rows_in[k], 16 * HALVES * ((e - k) // 2) if isinstance(e, int)
                     else e * (8 * HALVES) - 8 * k * HALVES)
                wait(dve, dec[2], e)
                dve.tensor_copy(slot_f[:], yb[:, 2, 0:8 * HALVES].rearrange("p (h c) -> p h c", c=8)[:, :, 0:6])\
                    .then_inc(sl_cp, 1)
                dve.wait_ge(sl_cp, e + 1)
                col = lambda i: slot_f[:, :, i:i + 1].rearrange("p h a -> p (h a)")
                dve.scalar_tensor_tensor(out=slot_a[:], in0=col(0), scalar=float(ROWS), in1=col(1),
                                         op0=ALU.mult, op1=ALU.add).then_inc(dec[0], 1)
                dve.tensor_reduce(wts_g[k][:], slot_f[:, :, 3:6], AX.X, ALU.add)
                dve.wait_ge(dec[0], e + 1)
                dve.scalar_tensor_tensor(out=slot_b[:], in0=col(2), scalar=-FAR, in1=slot_a[:],
                                         op0=ALU.mult, op1=ALU.add).then_inc(dec[1], 1)
                dve.wait_ge(dec[1], e + 1)
                dve.tensor_scalar(idx_g[k][:], slot_b[:], FAR, None, ALU.add).then_inc(sl_ok, 1)
                dve.engine_nop().then_inc(dec[2], 1)

            def keep_slots(e, k):
                wait(dve, added, 16 * HALVES * (e - 1) if isinstance(e, int) else e * (16 * HALVES) - 16 * HALVES)
                dve.wait_ge(sl_ok, e + 1)
                wait(dve, e_ok, HALVES * e - HALVES)
                dve.tensor_copy(idx_s[k][:], idx_g[k][:])
                dve.tensor_copy(wts_s[k][:], wts_g[k][:]).then_inc(kept, 1)

            def low_w(e, k, c):
                dve.wait_ge(ew_h, LB * e + c + 1)
                wait(dve, e_mm, EJ * e - EJ)
                dve.tensor_tensor(ew[k][:, c, 1, :], raw_w[k][:, c, :], ew[k][:, c, 0, :].bitcast(fp32),
                                  ALU.subtract).then_inc(ew_l, 1)

            def low_rows(e, k):
                for h in range(HALVES):
                    dve.wait_ge(g_h, HALVES * e + h + 1)
                    wait(dve, e_mm, EJ * e - EJ)
                    cols = slice(h * P, (h + 1) * P)
                    dve.tensor_tensor(xgT[k][:, :, 1, cols], yb[:, h, :].rearrange("p (c n) -> p c n", c=LB),
                                      xgT[k][:, :, 0, cols].bitcast(fp32), ALU.subtract).then_inc(g_l, 1)

            def e_middle(e, k, j):
                m, s = EK[j], (EJ * k + j) % 2
                dve.wait_ge(e_sil, EJ * e + j + 1)
                wait(dve, e_midh, EJ * e + j - 1)
                wait(dve, e_midl, EJ * e + j - 1)
                dve.tensor_tensor(mid[0:m, s, :], sil[0:m, s, :], gu[0:m, s, CAP:2 * CAP], ALU.mult)\
                    .then_inc(e_mid, 1)

            def weigh(e, k):
                dve.wait_ge(kept, e + 1)
                for h in range(HALVES):
                    dve.wait_ge(e_dn, HALVES * e + h + 1)
                    wait(dve, added, 16 * HALVES * e)
                    dve.tensor_scalar(yo[:, h, :], mb[:, h, :], wts_s[k][:, h:h + 1], None, ALU.mult)\
                        .then_inc(e_ok, 1)

            def unit(e, k, before, next1, next2):
                keep_slots(e, k)
                if next2:
                    one_hot(e + 2)
                if next1:
                    low_w(e + 1, 1 - k, 0)
                e_middle(e, k, 0)
                if next1:
                    low_w(e + 1, 1 - k, 1)
                if before:
                    weigh(e - 1, 1 - k)
                if next1:
                    low_w(e + 1, 1 - k, 2)
                e_middle(e, k, 1)
                if next1:
                    low_rows(e + 1, 1 - k)
                    low_w(e + 1, 1 - k, 3)
                if next2:
                    decode(e + 2, k)
                e_middle(e, k, 2)

            scores()
            middle(NG - 1, 0)
            softmax()
            middle(NG - 1, 1)
            top()
            middle(NG - 1, 2)
            ranks()
            middle(NG - 1, 3)
            weights()
            middle(NG - 1, 4)
            one_hot(0)
            middle(NG - 1, 5)
            decode(0, 0)
            one_hot(1)
            chunk_sum(NG - 1)
            decode(1, 1)
            for c in range(LB):
                low_w(0, 0, c)
            low_rows(0, 0)
            dve.wait_ge(out_out, 16 * TT * NG)
            unit(0, 0, False, True, True)
            unit(1, 1, True, True, True)
            with dve.Fori(1, E // 2 - 1) as i:
                unit(2 * i, 0, True, True, True)
                unit(2 * i + 1, 1, True, True, True)
            unit(E - 2, 0, True, True, False)
            unit(E - 1, 1, True, False, False)
            weigh(E - 1, 1)


_INS = ['x', 'ctx_2048', 'L0_xattn_ssm_kernel', 'L0_xattn_D', 'L0_ffn_gate_w', 'L0_ffn_w_gate', 'L0_ffn_w_up',
        'L0_ffn_w_down', 'L0_ffn_sw_gate', 'L0_ffn_sw_up', 'L0_ffn_sw_down']
_OUTS = [((8, 256, 512), 'float32')]


def kernel(**inputs):
    import numpy as _np
    import concourse.bacc as _bacc
    from concourse import mybir as _mybir
    from concourse.bass_utils import run_bass_kernel_spmd as _run

    nc = _bacc.Bacc("TRN2", target_bir_lowering=False, num_devices=1)
    arrays, args = {}, []
    for name in _INS:
        a = _np.ascontiguousarray(inputs[name])
        arrays[f"in_{name}_dram"] = a
        args.append(nc.dram_tensor(f"in_{name}_dram", a.shape, _mybir.dt.from_np(a.dtype), kind="ExternalInput").ap())
    for i, (shape, dtype) in enumerate(_OUTS):
        dt = _mybir.dt.from_np(_np.dtype(dtype))
        args.append(nc.dram_tensor(f"out_{i}_dram", shape, dt, kind="ExternalOutput").ap())
    xattn_moe_kernel(nc, *args)
    r = _run(nc, [arrays], core_ids=[0])
    got = tuple(r.results[0][f"out_{i}_dram"] for i in range(len(_OUTS)))
    return got[0]
```

```python
import concourse.bass as bass
from concourse import mybir
from contextlib import ExitStack

fp32 = mybir.dt.float32
fp32r = mybir.dt.float32r
bf16 = mybir.dt.bfloat16
int32 = mybir.dt.int32
ALU = mybir.AluOpType
ACT = mybir.ActivationFunctionType
AX = mybir.AxisListType

P = 128
PASSES = ((0, 0), (0, 1), (1, 0))


def wait(eng, sem, value):
    if not (isinstance(value, int) and value <= 0):
        eng.wait_ge(sem, value)


def xattn_moe_kernel(nc, x, ctx, taps, skip, gate_w, w_gate, w_up, w_down, sw_gate, sw_up, sw_down, out):
    B, ROWS, L = x.shape
    H = taps.shape[0]
    HD = ROWS // H
    E, _, I = w_gate.shape
    IS = sw_gate.shape[1]
    CAP, TOPK, EPS = 256, 4, 1e-5
    T = B * ROWS
    LB = L // P
    GH = 4
    GR = GH * HD
    NG = H // GH
    TR = P // B
    TT = GR // TR
    GT = TT * P
    PAIRS = HD * (HD + 1) // 2
    PW = PAIRS * B
    POFF = [B * sum(HD - d for d in range(s)) for s in range(HD + 1)]
    TW = P + L
    SJ = -(-IS // P)
    SK = [min(P, IS - j * P) for j in range(SJ)]
    EJ = -(-I // P)
    EK = [min(P, I - j * P) for j in range(EJ)]
    HALVES = CAP // P
    NT = NG * TT
    TE = NT * E
    FAR = float(1 << 20)

    toep_dram = nc.dram_tensor("toeplitz_taps", [H, 2, TW], fp32).ap()
    xn_dram = nc.dram_tensor("normalised_tokens", [T, L], fp32).ap()
    x_g = x.rearrange("b (g t r) l -> g t r b l", t=TT, r=TR)
    c_g = ctx.rearrange("b (g t r) l -> g t r b l", t=TT, r=TR)
    xn_g = xn_dram.rearrange("(b g t r) l -> g t r b l", b=B, t=TT, r=TR)
    out_g = out.rearrange("b (g t r) l -> g t r b l", t=TT, r=TR)
    out_rows = out.rearrange("b r l -> (b r) l")
    wg_e = w_gate.rearrange("e (c p) i -> e p c i", p=P)
    wu_e = w_up.rearrange("e (c p) i -> e p c i", p=P)

    es = ExitStack()
    with es:
        def sem(name):
            return es.enter_context(nc.semaphore(name))

        arena_bytes = (nc.sbuf_bytes_remaining - 256) // 32 * 32
        arena = es.enter_context(nc.sbuf_tensor("arena", [P, arena_bytes // 4], fp32))
        arena_base = nc.sbuf_base - arena_bytes
        cursor = [arena_base]

        def place(name, shape, dt):
            size = 1
            for n in shape[1:]:
                size *= n
            size = -(-size * (2 if dt == bf16 else 4) // 32) * 32
            t = nc.alloc_sbuf_tensor_at(name, shape, dt, offset=cursor[0])
            cursor[0] += size
            assert cursor[0] <= arena_base + arena_bytes, (name, cursor[0])
            return t

        ident = place("ident", [P, P], fp32)
        same_b = place("same_b", [P, P], bf16)
        before_in_b = place("before_in_b", [P, P], bf16)
        earlier_b = place("earlier_b", [P, P], bf16)
        later_row = place("later_row", [P, P], bf16)
        col_i = place("col_i", [P, P], int32)
        colmod_i = place("colmod_i", [P, P], int32)
        row_i = place("row_i", [P, 3], int32)
        row_f = place("row_f", [P, 3], fp32)
        iota_i = place("iota_i", [P, CAP], int32)
        iota_c = place("iota_c", [P, CAP], bf16)
        tok_i = place("tok_i", [P, TE], int32)
        carrier = place("carrier", [P, 3], fp32)
        carrier_d = place("carrier_d", [P, 2], fp32)
        half_neg = place("half_neg", [P, TT], fp32)
        gwT = place("gwT", [P, LB, 2, E], fp32r)
        logits = place("logits", [P, NG, TT * E], fp32)
        xstat = place("xstat", [P, TT, 6], fp32)
        xmv = place("xmv", [P, TT, 2], fp32)
        xve = place("xve", [P, TT], fp32)
        xrs = place("xrs", [P, TT], fp32)
        xnm = place("xnm", [P, TT], fp32)
        xnb = place("xnb", [P, TT], fp32)
        tstat = place("tstat", [P, TT, 6], fp32)
        tmv = place("tmv", [P, TT, 2], fp32)
        tve = place("tve", [P, TT], fp32)
        trs = place("trs", [P, TT], fp32)
        tnm = place("tnm", [P, TT], fp32)
        tnb = place("tnb", [P, TT], fp32)
        shared_at = cursor[0]
        sw = place("sw", [P, LB, 2, 2 * IS], fp32r)
        sd = place("sd", [P, SJ, 2, L], fp32r)
        xT = place("xT", [P, LB, 2, GT], fp32r)
        sil = place("sil", [P, 2, CAP], fp32)
        mid = place("mid", [P, 2, CAP], fp32)
        stage_at = cursor[0]
        midh = place("midh", [P, SJ, CAP], fp32r)
        midl = place("midl", [P, SJ, CAP], fp32r)
        ffn_end = cursor[0]
        cursor[0] = stage_at
        sw_raw = place("sw_raw", [P, 2, 2 * IS], fp32)
        cursor[0] = ffn_end
        yo = place("yo", [P, TT, L], fp32)
        x1 = place("x1", [P, 2, TT, L], fp32)
        xn = place("xn", [P, TT, L], fp32)
        zone = cursor[0]
        x_t = place("x_t", [P, 3, TT, L], fp32)
        c_t = place("c_t", [P, TT, L], fp32)
        xq = place("xq", [P, TT, L], fp32)
        kT = place("kT", [P, 2, LB, GR * B], fp32)
        qT = place("qT", [P, 2, LB, GR * B], fp32)
        kv = place("kv", [P, 2, LB, PW], fp32)
        kvh = place("kvh", [P, 2, LB, PW], fp32r)
        kvl = place("kvl", [P, 2, LB, PW], fp32r)
        toep = [place(f"toep{n}", [P, 2, L], fp32r) for n in range(2)]
        oT = place("oT", [P, LB, GR * B], fp32)
        prod_at = cursor[0]
        prod = place("prod", [P, 2, LB, HD, HD * B], fp32)
        cursor[0] = prod_at
        tap_rows = place("tap_rows", [H, L], fp32)
        pad = place("pad", [H, TW], fp32)
        padhl = place("padhl", [H, 2, TW], fp32r)
        skip_t = place("skip_t", [H, 1], fp32)
        gate_rows = place("gate_rows", [E, L], fp32)
        cursor[0] = zone
        ew0 = place("ew0", [P, LB, 2, 2 * I], fp32r)
        ed0 = place("ed0", [P, EJ, 2, L], fp32r)
        raw_w0 = place("raw_w0", [P, LB, 2 * I], fp32)
        raw_d0 = place("raw_d0", [P, EJ, L], fp32)
        xg = [place(f"xg{k}", [P, HALVES, L], fp32) for k in range(2)]
        onehot = place("onehot", [P, NT, CAP], bf16)
        routing_at = cursor[0]
        cursor[0] = shared_at
        raw_w = [raw_w0, place("raw_w1", [P, LB, 2 * I], fp32)]
        raw_d = [raw_d0, place("raw_d1", [P, EJ, L], fp32)]
        ew = [ew0, place("ew1", [P, LB, 2, 2 * I], fp32r)]
        assert raw_w[1] is not None and cursor[0] <= shared_at + LB * 4 * IS * 4
        ed = [ed0, place("ed1", [P, EJ, 2, L], fp32r)]
        xgT = [xT, place("xgT1", [P, LB, 2, CAP], fp32r)]
        cursor[0] = routing_at
        PADW = E + 8
        scp = place("scp", [P, NT, PADW], fp32)
        rep = place("rep", [P, NT, PADW], fp32)
        top8 = place("top8", [P, NT, 8], fp32)
        r_max = place("r_max", [P, NT], fp32)
        r_sum = place("r_sum", [P, NT], fp32)
        r_rec = place("r_rec", [P, NT], fp32)
        chosen = place("chosen", [P, TE], fp32)
        chosen_b = place("chosen_b", [P, TE], bf16)
        run = place("run", [P, TE], fp32)
        excl_b = place("excl_b", [P, TE], bf16)
        tot_b = place("tot_b", [P, TE], bf16)
        reset = place("reset", [P, TE], fp32)
        rank = place("rank", [P, TE], fp32)
        wt = place("wt", [P, TE], fp32)
        wtmp = place("wtmp", [P, TE], fp32)
        V = place("V", [P, TE, 6], bf16)
        slot_f = place("slot_f", [P, HALVES, 6], fp32)
        slot_a = place("slot_a", [P, HALVES], fp32)
        slot_b = place("slot_b", [P, HALVES], fp32)
        idx_g = [place(f"idx_g{k}", [P, HALVES], int32) for k in range(2)]
        idx_s = [place(f"idx_s{k}", [P, HALVES], int32) for k in range(2)]
        wts_g = [place(f"wts_g{k}", [P, HALVES], fp32) for k in range(2)]
        wts_s = [place(f"wts_s{k}", [P, HALVES], fp32) for k in range(2)]

        yb = es.enter_context(nc.psum_tensor("yb", [P, LB, 512], fp32))
        gu = es.enter_context(nc.psum_tensor("gu", [P, 2, 512], fp32))
        mb = es.enter_context(nc.psum_tensor("mb", [P, 2, 512], fp32))
        egu = [gu[:, 0, :], gu[:, 1, :], yb[:, 3, :]]

        taps_in, taps_out = sem("taps_in"), sem("taps_out")
        gate_in = sem("gate_in")
        swraw_in = [sem("swraw_in0"), sem("swraw_in1")]
        sd_in = sem("sd_in")
        ctx_in, x_in = sem("ctx_in"), sem("x_in")
        toep_in = [sem("toep_in0"), sem("toep_in1")]
        xn_out, out_out = sem("xn_out"), sem("out_out")
        raw_in = [sem("raw_in0"), sem("raw_in1")]
        rawd_in = [sem("rawd_in0"), sem("rawd_in1")]
        rows_in = [sem("rows_in0"), sem("rows_in1")]
        added = sem("added")
        consts = sem("consts")
        pad_ok, skip_ok, taps_hl = sem("pad_ok"), sem("skip_ok"), sem("taps_hl")
        gate_t, gate_h, gate_l = sem("gate_t"), sem("gate_h"), sem("gate_l")
        sw_h, sw_l = sem("sw_h"), sem("sw_l")
        x_pow, t_pow = sem("x_pow"), sem("t_pow")
        x_stat, x_rs, x_nrm = sem("x_stat"), sem("x_rs"), sem("x_nrm")
        c_tr, q_tr = sem("c_tr"), sem("q_tr")
        k_ev, q_ev = sem("k_ev"), sem("q_ev")
        kv_m, kv_h, kv_l = sem("kv_m"), sem("kv_h"), sem("kv_l")
        conv = sem("conv")
        d_mul, d_sum = sem("d_mul"), sem("d_sum")
        o_tr = sem("o_tr")
        x1_ok, t_stat, t_rs, t_nrm = sem("x1_ok"), sem("t_stat"), sem("t_rs"), sem("t_nrm")
        n_tr, n_h, n_l = sem("n_tr"), sem("n_h"), sem("n_l")
        lg_mm, lg_ok = sem("lg_mm"), sem("lg_ok")
        gu_mm, sil_ok, mid_ok, mid_h, mid_l = sem("gu_mm"), sem("sil_ok"), sem("mid_ok"), sem("mid_h"), sem("mid_l")
        dn_mm, dn_ok = sem("dn_mm"), sem("dn_ok")
        rt, rt_exp, rt_mm = sem("rt"), sem("rt_exp"), sem("rt_mm")
        rt_c = sem("rt_c")
        ew_h, ew_l, ed_h, ed_l = sem("ew_h"), sem("ew_l"), sem("ed_h"), sem("ed_l")
        oh_ok, sl_mm, sl_ok, sl_cp = sem("oh_ok"), sem("sl_mm"), sem("sl_ok"), sem("sl_cp")
        chain = sem("chain")
        g_tr, g_h, g_l = sem("g_tr"), sem("g_h"), sem("g_l")
        e_mm, e_sil, e_mid, e_midh, e_midl = sem("e_mm"), sem("e_sil"), sem("e_mid"), sem("e_midh"), sem("e_midl")
        e_dn, e_ok = sem("e_dn"), sem("e_ok")
        xg_zero = sem("xg_zero")
        dec = [sem("dec0"), sem("dec1"), sem("dec2")]
        kept = sem("kept")

        carried = [sem("carried0"), sem("carried1")]
        N_CONST = 10
        SW_PIECES = LB + SJ // 2

        block = es.enter_context(nc.Block())

        @block.sync
        def _(sp):
            def load_group(g, parts="cx"):
                for t in range(TT):
                    if "c" in parts:
                        sp.dma_start(c_t[:, t, :], c_g[g, t]).then_inc(ctx_in, 16)
                for t in range(TT):
                    if "x" in parts:
                        sp.dma_start(x_t[:, bass.ds(g % 3, 1), t, :].rearrange("p s l -> p (s l)"),
                                     x_g[g, t]).then_inc(x_in, 16)

            def load_toep(n, k):
                h = toep_dram[n]
                src = bass.AP(h.tensor, h.offset, [[1, P], [TW, 2], [1, L]])
                sp.dma_start(toep[k][:].bitcast(fp32), src).then_inc(toep_in[k], 16)

            def load_shared(piece):
                if piece < LB:
                    rows = slice(piece * P, (piece + 1) * P)
                    sp.dma_start(sw_raw[:, piece % 2, 0:IS], sw_gate[rows, :]).then_inc(swraw_in[piece % 2], 16)
                    sp.dma_start(sw_raw[:, piece % 2, IS:2 * IS], sw_up[rows, :]).then_inc(swraw_in[piece % 2], 16)
                else:
                    for h in range(2):
                        j = 2 * (piece - LB) + h
                        sp.dma_start(yo[0:SK[j], h, :], sw_down[j * P:j * P + SK[j], :]).then_inc(sd_in, 16)

            def store(dst_g, src, g, done, signal, count):
                for t in range(TT):
                    wait(sp, done, count + t + 1)
                    sp.dma_start(dst_g[g, t], src[:, t, :]).then_inc(signal, 16)

            def steps(g, heads, post, chunk, ahead):
                for hl in range(GH):
                    if heads:
                        n = GH * g + hl
                        if not (isinstance(n, int) and n + 2 >= H):
                            sp.wait_ge(conv, n + 1)
                            load_toep(n + 2, hl % 2)
                    if hl == 0 and post:
                        store(xn_g, xn, g - 1, t_nrm, xn_out, TT * (g - 1))
                    if hl == 0 and chunk:
                        store(out_g, yo, g - 2, dn_ok, out_out, TT * (g - 2))
                    if hl == 1 and ahead:
                        wait(sp, x1_ok, TT * g)
                        wait(sp, c_tr, TT * (g + 2))
                        load_group(g + 2)

            load_group(0, parts="c")
            sp.dma_start(tap_rows[:], taps).then_inc(taps_in, 16)
            sp.dma_start(skip_t[:], skip.rearrange("(h a) -> h a", a=1)).then_inc(taps_in, 16)
            load_group(0, parts="x")
            sp.dma_start(gate_rows[:], gate_w).then_inc(gate_in, 16)
            sp.wait_ge(taps_hl, 1)
            sp.dma_start(toep_dram, padhl[:].bitcast(fp32)).then_inc(taps_out, 16)
            sp.wait_ge(taps_out, 16)
            load_toep(0, 0)
            load_toep(1, 1)
            sp.wait_ge(c_tr, TT)
            load_group(1)
            load_shared(0)
            load_shared(1)
            sp.wait_ge(conv, 1)
            load_toep(2, 0)
            for piece in range(2, LB):
                sp.wait_ge(sw_h, piece - 1)
                sp.wait_ge(sw_l, piece - 1)
                load_shared(piece)
            sp.wait_ge(conv, 2)
            load_toep(3, 1)
            sp.wait_ge(c_tr, TT * 2)
            load_group(2)
            load_shared(LB)
            sp.wait_ge(conv, 3)
            load_toep(4, 0)
            sp.wait_ge(conv, 4)
            load_toep(5, 1)
            sp.wait_ge(conv, 5)
            load_toep(6, 0)
            store(xn_g, xn, 0, t_nrm, xn_out, 0)
            sp.wait_ge(sw_h, LB + 1)
            sp.wait_ge(sw_l, LB + 1)
            load_shared(LB + 1)
            sp.wait_ge(conv, 6)
            load_toep(7, 1)
            sp.wait_ge(x1_ok, TT)
            sp.wait_ge(c_tr, TT * 3)
            load_group(3)
            sp.wait_ge(sw_h, LB + 2)
            sp.wait_ge(sw_l, LB + 2)
            load_shared(LB + 2)
            sp.wait_ge(conv, 7)
            load_toep(8, 0)
            sp.wait_ge(conv, 8)
            load_toep(9, 1)
            steps(2, True, True, True, True)
            with sp.Fori(3, NG - 2) as g:
                steps(g, True, True, True, True)
            steps(NG - 2, True, True, True, False)
            steps(NG - 1, True, True, True, False)
            steps(NG, False, True, True, False)

            def load_raw_w(e, k):
                sp.dma_start(raw_w[k][:, :, 0:I], wg_e[e]).then_inc(raw_in[k], 16)
                sp.dma_start(raw_w[k][:, :, I:2 * I], wu_e[e]).then_inc(raw_in[k], 16)

            def load_raw_d(e, k):
                sp.dma_start(raw_d[k][:, 0:2, :], w_down[e, 0:2 * P, :].rearrange("(j p) l -> p j l", p=P))\
                    .then_inc(rawd_in[k], 16)
                sp.dma_start(raw_d[k][0:EK[2], 2, :], w_down[e, 2 * P:I, :]).then_inc(rawd_in[k], 16)

            sp.wait_ge(conv, H)
            sp.wait_ge(d_sum, H)
            sp.wait_ge(n_l, TT * NG)
            sp.wait_ge(o_tr, TT * NG)
            sp.wait_ge(x1_ok, TT * NG)
            load_raw_w(0, 0)
            load_raw_d(0, 0)
            sp.wait_ge(gu_mm, SJ * NG)
            load_raw_w(1, 1)
            load_raw_d(1, 1)
            store(out_g, yo, NG - 1, dn_ok, out_out, TT * (NG - 1))

            def next_raw(e, k):
                sp.wait_ge(ew_h, LB * (e + 1))
                sp.wait_ge(ew_l, LB * (e + 1))
                load_raw_w(e + 2, k)
                sp.wait_ge(ed_h, e + 1)
                sp.wait_ge(ed_l, e + 1)
                load_raw_d(e + 2, k)

            with sp.Fori(0, E // 2 - 1) as i:
                for k in range(2):
                    next_raw(2 * i + k, k)
            sp.wait_ge(out_out, 16 * TT * NG)
            sp.wait_ge(xn_out, 16 * TT * NG)

        @block.tensor
        def _(pe):
            def transposes(dst, src):
                for c in range(LB):
                    last = pe.transpose(dst[:, c * P:(c + 1) * P], src(c), ident[:])
                return last

            def convolve(n, hl):
                s = hl % 2
                pe.wait_ge(kv_h, n + 1)
                pe.wait_ge(kv_l, n + 1)
                pe.wait_ge(toep_in[s], 16 * ((n - s) // 2 + 1) if isinstance(n, int) else n * 8 + (16 - 8 * s))
                wait(pe, d_mul, n)
                for lb in range(LB):
                    steps = [(m, a, b) for m in range(lb + 1) for a, b in PASSES]
                    for i, (m, a, b) in enumerate(steps):
                        d = (LB - 1 - lb + m) * P
                        rhs = (kvh, kvl)[b]
                        last = pe.matmul(yb[:, lb, 0:PW], toep[s][:, a, d:d + P], rhs[:, s, m, :],
                                         start=(i == 0), stop=(i == len(steps) - 1))
                last.then_inc(conv, 1)

            def prep_ctx(g):
                pe.wait_ge(ctx_in, 32 * g + 32)
                wait(pe, n_l, TT * (g - 1))
                wait(pe, lg_ok, g - 1)
                for t in range(TT):
                    wait(pe, q_ev, TT * (g - 1) + t + 1)
                    transposes(mb[:, t, :], lambda c: c_t[:, t, c * P:(c + 1) * P]).then_inc(c_tr, 1)

            def prep_q(g):
                for t in range(TT):
                    pe.wait_ge(x_nrm, TT * g + t + 1)
                    pe.wait_ge(k_ev, TT * g + t + 1)
                    transposes(mb[:, t, :], lambda c: xq[:, t, (LB - 1 - c) * P:(LB - c) * P]).then_inc(q_tr, 1)

            def mixed_out(g, nq):
                pe.wait_ge(d_sum, GH * (g + 1))
                for t in range(TT):
                    wait(pe, q_ev, TT * nq + t + 1)
                    last = transposes(mb[:, t, :], lambda c: oT[:, LB - 1 - c, t * P:(t + 1) * P])
                    last.then_inc(o_tr, 1)

            def normalised(g):
                for t in range(TT):
                    pe.wait_ge(t_nrm, TT * g + t + 1)
                    pe.wait_ge(x1_ok, TT * g + t + 1)
                    transposes(mb[:, t, :], lambda c: xn[:, t, c * P:(c + 1) * P]).then_inc(n_tr, 1)

            def router(g):
                pe.wait_ge(n_h, TT * g + TT)
                pe.wait_ge(n_l, TT * g + TT)
                for t in range(TT):
                    for c in range(LB):
                        for a, b in PASSES:
                            last = pe.matmul(mb[:, 1, t * E:(t + 1) * E], xT[:, c, a, t * P:(t + 1) * P],
                                             gwT[:, c, b, :], start=(c == 0 and (a, b) == PASSES[0]),
                                             stop=(c == LB - 1 and (a, b) == PASSES[-1]))
                last.then_inc(lg_mm, 1)

            def gate_up(g, j):
                m = SK[j]
                pe.wait_ge(n_h, TT * g + TT)
                pe.wait_ge(n_l, TT * g + TT)
                if j < TT:
                    wait(pe, dn_ok, TT * g)
                else:
                    wait(pe, mid_ok, SJ * g + j - 1)
                for u in range(2):
                    for c in range(LB):
                        for a, b in PASSES:
                            col = u * IS + j * P
                            last = pe.matmul(gu[0:m, j % 2, u * GT:(u + 1) * GT], sw[:, c, a, col:col + m],
                                             xT[:, c, b, :], start=(c == 0 and (a, b) == PASSES[0]),
                                             stop=(c == LB - 1 and (a, b) == PASSES[-1]))
                last.then_inc(gu_mm, 1)

            def down(g):
                pe.wait_ge(mid_h, SJ * g + SJ)
                pe.wait_ge(mid_l, SJ * g + SJ)
                for t in range(TT):
                    for j in range(SJ):
                        for a, b in PASSES:
                            lhs = (midh, midl)[a]
                            last = pe.matmul(gu[:, t, :], lhs[0:SK[j], j, t * P:(t + 1) * P], sd[0:SK[j], j, b, :],
                                             start=(j == 0 and (a, b) == PASSES[0]),
                                             stop=(j == SJ - 1 and (a, b) == PASSES[-1]))
                    last.then_inc(dn_mm, 1)

            def steps(g, prep, post, chunk):
                convolve(GH * g, 0)
                if post:
                    mixed_out(g - 1, g)
                if chunk:
                    down(g - 2)
                if post:
                    normalised(g - 1)
                convolve(GH * g + 1, 1)
                if post:
                    router(g - 1)
                if prep:
                    prep_ctx(g + 1)
                if post:
                    gate_up(g - 1, 0)
                    gate_up(g - 1, 1)
                convolve(GH * g + 2, 2)
                if post:
                    gate_up(g - 1, 2)
                    gate_up(g - 1, 3)
                if prep:
                    prep_q(g + 1)
                convolve(GH * g + 3, 3)
                if post:
                    gate_up(g - 1, 4)
                    gate_up(g - 1, 5)

            pe.wait_ge(consts, 2)
            prep_ctx(0)
            prep_q(0)
            pe.wait_ge(gate_in, 16)
            pe.wait_ge(q_ev, TT)
            for c in range(LB):
                last = pe.transpose(mb[:, 0, c * E:(c + 1) * E], gate_rows[:, c * P:(c + 1) * P], ident[0:E, 0:E])
            last.then_inc(gate_t, 1)
            pe.wait_ge(gate_h, 1)
            pe.wait_ge(gate_l, 1)
            steps(0, True, False, False)
            pe.wait_ge(sw_h, LB)
            pe.wait_ge(sw_l, LB)
            steps(1, True, True, False)
            pe.wait_ge(sw_h, SW_PIECES)
            pe.wait_ge(sw_l, SW_PIECES)
            steps(2, True, True, True)
            with pe.Fori(3, NG - 1) as g:
                steps(g, True, True, True)
            steps(NG - 1, False, True, True)
            mixed_out(NG - 1, NG - 1)
            down(NG - 2)
            normalised(NG - 1)
            router(NG - 1)
            for j in range(SJ - 2):
                gate_up(NG - 1, j)
            pe.wait_ge(rt_c, 1)
            for lhs, rhs in ((before_in_b, chosen_b), (same_b, excl_b), (earlier_b, tot_b)):
                last = pe.matmul(yb[:, 0, 0:TE], lhs[:], rhs[:], start=(lhs is before_in_b),
                                 stop=(lhs is earlier_b))
            last.then_inc(rt_mm, 1)
            for j in range(SJ - 2, SJ):
                gate_up(NG - 1, j)
            down(NG - 1)

            def slots(e):
                pe.wait_ge(oh_ok, e + 1)
                wait(pe, sl_cp, e)
                for h in range(HALVES):
                    for t in range(NT):
                        col = e * NT + t
                        last = pe.matmul(yb[:, 2, h * 8:h * 8 + 6], onehot[:, t, h * P:(h + 1) * P],
                                         V[:, bass.ds(col, 1), :].rearrange("p a c -> p (a c)"),
                                         start=(t == 0), stop=(t == NT - 1))
                last.then_inc(sl_mm, 1)

            def rows_t(e, k):
                pe.wait_ge(rows_in[k], 16 * HALVES * ((e - k) // 2) + 16 * HALVES if isinstance(e, int)
                           else e * (8 * HALVES) + (16 - 8 * k) * HALVES)
                for h in range(HALVES):
                    wait(pe, g_l, HALVES * e - HALVES + h + 1)
                    transposes(yb[:, h, :], lambda c: xg[k][:, h, c * P:(c + 1) * P]).then_inc(g_tr, 1)

            def expert_gu(e, k, j):
                m = EK[j]
                if j == 0:
                    pe.wait_ge(ew_h, LB * e + LB)
                    pe.wait_ge(ew_l, LB * e + LB)
                    pe.wait_ge(g_h, HALVES * e + HALVES)
                    pe.wait_ge(g_l, HALVES * e + HALVES)
                wait(pe, e_mid, EJ * e - EJ + j + 1)
                for u in range(2):
                    for c in range(LB):
                        for a, b in PASSES:
                            col = u * I + j * P
                            last = pe.matmul(egu[j][0:m, u * CAP:(u + 1) * CAP], ew[k][:, c, a, col:col + m],
                                             xgT[k][:, c, b, :], start=(c == 0 and (a, b) == PASSES[0]),
                                             stop=(c == LB - 1 and (a, b) == PASSES[-1]))
                last.then_inc(e_mm, 1)

            def expert_down(e, k):
                pe.wait_ge(e_midh, EJ * e + EJ)
                pe.wait_ge(e_midl, EJ * e + EJ)
                pe.wait_ge(ed_h, e + 1)
                pe.wait_ge(ed_l, e + 1)
                for h in range(HALVES):
                    wait(pe, e_ok, HALVES * e - HALVES + h + 1)
                    for j in range(EJ):
                        for a, b in PASSES:
                            lhs = (midh, midl)[a]
                            last = pe.matmul(mb[:, h, :], lhs[0:EK[j], EJ * k + j, h * P:(h + 1) * P],
                                             ed[k][0:EK[j], j, b, :], start=(j == 0 and (a, b) == PASSES[0]),
                                             stop=(j == EJ - 1 and (a, b) == PASSES[-1]))
                    last.then_inc(e_dn, 1)

            def unit(e, k, before, next1, next2):
                expert_gu(e, k, 0)
                expert_gu(e, k, 1)
                if next2:
                    slots(e + 2)
                if next1:
                    rows_t(e + 1, 1 - k)
                if before:
                    expert_down(e - 1, 1 - k)
                expert_gu(e, k, 2)

            slots(0)
            slots(1)
            rows_t(0, 0)
            pe.wait_ge(dn_ok, TT * NG)
            unit(0, 0, False, True, True)
            unit(1, 1, True, True, True)
            with pe.Fori(1, E // 2 - 1) as i:
                unit(2 * i, 0, True, True, True)
                unit(2 * i + 1, 1, True, True, True)
            unit(E - 2, 0, True, True, False)
            unit(E - 1, 1, True, False, False)
            expert_down(E - 1, 1)

        @block.scalar
        def _(act):
            def split_shared(piece):
                s = piece % 2
                if piece < LB:
                    act.wait_ge(swraw_in[s], 32 * (piece // 2 + 1))
                    act.activation(sw[:, piece, 0, :], sw_raw[:, s, :], ACT.Copy).then_inc(sw_h, 1)
                else:
                    act.wait_ge(sd_in, 32 * (piece - LB + 1))
                    for h in range(2):
                        j = 2 * (piece - LB) + h
                        last = act.activation(sd[0:SK[j], j, 0, :], yo[0:SK[j], h, :], ACT.Copy)
                    last.then_inc(sw_h, 1)

            def norm(dst, src, t, rs, nb, signal):
                act.activation(dst, src, ACT.Identity, bias=nb[:, t:t + 1], scale=rs[:, t:t + 1]).then_inc(signal, 1)

            def norm_q(g):
                act.wait_ge(x_rs, g + 1)
                for t in range(TT):
                    wait(act, q_tr, TT * (g - 1) + t + 1)
                    norm(xq[:, t, ::-1], x_t[:, bass.ds(g % 3, 1), t, :].rearrange("p s l -> p (s l)"), t,
                         xrs, xnb, x_nrm)

            def norm_tokens(g):
                act.wait_ge(t_rs, g + 1)
                wait(act, n_tr, TT * g)
                wait(act, xn_out, 16 * TT * g)
                for t in range(TT):
                    norm(xn[:, t, :], x1[:, bass.ds(g % 2, 1), t, :].rearrange("p s l -> p (s l)"), t,
                         trs, tnb, t_nrm)

            def evacuate(dst, g, arrived, signal, free, free_at):
                for t in range(TT):
                    act.wait_ge(arrived, TT * g + t + 1)
                    wait(act, free, free_at)
                    tile = dst[:, bass.ds(g % 2, 1), :, t * P:(t + 1) * P].rearrange("p s c w -> p (s c) w")
                    act.activation(tile, mb[:, t, :].rearrange("p (c w) -> p c w", c=LB), ACT.Copy).then_inc(signal, 1)

            def round_kv(n, s):
                act.wait_ge(kv_m, n + 1)
                wait(act, conv, n - 1)
                act.activation(kvh[:, s, :, :], kv[:, s, :, :], ACT.Copy).then_inc(kv_h, 1)

            def silu(g, j):
                m = SK[j]
                act.wait_ge(gu_mm, SJ * g + j + 1)
                wait(act, mid_ok, SJ * g + max(j - 1, 0))
                act.activation(sil[0:m, j % 2, :], gu[0:m, j % 2, 0:GT], ACT.Silu).then_inc(sil_ok, 1)

            def round_mid(g, j):
                m = SK[j]
                act.wait_ge(mid_ok, SJ * g + j + 1)
                wait(act, dn_mm, TT * g)
                act.activation(midh[0:m, j, :], mid[0:m, j % 2, :], ACT.Copy).then_inc(mid_h, 1)

            def round_tokens(g):
                for t in range(TT):
                    act.wait_ge(n_tr, TT * g + t + 1)
                    wait(act, gu_mm, SJ * g)
                    wait(act, lg_mm, g)
                    act.activation(xT[:, :, 0, t * P:(t + 1) * P], mb[:, t, :].rearrange("p (c k) -> p c k", c=LB),
                                   ACT.Copy).then_inc(n_h, 1)

            def keep_scores(g):
                act.wait_ge(lg_mm, g + 1)
                act.activation(logits[:, bass.ds(g, 1), :].rearrange("p a e -> p (a e)"), mb[:, 1, 0:TT * E],
                               ACT.Copy).then_inc(lg_ok, 1)

            def steps(g, prep, post, extra=()):
                round_kv(GH * g + 2, 0)
                if post:
                    norm_tokens(g - 1)
                    round_tokens(g - 1)
                for piece in extra[0:1]:
                    split_shared(piece)
                round_kv(GH * g + 3, 1)
                if post:
                    keep_scores(g - 1)
                if prep:
                    evacuate(kT, g + 1, c_tr, k_ev, kv_m, GH * g)
                for piece in extra[1:2]:
                    split_shared(piece)
                if post:
                    for j in range(2):
                        silu(g - 1, j)
                        round_mid(g - 1, j)
                if prep:
                    norm_q(g + 1)
                    round_kv(GH * g + 4, 0)
                for piece in extra[2:3]:
                    split_shared(piece)
                if post:
                    for j in range(2, 4):
                        silu(g - 1, j)
                        round_mid(g - 1, j)
                if prep:
                    evacuate(qT, g + 1, q_tr, q_ev, d_mul, GH * g)
                    round_kv(GH * g + 5, 1)
                for piece in extra[3:4]:
                    split_shared(piece)
                if post:
                    for j in range(4, 6):
                        silu(g - 1, j)
                        round_mid(g - 1, j)

            evacuate(kT, 0, c_tr, k_ev, c_tr, 0)
            norm_q(0)
            round_kv(0, 0)
            evacuate(qT, 0, q_tr, q_ev, q_tr, 0)
            act.wait_ge(gate_t, 1)
            act.activation(gwT[:, :, 0, :], mb[:, 0, 0:LB * E].rearrange("p (c e) -> p c e", c=LB), ACT.Copy)\
                .then_inc(gate_h, 1)
            round_kv(1, 1)
            steps(0, True, False, (0, 1, 2, 3))
            steps(1, True, True, (4, 5, 6))
            steps(2, True, True)
            with act.Fori(3, NG - 1) as g:
                steps(g, True, True)
            steps(NG - 1, False, True)
            norm_tokens(NG - 1)
            round_tokens(NG - 1)
            keep_scores(NG - 1)
            act.wait_ge(rt, 1)
            act.activation(scp[:, :, 0:E], rep[:, :, 0:E], ACT.Exp).then_inc(rt_exp, 1)

            def split_w(e, k, c):
                act.wait_ge(raw_in[k], 32 * ((e - k) // 2) + 32 if isinstance(e, int) else e * 16 + (32 - 16 * k))
                wait(act, e_mm, EJ * e - EJ)
                act.activation(ew[k][:, c, 0, :], raw_w[k][:, c, :], ACT.Copy).then_inc(ew_h, 1)

            def split_d(e, k):
                act.wait_ge(rawd_in[k], 32 * ((e - k) // 2) + 32 if isinstance(e, int) else e * 16 + (32 - 16 * k))
                wait(act, e_dn, HALVES * e - HALVES)
                act.activation(ed[k][:, 0:2, 0, :], raw_d[k][:, 0:2, :], ACT.Copy)
                act.activation(ed[k][0:EK[2], 2, 0, :], raw_d[k][0:EK[2], 2, :], ACT.Copy).then_inc(ed_h, 1)

            def weigh(e, k):
                act.wait_ge(kept, e + 1)
                for h in range(HALVES):
                    act.wait_ge(e_dn, HALVES * e + h + 1)
                    wait(act, added, 16 * HALVES * e)
                    act.activation(yo[:, h, :], mb[:, h, :], ACT.Copy, scale=wts_s[k][:, h:h + 1]).then_inc(e_ok, 1)

            def round_rows(e, k):
                for h in range(HALVES):
                    act.wait_ge(g_tr, HALVES * e + h + 1)
                    wait(act, e_mm, EJ * e - EJ)
                    act.activation(xgT[k][:, :, 0, h * P:(h + 1) * P],
                                   yb[:, h, :].rearrange("p (c n) -> p c n", c=LB), ACT.Copy).then_inc(g_h, 1)

            def e_silu(e, k, j):
                m, s = EK[j], (EJ * k + j) % 2
                act.wait_ge(e_mm, EJ * e + j + 1)
                wait(act, e_mid, EJ * e + j - 1)
                act.activation(sil[0:m, s, :], egu[j][0:m, 0:CAP], ACT.Silu).then_inc(e_sil, 1)

            def e_round(e, k, j):
                m, s = EK[j], (EJ * k + j) % 2
                act.wait_ge(e_mid, EJ * e + j + 1)
                wait(act, e_dn, HALVES * e - HALVES)
                act.activation(midh[0:m, EJ * k + j, :], mid[0:m, s, :], ACT.Copy).then_inc(e_midh, 1)

            def unit(e, k, before, next1):
                if before:
                    e_round(e - 1, 1 - k, 2)
                split_d(e, k)
                if next1:
                    for c in range(LB):
                        split_w(e + 1, 1 - k, c)
                e_silu(e, k, 0)
                e_round(e, k, 0)
                e_silu(e, k, 1)
                e_round(e, k, 1)
                if next1:
                    round_rows(e + 1, 1 - k)
                if before:
                    weigh(e - 1, 1 - k)
                e_silu(e, k, 2)

            for j in range(SJ):
                silu(NG - 1, j)
                round_mid(NG - 1, j)
                if j >= 2:
                    split_w(0, 0, j - 2)
            act.wait_ge(dn_mm, TT * NG)
            round_rows(0, 0)
            act.wait_ge(out_out, 16 * TT * NG)
            unit(0, 0, False, True)
            unit(1, 1, True, True)
            with act.Fori(1, E // 2 - 1) as i:
                unit(2 * i, 0, True, True)
                unit(2 * i + 1, 1, True, True)
            unit(E - 2, 0, True, True)
            unit(E - 1, 1, True, False)
            e_round(E - 1, 1, 2)
            weigh(E - 1, 1)

        @block.gpsimd
        def _(pool):
            made = [0]

            def const(ins, after=True):
                ins.then_inc(consts, 1)
                made[0] += 1
                pool.wait_ge(consts, made[0])

            pool.memset(pad[:], 0.0).then_inc(pad_ok, 1)
            const(pool.memset(ident[:], 0.0))
            const(pool.affine_select(out=ident[:], in_=ident[:], compare_op=ALU.not_equal, fill=1.0, base=0,
                                     pattern=[[-1, P]], channel_multiplier=1))
            const(pool.memset(half_neg[:], -0.5))
            const(pool.iota(col_i[:], [[1, P]], base=0, channel_multiplier=0))
            const(pool.iota(colmod_i[:], [[0, TR], [1, B]], base=0, channel_multiplier=0))
            const(pool.iota(row_i[:, 0:1], [[0, 1]], base=0, channel_multiplier=1))
            const(pool.iota(iota_i[:], [[1, CAP]], base=0, channel_multiplier=0))
            const(pool.tensor_copy(iota_c[:], iota_i[:]))
            const(pool.iota(tok_i[:], [[0, E], [TR, NT]], base=0, channel_multiplier=0))
            const(pool.memset(carrier[:], 0.0))
            assert made[0] == N_CONST

            def inverse(rs, nb, ve, nm, steps, ready, count, used, signal):
                pool.wait_ge(ready, count)
                wait(pool, used, TT * (count - 1))
                pool.tensor_tensor(rs[:], ve[:], half_neg[:], ALU.pow).then_inc(steps, 1)
                pool.wait_ge(steps, count)
                pool.tensor_tensor(nb[:], nm[:], rs[:], ALU.mult).then_inc(signal, 1)

            def inverse_x(g):
                inverse(xrs, xnb, xve, xnm, x_pow, x_stat, g + 1, x_nrm, x_rs)

            def inverse_t(g):
                inverse(trs, tnb, tve, tnm, t_pow, t_stat, g + 1, t_nrm, t_rs)

            def pairs(n, g, hl):
                s = hl % 2
                pool.wait_ge(k_ev, TT * g + TT)
                wait(pool, kv_h, n - 1)
                wait(pool, kv_l, n - 1)
                src = kT[:, bass.ds(g % 2, 1), :, hl * HD * B:(hl + 1) * HD * B].rearrange("p s c w -> p (s c) w")
                for d in range(HD):
                    w = (HD - d) * B
                    last = pool.tensor_tensor(kv[:, s, :, POFF[d]:POFF[d] + w], src[:, :, 0:w],
                                              src[:, :, d * B:HD * B], ALU.mult)
                last.then_inc(kv_m, 1)

            def low_kv(n, s):
                pool.wait_ge(kv_h, n + 1)
                wait(pool, conv, n - 1)
                pool.wait_ge(kv_m, n + 1)
                pool.tensor_tensor(kvl[:, s, :, :], kv[:, s, :, :], kvh[:, s, :, :].bitcast(fp32), ALU.subtract)\
                    .then_inc(kv_l, 1)

            def low_mid(g, j):
                m = SK[j]
                pool.wait_ge(mid_h, SJ * g + j + 1)
                wait(pool, dn_mm, TT * g)
                pool.tensor_tensor(midl[0:m, j, :], mid[0:m, j % 2, :], midh[0:m, j, :].bitcast(fp32), ALU.subtract)\
                    .then_inc(mid_l, 1)

            def steps(g, prep, post, chunk):
                if chunk:
                    low_mid(g - 2, 4)
                pairs(GH * g + 2, g, 2)
                if chunk:
                    low_mid(g - 2, 5)
                low_kv(GH * g + 2, 0)
                pairs(GH * g + 3, g, 3)
                if post:
                    inverse_t(g - 1)
                low_kv(GH * g + 3, 1)
                if post:
                    low_mid(g - 1, 0)
                    low_mid(g - 1, 1)
                if prep:
                    inverse_x(g + 1)
                    pairs(GH * g + 4, g + 1, 0)
                    low_kv(GH * g + 4, 0)
                if post:
                    low_mid(g - 1, 2)
                if prep:
                    pairs(GH * g + 5, g + 1, 1)
                if post:
                    low_mid(g - 1, 3)
                if prep:
                    low_kv(GH * g + 5, 1)

            pairs(0, 0, 0)
            inverse_x(0)
            low_kv(0, 0)
            pairs(1, 0, 1)
            low_kv(1, 1)
            steps(0, True, False, False)
            steps(1, True, True, False)
            steps(2, True, True, True)
            with pool.Fori(3, NG - 1) as g:
                steps(g, True, True, True)
            steps(NG - 1, False, True, True)
            low_mid(NG - 2, 4)
            low_mid(NG - 2, 5)
            inverse_t(NG - 1)
            pool.wait_ge(rt, 1)
            pool.wait_ge(conv, H)
            pool.wait_ge(d_sum, H)
            pool.wait_ge(o_tr, TT * NG)
            pool.wait_ge(n_l, TT * NG)
            for k in range(2):
                pool.memset(xg[k][:], 0.0).then_inc(xg_zero, 1)
            pool.wait_ge(xg_zero, 2)

            def gather(e, k):
                pool.wait_ge(sl_ok, e + 1)
                wait(pool, g_tr, HALVES * e - HALVES)
                wait(pool, carried[0], e)
                pool.tensor_tensor(carrier[:, 0:1], carrier[:, 2:3], carrier[:, 2:3], ALU.mult)\
                    .then_inc(carried[0], 1)
                for h in range(HALVES):
                    pool.indirect_dma_start(xg[k][:, h, :], None, xn_dram,
                                            bass.IndirectOffsetOnAxis(idx_g[k][:, h:h + 1], 0),
                                            bounds_check=T - 1, oob_is_err=False).then_inc(rows_in[k], 16)

            def scatter(e, k):
                wait(pool, added, 16 * HALVES * e)
                for h in range(HALVES):
                    if h == 0:
                        pool.wait_ge(e_ok, HALVES * e + HALVES)
                        wait(pool, carried[1], e)
                        pool.tensor_tensor(carrier[:, 1:2], carrier[:, 2:3], carrier[:, 2:3], ALU.mult)\
                            .then_inc(carried[1], 1)
                    pool.indirect_dma_start(out_rows, bass.IndirectOffsetOnAxis(idx_s[k][:, h:h + 1], 0),
                                            yo[:, h, :], None, bounds_check=T - 1, oob_is_err=False,
                                            compute_op=ALU.add).then_inc(added, 16)

            def low_d(e, k):
                pool.wait_ge(ed_h, e + 1)
                wait(pool, e_dn, HALVES * e - HALVES)
                pool.tensor_tensor(ed[k][:, 0:2, 1, :], raw_d[k][:, 0:2, :], ed[k][:, 0:2, 0, :].bitcast(fp32),
                                   ALU.subtract)
                pool.tensor_tensor(ed[k][0:EK[2], 2, 1, :], raw_d[k][0:EK[2], 2, :],
                                   ed[k][0:EK[2], 2, 0, :].bitcast(fp32), ALU.subtract).then_inc(ed_l, 1)

            def e_low(e, k, j):
                m, s = EK[j], (EJ * k + j) % 2
                pool.wait_ge(e_midh, EJ * e + j + 1)
                wait(pool, e_dn, HALVES * e - HALVES)
                pool.tensor_tensor(midl[0:m, EJ * k + j, :], mid[0:m, s, :],
                                   midh[0:m, EJ * k + j, :].bitcast(fp32), ALU.subtract).then_inc(e_midl, 1)

            def unit(e, k, before, next2):
                if before:
                    e_low(e - 1, 1 - k, 2)
                low_d(e, k)
                e_low(e, k, 0)
                e_low(e, k, 1)
                if next2:
                    gather(e + 2, k)
                if before:
                    scatter(e - 1, 1 - k)

            for j in range(SJ):
                low_mid(NG - 1, j)
            pool.wait_ge(xn_out, 16 * TT * NG)
            gather(0, 0)
            gather(1, 1)
            pool.wait_ge(out_out, 16 * TT * NG)
            unit(0, 0, False, True)
            unit(1, 1, True, True)
            with pool.Fori(1, E // 2 - 1) as i:
                unit(2 * i, 0, True, True)
                unit(2 * i + 1, 1, True, True)
            unit(E - 2, 0, True, False)
            unit(E - 1, 1, True, False)
            e_low(E - 1, 1, 2)
            scatter(E - 1, 1)
            pool.wait_ge(added, 16 * HALVES * E)

        @block.vector
        def _(dve):
            links = [0]

            def link(ins):
                links[0] += 1
                ins.then_inc(chain, 1)
                dve.wait_ge(chain, links[0])

            def split_shared(piece):
                s = piece % 2
                dve.wait_ge(sw_h, piece + 1)
                if piece < LB:
                    dve.tensor_tensor(sw[:, piece, 1, :], sw_raw[:, s, :], sw[:, piece, 0, :].bitcast(fp32),
                                      ALU.subtract).then_inc(sw_l, 1)
                else:
                    for h in range(2):
                        j = 2 * (piece - LB) + h
                        last = dve.tensor_tensor(sd[0:SK[j], j, 1, :], yo[0:SK[j], h, :],
                                                 sd[0:SK[j], j, 0, :].bitcast(fp32), ALU.subtract)
                    last.then_inc(sw_l, 1)

            def stats(tile, st, mv, ve, nm, signal):
                for t in range(TT):
                    dve.bn_stats(st[:, t, :], tile(t))
                dve.drain()
                for t in range(TT):
                    dve.bn_aggr(mv[:, t, :], st[:, t, :])
                dve.drain()
                dve.tensor_scalar(nm[:], mv[:, :, 0:1].rearrange("p t a -> p (t a)"), -1.0, None, ALU.mult)
                dve.tensor_scalar(ve[:], mv[:, :, 1:2].rearrange("p t a -> p (t a)"), EPS, None, ALU.add)\
                    .then_inc(signal, 1)

            def x_tile(g, t):
                return x_t[:, bass.ds(g % 3, 1), t, :].rearrange("p s l -> p (s l)")

            def x1_tile(g, t):
                return x1[:, bass.ds(g % 2, 1), t, :].rearrange("p s l -> p (s l)")

            def prep_stats(g):
                dve.wait_ge(x_in, 32 * g + 32)
                wait(dve, x_rs, g)
                dve.tensor_copy(carrier_d[:, 0:1], carrier_d[:, 1:2])
                stats(lambda t: x_tile(g, t), xstat, xmv, xve, xnm, x_stat)

            def multiply(n, g, hl):
                s = hl % 2
                dve.wait_ge(conv, n + 1)
                dve.wait_ge(q_ev, TT * g + TT)
                wait(dve, d_sum, n - 1)
                q = qT[:, bass.ds(g % 2, 1), :, hl * HD * B:(hl + 1) * HD * B].rearrange("p s c w -> p (s c) w")
                for d in range(HD):
                    w = (HD - d) * B
                    last = dve.tensor_tensor(prod[:, s, :, d, d * B:HD * B], yb[:, :, POFF[d]:POFF[d] + w],
                                             q[:, :, 0:w], ALU.mult)
                    if d:
                        last = dve.tensor_tensor(prod[:, s, :, HD - d, 0:w], yb[:, :, POFF[d]:POFF[d] + w],
                                                 q[:, :, d * B:HD * B], ALU.mult)
                last.then_inc(d_mul, 1)

            def add_up(n, g, hl):
                s = hl % 2
                dve.wait_ge(d_mul, n + 1)
                wait(dve, o_tr, TT * g)
                dve.tensor_reduce(oT[:, :, hl * HD * B:(hl + 1) * HD * B],
                                  prod[:, s, :, :, :].rearrange("p c i w -> p c w i"), AX.X, ALU.add)\
                    .then_inc(d_sum, 1)

            def add_x(g):
                for t in range(TT):
                    dve.wait_ge(o_tr, TT * g + t + 1)
                    wait(dve, dn_ok, TT * (g - 1))
                    dve.tensor_tensor(x1_tile(g, t), mb[:, t, ::-1], x_tile(g, t), ALU.add).then_inc(x1_ok, 1)
                dve.wait_ge(x1_ok, TT * g + TT)
                wait(dve, t_rs, g)
                dve.tensor_copy(carrier_d[:, 0:1], carrier_d[:, 1:2])
                stats(lambda t: x1_tile(g, t), tstat, tmv, tve, tnm, t_stat)

            def low_tokens(g):
                for t in range(TT):
                    dve.wait_ge(n_h, TT * g + t + 1)
                    wait(dve, gu_mm, SJ * g)
                    cols = slice(t * P, (t + 1) * P)
                    dve.tensor_tensor(xT[:, :, 1, cols], mb[:, t, :].rearrange("p (c n) -> p c n", c=LB),
                                      xT[:, :, 0, cols].bitcast(fp32), ALU.subtract).then_inc(n_l, 1)

            def middle(g, j):
                m = SK[j]
                dve.wait_ge(sil_ok, SJ * g + j + 1)
                wait(dve, mid_h, SJ * g + max(j - 1, 0))
                wait(dve, mid_l, SJ * g + max(j - 1, 0))
                dve.tensor_tensor(mid[0:m, j % 2, :], sil[0:m, j % 2, :], gu[0:m, j % 2, GT:2 * GT], ALU.mult)\
                    .then_inc(mid_ok, 1)

            def chunk_sum(g, tiles=range(TT)):
                for t in tiles:
                    dve.wait_ge(dn_mm, TT * g + t + 1)
                    wait(dve, out_out, 16 * TT * g)
                    dve.tensor_tensor(yo[:, t, :], gu[:, t, :], x1_tile(g, t), ALU.add).then_inc(dn_ok, 1)

            def steps(g, prep, post, chunk, extra=()):
                multiply(GH * g, g, 0)
                if post:
                    add_x(g - 1)
                if chunk:
                    chunk_sum(g - 2, [0])
                add_up(GH * g, g, 0)
                if chunk:
                    chunk_sum(g - 2, [1])
                if post:
                    low_tokens(g - 1)
                for piece in extra[0:1]:
                    split_shared(piece)
                for hl in range(1, GH):
                    multiply(GH * g + hl, g, hl)
                    if post:
                        middle(g - 1, 2 * hl - 2)
                    add_up(GH * g + hl, g, hl)
                    if post:
                        middle(g - 1, 2 * hl - 1)
                    if prep and hl == 1:
                        prep_stats(g + 1)
                    for piece in extra[hl:hl + 1]:
                        split_shared(piece)

            dve.memset(carrier_d[:], 0.0)
            dve.wait_ge(taps_in, 32)
            dve.wait_ge(pad_ok, 1)
            link(dve.tensor_copy(pad[:, 0:L], tap_rows[:, ::-1]))
            link(dve.tensor_tensor(pad[:, L - 1:L], pad[:, L - 1:L], skip_t[:], ALU.add))
            link(dve.tensor_copy(padhl[:, 0, :], pad[:]))
            dve.tensor_tensor(padhl[:, 1, :], pad[:], padhl[:, 0, :].bitcast(fp32), ALU.subtract).then_inc(taps_hl, 1)
            prep_stats(0)
            dve.wait_ge(consts, N_CONST)
            dve.tensor_scalar(row_i[:, 1:2], row_i[:, 0:1], B - 1, None, ALU.bitwise_and)
            link(dve.tensor_scalar(row_i[:, 2:3], row_i[:, 0:1], B.bit_length() - 1, None, ALU.logical_shift_right))
            link(dve.tensor_copy(row_f[:], row_i[:]))
            dve.tensor_scalar(later_row[:], col_i[:], row_f[:, 0:1], None, ALU.is_gt)
            dve.tensor_scalar(earlier_b[:], colmod_i[:], row_f[:, 1:2], None, ALU.is_gt)
            link(dve.tensor_scalar(same_b[:], colmod_i[:], row_f[:, 1:2], None, ALU.is_equal))
            link(dve.tensor_tensor(before_in_b[:], same_b[:], later_row[:], ALU.mult))
            dve.wait_ge(gate_h, 1)
            dve.tensor_tensor(gwT[:, :, 1, :], mb[:, 0, 0:LB * E].rearrange("p (c e) -> p c e", c=LB),
                              gwT[:, :, 0, :].bitcast(fp32), ALU.subtract).then_inc(gate_l, 1)
            steps(0, True, False, False, (0, 1, 2, 3))
            steps(1, True, True, False, (4, 5, 6))
            steps(2, True, True, True)
            with dve.Fori(3, NG - 1) as g:
                steps(g, True, True, True)
            steps(NG - 1, False, True, True)
            add_x(NG - 1)
            chunk_sum(NG - 2)
            low_tokens(NG - 1)

            tiles = logits[:].rearrange("p g (t e) -> p (g t) e", e=E)

            def scores():
                dve.wait_ge(lg_ok, NG)
                dve.wait_ge(taps_out, 16)
                link(dve.tensor_reduce(r_max[:], tiles, AX.X, ALU.max))
                dve.memset(scp[:, :, E:PADW], -1.0)
                dve.memset(reset[:], 1.0)
                dve.tensor_tensor(rep[:, :, 0:E], tiles, r_max[:].unsqueeze(2).broadcast_to([P, NT, E]),
                                  ALU.subtract).then_inc(rt, 1)

            def softmax():
                dve.wait_ge(rt_exp, 1)
                link(dve.tensor_reduce(r_sum[:], scp[:, :, 0:E], AX.X, ALU.add))
                link(dve.reciprocal(r_rec[:], r_sum[:]))
                link(dve.tensor_tensor(rep[:, :, 0:E], scp[:, :, 0:E],
                                       r_rec[:].unsqueeze(2).broadcast_to([P, NT, E]), ALU.mult))
                link(dve.tensor_copy(scp[:, :, 0:E], rep[:, :, 0:E]))

            def top():
                for t in range(NT):
                    last = dve.max(top8[:, t, :], scp[:, t, :])
                link(last)
                link(dve.tensor_reduce(r_sum[:], top8[:, :, 0:TOPK], AX.X, ALU.add))
                dve.memset(top8[:, :, TOPK:8], -1.0)
                link(dve.tensor_scalar(r_sum[:], r_sum[:], 1e-20, None, ALU.add))
                for t in range(NT):
                    last = dve.match_replace(rep[:, t, :], top8[:, t, :], scp[:, t, :], -2.0)
                link(dve.reciprocal(r_rec[:], r_sum[:]))

            def ranks():
                link(dve.tensor_tensor(chosen[:].rearrange("p (e n) -> p n e", n=NT), rep[:, :, 0:E],
                                       scp[:, :, 0:E], ALU.not_equal))
                link(dve.memset(reset[:].rearrange("p (e n) -> p e n", n=NT)[:, :, 0:1], 0.0))
                dve.tensor_copy(chosen_b[:], chosen[:])
                link(dve.tensor_tensor_scan(run[:], reset[:], chosen[:], 0.0, ALU.mult, ALU.add))
                dve.tensor_tensor(excl_b[:], run[:], chosen[:], ALU.subtract)
                dve.tensor_copy(tot_b[:].rearrange("p (e n) -> p e n", n=NT),
                                run[:].rearrange("p (e n) -> p e n", n=NT)[:, :, NT - 1:NT]
                                .broadcast_to([P, E, NT])).then_inc(rt_c, 1)

            def weights():
                col = lambda i: V[:, :, i:i + 1].rearrange("p c a -> p (c a)")
                link(dve.tensor_tensor(wt[:].rearrange("p (e n) -> p n e", n=NT), scp[:, :, 0:E],
                                       r_rec[:].unsqueeze(2).broadcast_to([P, NT, E]), ALU.mult))
                dve.tensor_scalar(col(0), reset[:], 0.0, row_f[:, 1:2], ALU.mult, ALU.add)
                dve.tensor_scalar(col(1), tok_i[:], row_f[:, 2:3], None, ALU.add)
                dve.memset(col(2), 1.0)
                for part in range(3):
                    link(dve.tensor_copy(col(3 + part), wt[:]))
                    if part < 2:
                        link(dve.tensor_tensor(wtmp[:], wt[:], col(3 + part), ALU.subtract))
                        link(dve.tensor_copy(wt[:], wtmp[:]))
                dve.wait_ge(rt_mm, 1)
                link(dve.scalar_tensor_tensor(out=rank[:], in0=yb[:, 0, 0:TE], scalar=1.0, in1=chosen[:],
                                              op0=ALU.add, op1=ALU.mult))
                link(dve.tensor_scalar(rank[:], rank[:], -1.0, None, ALU.add))

            def one_hot(e):
                wait(dve, sl_mm, e)
                for t in range(NT):
                    col = e * NT + t
                    last = dve.tensor_scalar(onehot[:, t, :], iota_c[:], rank[:, bass.ds(col, 1)], None,
                                             ALU.is_equal)
                last.then_inc(oh_ok, 1)

            def decode(e, k):
                dve.wait_ge(sl_mm, e + 1)
                wait(dve, rows_in[k], 16 * HALVES * ((e - k) // 2) if isinstance(e, int)
                     else e * (8 * HALVES) - 8 * k * HALVES)
                wait(dve, dec[2], e)
                dve.tensor_copy(slot_f[:], yb[:, 2, 0:8 * HALVES].rearrange("p (h c) -> p h c", c=8)[:, :, 0:6])\
                    .then_inc(sl_cp, 1)
                dve.wait_ge(sl_cp, e + 1)
                col = lambda i: slot_f[:, :, i:i + 1].rearrange("p h a -> p (h a)")
                dve.scalar_tensor_tensor(out=slot_a[:], in0=col(0), scalar=float(ROWS), in1=col(1),
                                         op0=ALU.mult, op1=ALU.add).then_inc(dec[0], 1)
                dve.tensor_reduce(wts_g[k][:], slot_f[:, :, 3:6], AX.X, ALU.add)
                dve.wait_ge(dec[0], e + 1)
                dve.scalar_tensor_tensor(out=slot_b[:], in0=col(2), scalar=-FAR, in1=slot_a[:],
                                         op0=ALU.mult, op1=ALU.add).then_inc(dec[1], 1)
                dve.wait_ge(dec[1], e + 1)
                dve.tensor_scalar(idx_g[k][:], slot_b[:], FAR, None, ALU.add).then_inc(sl_ok, 1)
                dve.engine_nop().then_inc(dec[2], 1)

            def keep_slots(e, k):
                wait(dve, added, 16 * HALVES * (e - 1) if isinstance(e, int) else e * (16 * HALVES) - 16 * HALVES)
                dve.wait_ge(sl_ok, e + 1)
                wait(dve, e_ok, HALVES * e - HALVES)
                dve.tensor_copy(idx_s[k][:], idx_g[k][:])
                dve.tensor_copy(wts_s[k][:], wts_g[k][:]).then_inc(kept, 1)

            def low_w(e, k, c):
                dve.wait_ge(ew_h, LB * e + c + 1)
                wait(dve, e_mm, EJ * e - EJ)
                dve.tensor_tensor(ew[k][:, c, 1, :], raw_w[k][:, c, :], ew[k][:, c, 0, :].bitcast(fp32),
                                  ALU.subtract).then_inc(ew_l, 1)

            def low_rows(e, k):
                for h in range(HALVES):
                    dve.wait_ge(g_h, HALVES * e + h + 1)
                    wait(dve, e_mm, EJ * e - EJ)
                    cols = slice(h * P, (h + 1) * P)
                    dve.tensor_tensor(xgT[k][:, :, 1, cols], yb[:, h, :].rearrange("p (c n) -> p c n", c=LB),
                                      xgT[k][:, :, 0, cols].bitcast(fp32), ALU.subtract).then_inc(g_l, 1)

            def e_middle(e, k, j):
                m, s = EK[j], (EJ * k + j) % 2
                dve.wait_ge(e_sil, EJ * e + j + 1)
                wait(dve, e_midh, EJ * e + j - 1)
                wait(dve, e_midl, EJ * e + j - 1)
                dve.tensor_tensor(mid[0:m, s, :], sil[0:m, s, :], egu[j][0:m, CAP:2 * CAP], ALU.mult)\
                    .then_inc(e_mid, 1)

            def unit(e, k, before, next1, next2):
                if before:
                    e_middle(e - 1, 1 - k, 2)
                if next2:
                    one_hot(e + 2)
                e_middle(e, k, 0)
                if next1:
                    low_w(e + 1, 1 - k, 0)
                    low_w(e + 1, 1 - k, 1)
                e_middle(e, k, 1)
                keep_slots(e, k)
                if next2:
                    decode(e + 2, k)
                if next1:
                    low_w(e + 1, 1 - k, 2)
                    low_rows(e + 1, 1 - k)
                    low_w(e + 1, 1 - k, 3)

            scores()
            middle(NG - 1, 0)
            softmax()
            middle(NG - 1, 1)
            top()
            middle(NG - 1, 2)
            ranks()
            middle(NG - 1, 3)
            weights()
            one_hot(0)
            middle(NG - 1, 4)
            low_w(0, 0, 0)
            low_w(0, 0, 1)
            middle(NG - 1, 5)
            low_w(0, 0, 2)
            low_w(0, 0, 3)
            chunk_sum(NG - 1)
            decode(0, 0)
            one_hot(1)
            decode(1, 1)
            low_rows(0, 0)
            unit(0, 0, False, True, True)
            unit(1, 1, True, True, True)
            with dve.Fori(1, E // 2 - 1) as i:
                unit(2 * i, 0, True, True, True)
                unit(2 * i + 1, 1, True, True, True)
            unit(E - 2, 0, True, True, False)
            unit(E - 1, 1, True, False, False)
            e_middle(E - 1, 1, 2)
            dve.wait_ge(e_ok, HALVES * E)


_INS = ['x', 'ctx_2048', 'L0_xattn_ssm_kernel', 'L0_xattn_D', 'L0_ffn_gate_w', 'L0_ffn_w_gate', 'L0_ffn_w_up',
        'L0_ffn_w_down', 'L0_ffn_sw_gate', 'L0_ffn_sw_up', 'L0_ffn_sw_down']
_OUTS = [((8, 256, 512), 'float32')]


def kernel(**inputs):
    import numpy as _np
    import concourse.bacc as _bacc
    from concourse import mybir as _mybir
    from concourse.bass_utils import run_bass_kernel_spmd as _run

    nc = _bacc.Bacc("TRN2", target_bir_lowering=False, num_devices=1)
    arrays, args = {}, []
    for name in _INS:
        a = _np.ascontiguousarray(inputs[name])
        arrays[f"in_{name}_dram"] = a
        args.append(nc.dram_tensor(f"in_{name}_dram", a.shape, _mybir.dt.from_np(a.dtype), kind="ExternalInput").ap())
    for i, (shape, dtype) in enumerate(_OUTS):
        dt = _mybir.dt.from_np(_np.dtype(dtype))
        args.append(nc.dram_tensor(f"out_{i}_dram", shape, dt, kind="ExternalOutput").ap())
    xattn_moe_kernel(nc, *args)
    r = _run(nc, [arrays], core_ids=[0])
    got = tuple(r.results[0][f"out_{i}_dram"] for i in range(len(_OUTS)))
    return got[0]
```

```python
import concourse.bass as bass
from concourse import mybir
from contextlib import ExitStack

fp32 = mybir.dt.float32
fp32r = mybir.dt.float32r
bf16 = mybir.dt.bfloat16
int32 = mybir.dt.int32
ALU = mybir.AluOpType
ACT = mybir.ActivationFunctionType
AX = mybir.AxisListType

P = 128
PASSES = ((0, 0), (0, 1), (1, 0))


def wait(eng, sem, value):
    if not (isinstance(value, int) and value <= 0):
        eng.wait_ge(sem, value)


def xattn_moe_kernel(nc, x, ctx, taps, skip, gate_w, w_gate, w_up, w_down, sw_gate, sw_up, sw_down, out):
    B, ROWS, L = x.shape
    H = taps.shape[0]
    HD = ROWS // H
    E, _, I = w_gate.shape
    IS = sw_gate.shape[1]
    CAP, TOPK, EPS = 256, 4, 1e-5
    T = B * ROWS
    LB = L // P
    GH = 4
    GR = GH * HD
    NG = H // GH
    TR = P // B
    TT = GR // TR
    GT = TT * P
    PAIRS = HD * (HD + 1) // 2
    PW = PAIRS * B
    POFF = [B * sum(HD - d for d in range(s)) for s in range(HD + 1)]
    TW = P + L
    SJ = -(-IS // P)
    SK = [min(P, IS - j * P) for j in range(SJ)]
    ORDER = [SJ - 1] + list(range(SJ - 1))
    REST = SK[-1]
    UP = IS + E
    EJ = -(-I // P)
    EK = [min(P, I - j * P) for j in range(EJ)]
    HALVES = CAP // P
    NT = NG * TT
    TE = NT * E
    FAR = float(1 << 20)

    toep_dram = nc.dram_tensor("toeplitz_taps", [H, 2, TW], fp32).ap()
    xn_dram = nc.dram_tensor("normalised_tokens", [T, L], fp32).ap()
    x_g = x.rearrange("b (g t r) l -> g t r b l", t=TT, r=TR)
    c_g = ctx.rearrange("b (g t r) l -> g t r b l", t=TT, r=TR)
    xn_g = xn_dram.rearrange("(b g t r) l -> g t r b l", b=B, t=TT, r=TR)
    out_g = out.rearrange("b (g t r) l -> g t r b l", t=TT, r=TR)
    out_rows = out.rearrange("b r l -> (b r) l")
    wg_e = w_gate.rearrange("e (c p) i -> e p c i", p=P)
    wu_e = w_up.rearrange("e (c p) i -> e p c i", p=P)

    es = ExitStack()
    with es:
        def sem(name):
            return es.enter_context(nc.semaphore(name))

        arena_bytes = (nc.sbuf_bytes_remaining - 256) // 32 * 32
        arena = es.enter_context(nc.sbuf_tensor("arena", [P, arena_bytes // 4], fp32))
        arena_base = nc.sbuf_base - arena_bytes
        cursor = [arena_base]

        def place(name, shape, dt):
            size = 1
            for n in shape[1:]:
                size *= n
            size = -(-size * (2 if dt == bf16 else 4) // 32) * 32
            t = nc.alloc_sbuf_tensor_at(name, shape, dt, offset=cursor[0])
            cursor[0] += size
            assert cursor[0] <= arena_base + arena_bytes, (name, cursor[0])
            return t

        ident = place("ident", [P, P], fp32)
        same_b = place("same_b", [P, P], bf16)
        before_in_b = place("before_in_b", [P, P], bf16)
        earlier_b = place("earlier_b", [P, P], bf16)
        later_row = place("later_row", [P, P], bf16)
        col_i = place("col_i", [P, P], int32)
        colmod_i = place("colmod_i", [P, P], int32)
        row_i = place("row_i", [P, 3], int32)
        row_f = place("row_f", [P, 3], fp32)
        iota_c = place("iota_c", [P, P], bf16)
        tok_i = place("tok_i", [P, TE], int32)
        carrier = place("carrier", [P, 3], fp32)
        carrier_d = place("carrier_d", [P, 2], fp32)
        half_neg = place("half_neg", [P, TT], fp32)
        logits = place("logits", [P, NG, TT * E], fp32)
        lgT = place("lgT", [P, GT], fp32)
        xstat = place("xstat", [P, TT, 6], fp32)
        xmv = place("xmv", [P, TT, 2], fp32)
        xve = place("xve", [P, TT], fp32)
        xrs = place("xrs", [P, TT], fp32)
        xnm = place("xnm", [P, TT], fp32)
        xnb = place("xnb", [P, TT], fp32)
        tstat = place("tstat", [P, TT, 6], fp32)
        tmv = place("tmv", [P, TT, 2], fp32)
        tve = place("tve", [P, TT], fp32)
        trs = place("trs", [P, TT], fp32)
        tnm = place("tnm", [P, TT], fp32)
        tnb = place("tnb", [P, TT], fp32)
        shared_at = cursor[0]
        sw = place("sw", [P, LB, 2, UP + IS], fp32r)
        sd = place("sd", [P, SJ, 2, L], fp32r)
        xT = place("xT", [P, LB, 2, GT], fp32r)
        sil = place("sil", [P, 2, CAP], fp32)
        mid = place("mid", [P, 2, CAP], fp32)
        stage_at = cursor[0]
        midh = place("midh", [P, SJ, CAP], fp32r)
        midl = place("midl", [P, SJ, CAP], fp32r)
        ffn_end = cursor[0]
        cursor[0] = stage_at
        sw_raw = place("sw_raw", [P, 2, 2 * IS], fp32)
        cursor[0] = ffn_end
        yo = place("yo", [P, TT, L], fp32)
        x1 = place("x1", [P, 2, TT, L], fp32)
        xn = place("xn", [P, TT, L], fp32)
        zone = cursor[0]
        x_t = place("x_t", [P, 3, TT, L], fp32)
        spare_at = cursor[0] - TT * L * 4
        c_t = place("c_t", [P, TT, L], fp32)
        xq = place("xq", [P, TT, L], fp32)
        kT = place("kT", [P, 2, LB, GR * B], fp32)
        spare_end = cursor[0] - LB * GR * B * 4
        qT = place("qT", [P, 2, LB, GR * B], fp32)
        kv = place("kv", [P, 2, LB, PW], fp32)
        kvh = place("kvh", [P, 2, LB, PW], fp32r)
        kvl = place("kvl", [P, 2, LB, PW], fp32r)
        toep = [place(f"toep{n}", [P, 2, L], fp32r) for n in range(2)]
        oT = place("oT", [P, LB, GR * B], fp32)
        prod_at = cursor[0]
        prod = place("prod", [P, 2, LB, HD, HD * B], fp32)
        cursor[0] = prod_at
        tap_rows = place("tap_rows", [H, L], fp32)
        pad = place("pad", [H, TW], fp32)
        padhl = place("padhl", [H, 2, TW], fp32r)
        skip_t = place("skip_t", [H, 1], fp32)
        gate_rows = place("gate_rows", [E, L], fp32)
        PADW = E + 8
        cursor[0] = spare_at
        scp = place("scp", [P, NT, PADW], fp32)
        rep = place("rep", [P, NT, PADW], fp32)
        top8 = place("top8", [P, NT, 8], fp32)
        r_max = place("r_max", [P, NT], fp32)
        r_sum = place("r_sum", [P, NT], fp32)
        r_rec = place("r_rec", [P, NT], fp32)
        chosen = place("chosen", [P, TE], fp32)
        reset = place("reset", [P, TE], fp32)
        wt = place("wt", [P, TE], fp32)
        wtmp = place("wtmp", [P, TE], fp32)
        V = place("V", [P, TE, 6], bf16)
        run = place("run", [P, TE], fp32)
        excl_b = place("excl_b", [P, TE], bf16)
        tot_b = place("tot_b", [P, TE], bf16)
        chosen_b = place("chosen_b", [P, TE], bf16)
        assert cursor[0] <= spare_end
        cursor[0] = zone
        VH = place("VH", [P, TE, HALVES, 6], bf16)
        in_half = place("in_half", [P, HALVES, TE], bf16)
        assert cursor[0] <= spare_at
        cursor[0] = spare_end
        ew0 = place("ew0", [P, LB, 2, 2 * I], fp32r)
        ed0 = place("ed0", [P, EJ, 2, L], fp32r)
        raw_w0 = place("raw_w0", [P, LB, 2 * I], fp32)
        raw_d0 = place("raw_d0", [P, EJ, L], fp32)
        xg = [place(f"xg{k}", [P, HALVES, L], fp32) for k in range(2)]
        onehot = place("onehot", [P, NT, P], bf16)
        rank = place("rank", [P, TE], fp32)
        rank_in = place("rank_in", [P, TE], fp32)
        slot_f = place("slot_f", [P, HALVES, 6], fp32)
        slot_a = place("slot_a", [P, HALVES], fp32)
        slot_b = place("slot_b", [P, HALVES], fp32)
        idx_g = [place(f"idx_g{k}", [P, HALVES], int32) for k in range(2)]
        idx_s = [place(f"idx_s{k}", [P, HALVES], int32) for k in range(2)]
        wts_g = [place(f"wts_g{k}", [P, HALVES], fp32) for k in range(2)]
        wts_s = [place(f"wts_s{k}", [P, HALVES], fp32) for k in range(2)]
        cursor[0] = shared_at
        raw_w = [raw_w0, place("raw_w1", [P, LB, 2 * I], fp32)]
        raw_d = [raw_d0, place("raw_d1", [P, EJ, L], fp32)]
        ew = [ew0, place("ew1", [P, LB, 2, 2 * I], fp32r)]
        assert cursor[0] <= shared_at + LB * 2 * (UP + IS) * 4
        ed = [ed0, place("ed1", [P, EJ, 2, L], fp32r)]
        xgT = [xT, place("xgT1", [P, LB, 2, CAP], fp32r)]

        def raw_down(piece):
            return x1[:, 1, :, :] if piece == LB + 1 else yo[:]

        yb = es.enter_context(nc.psum_tensor("yb", [P, LB, 512], fp32))
        gu = es.enter_context(nc.psum_tensor("gu", [P, 2, 512], fp32))
        mb = es.enter_context(nc.psum_tensor("mb", [P, 2, 512], fp32))
        weighed = [yo, xn]
        egu = [gu[:, 0, :], gu[:, 1, :], yb[:, 3, :]]

        taps_in, taps_out = sem("taps_in"), sem("taps_out")
        gate_in = sem("gate_in")
        swraw_in = [sem("swraw_in0"), sem("swraw_in1")]
        sd_in = [sem("sd_in0"), sem("sd_in1")]
        ctx_in, x_in = sem("ctx_in"), sem("x_in")
        toep_in = [sem("toep_in0"), sem("toep_in1")]
        xn_out, out_out = sem("xn_out"), sem("out_out")
        raw_in = [sem("raw_in0"), sem("raw_in1")]
        rawd_in = [sem("rawd_in0"), sem("rawd_in1")]
        rows_in = [sem("rows_in0"), sem("rows_in1")]
        added = sem("added")
        consts = sem("consts")
        pad_ok, taps_hl = sem("pad_ok"), sem("taps_hl")
        gate_t, gate_h, gate_l = sem("gate_t"), sem("gate_h"), sem("gate_l")
        sw_h, sw_l = sem("sw_h"), sem("sw_l")
        sw_lp = sem("sw_lp")
        x_pow, t_pow = sem("x_pow"), sem("t_pow")
        x_stat, x_rs, x_nrm = sem("x_stat"), sem("x_rs"), sem("x_nrm")
        c_tr, q_tr = sem("c_tr"), sem("q_tr")
        k_ev, q_ev = sem("k_ev"), sem("q_ev")
        kv0_m, kv0_l = sem("kv0_m"), sem("kv0_l")
        kv_m, kv_l = sem("kv_m"), sem("kv_l")
        kv_h = sem("kv_h")
        conv = sem("conv")
        conv_half, d_half = sem("conv_half"), sem("d_half")
        d_mul, d_sum = sem("d_mul"), sem("d_sum")
        o_tr = sem("o_tr")
        x1_ok, t_stat, t_rs, t_nrm = sem("x1_ok"), sem("t_stat"), sem("t_rs"), sem("t_nrm")
        n_tr, n_h, n_l = sem("n_tr"), sem("n_h"), sem("n_l")
        lgT_ok, lg_tr, lg_ok = sem("lgT_ok"), sem("lg_tr"), sem("lg_ok")
        gu_mm, sil_ok, mid_ok, mid_h, mid_l = sem("gu_mm"), sem("sil_ok"), sem("mid_ok"), sem("mid_h"), sem("mid_l")
        rest_l = sem("rest_l")
        dn_mm, dn_ok = sem("dn_mm"), sem("dn_ok")
        rt, rt_exp, rt_mm = sem("rt"), sem("rt_exp"), sem("rt_mm")
        rt_c = sem("rt_c")
        ew_h, ew_l, ed_h, ed_l = sem("ew_h"), sem("ew_l"), sem("ed_h"), sem("ed_l")
        oh_ok, sl_mm, sl_ok, sl_cp = sem("oh_ok"), sem("sl_mm"), sem("sl_ok"), sem("sl_cp")
        chain = sem("chain")
        g_tr, g_h, g_l = sem("g_tr"), sem("g_h"), sem("g_l")
        e_mm, e_sil, e_mid, e_midh, e_midl = sem("e_mm"), sem("e_sil"), sem("e_mid"), sem("e_midh"), sem("e_midl")
        e_dn, e_ok = sem("e_dn"), sem("e_ok")
        xg_zero = sem("xg_zero")
        dec = [sem("dec0"), sem("dec1"), sem("dec2")]
        kept = sem("kept")

        carried = [sem("carried0"), sem("carried1")]
        N_CONST = 9
        SW_PIECES = LB + SJ // 2
        POOL_PIECES = (0, 3)
        DVE_PIECES = [p for p in range(SW_PIECES) if p not in POOL_PIECES]

        def low_done(eng, piece):
            if piece in POOL_PIECES:
                eng.wait_ge(sw_lp, POOL_PIECES.index(piece) + 1)
            else:
                eng.wait_ge(sw_l, DVE_PIECES.index(piece) + 1)

        def by_halves(n):
            return isinstance(n, int) and n < GH
        ROUND = [slice(0, TT * (NG - 2)), slice(TT * (NG - 2), NT)]

        block = es.enter_context(nc.Block())

        @block.sync
        def _(sp):
            def load_group(g, parts="cx"):
                for t in range(TT):
                    if "c" in parts:
                        sp.dma_start(c_t[:, t, :], c_g[g, t]).then_inc(ctx_in, 16)
                for t in range(TT):
                    if "x" in parts:
                        sp.dma_start(x_t[:, bass.ds(g % 3, 1), t, :].rearrange("p s l -> p (s l)"),
                                     x_g[g, t]).then_inc(x_in, 16)

            def load_toep(n, k):
                h = toep_dram[n]
                src = bass.AP(h.tensor, h.offset, [[1, P], [TW, 2], [1, L]])
                sp.dma_start(toep[k][:].bitcast(fp32), src).then_inc(toep_in[k], 16)

            def load_shared(piece):
                if piece < LB:
                    rows = slice(piece * P, (piece + 1) * P)
                    sp.dma_start(sw_raw[:, piece % 2, 0:IS], sw_gate[rows, :]).then_inc(swraw_in[piece % 2], 16)
                    sp.dma_start(sw_raw[:, piece % 2, IS:2 * IS], sw_up[rows, :]).then_inc(swraw_in[piece % 2], 16)
                else:
                    for h in range(2):
                        j = 2 * (piece - LB) + h
                        sp.dma_start(raw_down(piece)[0:SK[j], h, :], sw_down[j * P:j * P + SK[j], :])\
                            .then_inc(sd_in[(piece - LB) % 2], 16)
                        if j == SJ - 1:
                            sp.dma_start(raw_down(piece)[REST:2 * REST, h, :], sw_down[j * P:IS, :])\
                                .then_inc(sd_in[(piece - LB) % 2], 16)

            def store(dst_g, src, g, done, signal, count):
                for t in range(TT):
                    wait(sp, done, count + t + 1)
                    sp.dma_start(dst_g[g, t], src[:, t, :]).then_inc(signal, 16)

            def steps(g, heads, post, chunk, ahead):
                for hl in range(GH):
                    if heads:
                        n = GH * g + hl
                        if not (isinstance(n, int) and n + 2 >= H):
                            sp.wait_ge(conv, n + 1)
                            load_toep(n + 2, hl % 2)
                    if hl == 0 and post:
                        store(xn_g, xn, g - 1, t_nrm, xn_out, TT * (g - 1))
                    if hl == 0 and chunk:
                        store(out_g, yo, g - 2, dn_ok, out_out, TT * (g - 2))
                    if hl == 1 and ahead:
                        wait(sp, x1_ok, TT * g)
                        wait(sp, c_tr, TT * (g + 2))
                        load_group(g + 2)

            load_group(0, parts="c")
            sp.dma_start(tap_rows[:], taps).then_inc(taps_in, 16)
            sp.dma_start(skip_t[:], skip.rearrange("(h a) -> h a", a=1)).then_inc(taps_in, 16)
            load_group(0, parts="x")
            sp.dma_start(gate_rows[:], gate_w).then_inc(gate_in, 16)
            sp.wait_ge(taps_hl, 1)
            sp.dma_start(toep_dram, padhl[:].bitcast(fp32)).then_inc(taps_out, 16)
            sp.wait_ge(taps_out, 16)
            load_toep(0, 0)
            load_toep(1, 1)
            sp.wait_ge(c_tr, TT)
            load_group(1)
            load_shared(0)
            load_shared(1)

            def load_split_slot(piece):
                sp.wait_ge(sw_h, piece - 1)
                low_done(sp, piece - 2)
                load_shared(piece)

            sp.wait_ge(conv, 1)
            load_toep(2, 0)
            sp.wait_ge(conv, 2)
            load_toep(3, 1)
            load_split_slot(2)
            sp.wait_ge(conv, 3)
            load_toep(4, 0)
            sp.wait_ge(c_tr, TT * 2)
            load_group(2)
            sp.wait_ge(conv, 4)
            load_toep(5, 1)
            load_shared(LB)
            load_shared(LB + 1)
            load_split_slot(3)
            sp.wait_ge(conv, 5)
            load_toep(6, 0)
            load_split_slot(LB + 2)
            sp.wait_ge(conv, 6)
            load_toep(7, 1)
            store(xn_g, xn, 0, t_nrm, xn_out, 0)
            sp.wait_ge(x1_ok, TT)
            sp.wait_ge(c_tr, TT * 3)
            load_group(3)
            sp.wait_ge(conv, 7)
            load_toep(8, 0)
            sp.wait_ge(conv, 8)
            load_toep(9, 1)
            steps(2, True, True, True, True)
            with sp.Fori(3, NG - 2) as g:
                steps(g, True, True, True, True)
            steps(NG - 2, True, True, True, False)
            steps(NG - 1, True, True, True, False)
            steps(NG, False, True, True, False)

            def load_raw_w(e, k):
                sp.dma_start(raw_w[k][:, :, 0:I], wg_e[e]).then_inc(raw_in[k], 16)
                sp.dma_start(raw_w[k][:, :, I:2 * I], wu_e[e]).then_inc(raw_in[k], 16)

            def load_raw_d(e, k):
                sp.dma_start(raw_d[k][:, 0:2, :], w_down[e, 0:2 * P, :].rearrange("(j p) l -> p j l", p=P))\
                    .then_inc(rawd_in[k], 16)
                sp.dma_start(raw_d[k][0:EK[2], 2, :], w_down[e, 2 * P:I, :]).then_inc(rawd_in[k], 16)

            sp.wait_ge(conv, H)
            sp.wait_ge(d_sum, H)
            sp.wait_ge(n_l, TT * NG)
            sp.wait_ge(o_tr, TT * NG)
            sp.wait_ge(x1_ok, TT * NG)
            load_raw_w(0, 0)
            load_raw_d(0, 0)
            sp.wait_ge(gu_mm, SJ * NG)
            load_raw_w(1, 1)
            load_raw_d(1, 1)
            store(out_g, yo, NG - 1, dn_ok, out_out, TT * (NG - 1))

            def next_raw(e, k):
                sp.wait_ge(ew_h, LB * (e + 1))
                sp.wait_ge(ew_l, LB * (e + 1))
                load_raw_w(e + 2, k)
                sp.wait_ge(ed_h, e + 1)
                sp.wait_ge(ed_l, e + 1)
                load_raw_d(e + 2, k)

            with sp.Fori(0, E // 2 - 1) as i:
                for k in range(2):
                    next_raw(2 * i + k, k)
            sp.wait_ge(out_out, 16 * TT * NG)
            sp.wait_ge(xn_out, 16 * TT * NG)

        @block.tensor
        def _(pe):
            def transposes(dst, src):
                for c in range(LB):
                    last = pe.transpose(dst[:, c * P:(c + 1) * P], src(c), ident[:])
                return last

            def convolve(n, hl):
                s = hl % 2
                pe.wait_ge(kv_h, n + 1)
                if isinstance(n, int) and n == 0:
                    pe.wait_ge(kv0_l, 1)
                else:
                    pe.wait_ge(kv_l, n)
                pe.wait_ge(toep_in[s], 16 * ((n - s) // 2 + 1) if isinstance(n, int) else n * 8 + (16 - 8 * s))
                wait(pe, d_half if by_halves(n) else d_mul, n)
                for lb in range(LB):
                    if by_halves(n) and lb == LB // 2:
                        last.then_inc(conv_half, 1)
                        wait(pe, d_mul, n)
                    steps = [(m, a, b) for m in range(lb + 1) for a, b in PASSES]
                    for i, (m, a, b) in enumerate(steps):
                        d = (LB - 1 - lb + m) * P
                        rhs = (kvh, kvl)[b]
                        last = pe.matmul(yb[:, lb, 0:PW], toep[s][:, a, d:d + P], rhs[:, s, m, :],
                                         start=(i == 0), stop=(i == len(steps) - 1))
                last.then_inc(conv, 1)

            def prep_ctx(g):
                pe.wait_ge(ctx_in, 32 * g + 32)
                wait(pe, n_l, TT * (g - 1))
                for t in range(TT):
                    wait(pe, q_ev, TT * (g - 1) + t + 1)
                    transposes(mb[:, t, :], lambda c: c_t[:, t, c * P:(c + 1) * P]).then_inc(c_tr, 1)

            def prep_q(g):
                wait(pe, lg_ok, g - 1)
                for t in range(TT):
                    pe.wait_ge(x_nrm, TT * g + t + 1)
                    pe.wait_ge(k_ev, TT * g + t + 1)
                    transposes(mb[:, t, :], lambda c: xq[:, t, (LB - 1 - c) * P:(LB - c) * P]).then_inc(q_tr, 1)

            def mixed_out(g, nq):
                pe.wait_ge(d_sum, GH * (g + 1))
                for t in range(TT):
                    wait(pe, q_ev, TT * nq + t + 1)
                    last = transposes(mb[:, t, :], lambda c: oT[:, LB - 1 - c, t * P:(t + 1) * P])
                    last.then_inc(o_tr, 1)

            def normalised(g):
                for t in range(TT):
                    pe.wait_ge(t_nrm, TT * g + t + 1)
                    pe.wait_ge(x1_ok, TT * g + t + 1)
                    transposes(mb[:, t, :], lambda c: xn[:, t, c * P:(c + 1) * P]).then_inc(n_tr, 1)

            def router_waits(g):
                pe.wait_ge(lgT_ok, g + 1)
                pe.wait_ge(n_l, TT * g + TT)
                if not isinstance(g, int) or g < NG - 1:
                    pe.wait_ge(k_ev, TT * g + TT * 2)

            def router(g):
                at = SK[-1]
                for t in range(TT):
                    last = pe.transpose(mb[:, 1, t * E:(t + 1) * E], lgT[at:at + E, t * P:(t + 1) * P],
                                        ident[at:at + E, at:at + E])
                last.then_inc(lg_tr, 1)

            def gate_up(g, i):
                j = ORDER[i]
                if isinstance(g, int) and g == 0 and i == 0:
                    pe.wait_ge(sw_h, LB)
                    low_done(pe, 2)
                    low_done(pe, 3)
                pe.wait_ge(n_h, TT * g + TT)
                pe.wait_ge(n_l, TT * g + TT)
                if i < TT:
                    wait(pe, dn_ok, TT * (g - 1) + i + 1)
                else:
                    wait(pe, mid_ok, SJ * g + i - 1)
                if i == TT:
                    pe.wait_ge(lgT_ok, g + 1)
                for u in range(2):
                    m = SK[j] + (E if j == SJ - 1 and u == 0 else 0)
                    for c in range(LB):
                        for a, b in PASSES:
                            col = u * UP + j * P
                            last = pe.matmul(gu[0:m, i % 2, u * GT:(u + 1) * GT], sw[:, c, a, col:col + m],
                                             xT[:, c, b, :], start=(c == 0 and (a, b) == PASSES[0]),
                                             stop=(c == LB - 1 and (a, b) == PASSES[-1]))
                last.then_inc(gu_mm, 1)

            def down(g, tiles=range(TT)):
                last_chunk = isinstance(g, int) and g == NG - 1
                if isinstance(g, int) and g == 0:
                    pe.wait_ge(sw_h, SW_PIECES)
                    low_done(pe, SW_PIECES - 1)
                pe.wait_ge(mid_h, SJ * g + SJ - (1 if last_chunk else 0))
                pe.wait_ge(mid_l, (SJ - 1) * g + SJ - 1 - (1 if last_chunk else 0))
                pe.wait_ge(rest_l, g + 1)
                for t in tiles:
                    cols = slice(t * P, (t + 1) * P)
                    pe.matmul(gu[:, t, :], midh[0:2 * REST, SJ - 1, cols], sd[0:2 * REST, SJ - 1, 0, :],
                              start=True, stop=False)
                    pe.matmul(gu[:, t, :], midh[0:REST, SJ - 1, cols], sd[0:REST, SJ - 1, 1, :],
                              start=False, stop=False)
                    for j in range(SJ - 1):
                        if last_chunk and t == 0 and j == SJ - 2:
                            pe.wait_ge(mid_h, SJ * g + SJ)
                            pe.wait_ge(mid_l, (SJ - 1) * g + SJ - 1)
                        for a, b in PASSES:
                            last = pe.matmul(gu[:, t, :], (midh, midl)[a][:, j, cols], sd[:, j, b, :],
                                             start=False, stop=(j == SJ - 2 and (a, b) == PASSES[-1]))
                    last.then_inc(dn_mm, 1)

            def steps(g, prep, post, chunk):
                convolve(GH * g, 0)
                if post:
                    mixed_out(g - 1, g)
                if chunk:
                    down(g - 2)
                if post and chunk:
                    normalised(g - 1)
                convolve(GH * g + 1, 1)
                if post and not chunk:
                    normalised(g - 1)
                if prep:
                    prep_ctx(g + 1)
                if post:
                    gate_up(g - 1, 0)
                    gate_up(g - 1, 1)
                convolve(GH * g + 2, 2)
                if post:
                    router_waits(g - 1)
                    gate_up(g - 1, 2)
                    router(g - 1)
                    gate_up(g - 1, 3)
                if prep:
                    prep_q(g + 1)
                convolve(GH * g + 3, 3)
                if post:
                    gate_up(g - 1, 4)
                    gate_up(g - 1, 5)

            pe.wait_ge(consts, 2)
            prep_ctx(0)
            prep_q(0)
            convolve(0, 0)
            pe.wait_ge(gate_in, 16)
            pe.wait_ge(q_ev, TT)
            for c in range(LB):
                last = pe.transpose(mb[:, 0, c * E:(c + 1) * E], gate_rows[:, c * P:(c + 1) * P], ident[0:E, 0:E])
            last.then_inc(gate_t, 1)
            convolve(1, 1)
            pe.wait_ge(gate_h, 1)
            pe.wait_ge(gate_l, 1)
            prep_ctx(1)
            convolve(2, 2)
            convolve(3, 3)
            prep_q(1)
            steps(1, True, True, False)
            steps(2, True, True, True)
            with pe.Fori(3, NG - 1) as g:
                steps(g, True, True, True)
            steps(NG - 1, False, True, True)
            mixed_out(NG - 1, NG - 1)
            down(NG - 2)
            normalised(NG - 1)
            gate_up(NG - 1, 0)
            router_waits(NG - 1)
            router(NG - 1)
            for i in range(1, 3):
                gate_up(NG - 1, i)
            pe.wait_ge(rt_c, 1)
            for lhs, rhs in ((before_in_b, chosen_b), (same_b, excl_b), (earlier_b, tot_b)):
                last = pe.matmul(yb[:, 0, 0:TE], lhs[:], rhs[:], start=(lhs is before_in_b),
                                 stop=(lhs is earlier_b))
            last.then_inc(rt_mm, 1)
            for i in range(3, SJ):
                gate_up(NG - 1, i)

            def slots(e):
                pe.wait_ge(oh_ok, e + 1)
                wait(pe, sl_cp, e)
                for t in range(NT):
                    col = e * NT + t
                    last = pe.matmul(yb[:, 2, 0:HALVES * 6], onehot[:, t, :],
                                     VH[:, bass.ds(col, 1), :, :].rearrange("p a h c -> p (a h c)"),
                                     start=(t == 0), stop=(t == NT - 1))
                last.then_inc(sl_mm, 1)

            def rows_t(e, k):
                pe.wait_ge(rows_in[k], 16 * HALVES * ((e - k) // 2) + 16 * HALVES if isinstance(e, int)
                           else e * (8 * HALVES) + (16 - 8 * k) * HALVES)
                for h in range(HALVES):
                    wait(pe, g_l, HALVES * e - HALVES + h + 1)
                    transposes(yb[:, h, :], lambda c: xg[k][:, h, c * P:(c + 1) * P]).then_inc(g_tr, 1)

            def expert_gu(e, k, j):
                m = EK[j]
                if j == 0:
                    pe.wait_ge(ew_h, LB * e + LB)
                    pe.wait_ge(ew_l, LB * e + LB)
                    pe.wait_ge(g_h, HALVES * e + HALVES)
                    pe.wait_ge(g_l, HALVES * e + HALVES)
                if isinstance(e, int) and e == 0 and j < TT:
                    pe.wait_ge(dn_ok, TT * (NG - 1) + j + 1)
                wait(pe, e_mid, EJ * e - EJ + j + 1)
                for u in range(2):
                    for c in range(LB):
                        for a, b in PASSES:
                            col = u * I + j * P
                            last = pe.matmul(egu[j][0:m, u * CAP:(u + 1) * CAP], ew[k][:, c, a, col:col + m],
                                             xgT[k][:, c, b, :], start=(c == 0 and (a, b) == PASSES[0]),
                                             stop=(c == LB - 1 and (a, b) == PASSES[-1]))
                last.then_inc(e_mm, 1)

            def expert_down(e, k):
                pe.wait_ge(e_midh, EJ * e + EJ)
                pe.wait_ge(e_midl, EJ * e + EJ)
                pe.wait_ge(ed_h, e + 1)
                pe.wait_ge(ed_l, e + 1)
                for h in range(HALVES):
                    wait(pe, e_ok, HALVES * e - HALVES + h + 1)
                    for j in range(EJ):
                        for a, b in PASSES:
                            lhs = (midh, midl)[a]
                            last = pe.matmul(mb[:, h, :], lhs[0:EK[j], EJ * k + j, h * P:(h + 1) * P],
                                             ed[k][0:EK[j], j, b, :], start=(j == 0 and (a, b) == PASSES[0]),
                                             stop=(j == EJ - 1 and (a, b) == PASSES[-1]))
                    last.then_inc(e_dn, 1)

            def unit(e, k, before, next1, next2):
                expert_gu(e, k, 0)
                expert_gu(e, k, 1)
                if next2:
                    slots(e + 2)
                if next1:
                    rows_t(e + 1, 1 - k)
                else:
                    expert_gu(e, k, 2)
                if before:
                    expert_down(e - 1, 1 - k)
                if next1:
                    expert_gu(e, k, 2)

            slots(0)
            down(NG - 1, [0])
            slots(1)
            down(NG - 1, [1])
            rows_t(0, 0)
            unit(0, 0, False, True, True)
            unit(1, 1, True, True, True)
            with pe.Fori(1, E // 2 - 1) as i:
                unit(2 * i, 0, True, True, True)
                unit(2 * i + 1, 1, True, True, True)
            unit(E - 2, 0, True, True, False)
            unit(E - 1, 1, True, False, False)
            expert_down(E - 1, 1)

        @block.scalar
        def _(act):
            def split_shared(piece):
                s = piece % 2
                if piece < LB:
                    act.wait_ge(swraw_in[s], 32 * (piece // 2 + 1))
                    act.activation(sw[:, piece, 0, 0:IS], sw_raw[:, s, 0:IS], ACT.Copy)
                    act.activation(sw[:, piece, 0, UP:UP + IS], sw_raw[:, s, IS:2 * IS], ACT.Copy).then_inc(sw_h, 1)
                else:
                    act.wait_ge(sd_in[(piece - LB) % 2], 32 * ((piece - LB) // 2 + 1)
                                + (16 if piece == SW_PIECES - 1 else 0))
                    for h in range(2):
                        j = 2 * (piece - LB) + h
                        m = SK[j] if j < SJ - 1 else 2 * REST
                        last = act.activation(sd[0:m, j, 0, :], raw_down(piece)[0:m, h, :], ACT.Copy)
                    last.then_inc(sw_h, 1)

            def norm(dst, src, t, rs, nb, signal):
                act.activation(dst, src, ACT.Identity, bias=nb[:, t:t + 1], scale=rs[:, t:t + 1]).then_inc(signal, 1)

            def norm_q(g, tiles=range(TT)):
                act.wait_ge(x_rs, g + 1)
                for t in tiles:
                    wait(act, q_tr, TT * (g - 1) + t + 1)
                    norm(xq[:, t, ::-1], x_t[:, bass.ds(g % 3, 1), t, :].rearrange("p s l -> p (s l)"), t,
                         xrs, xnb, x_nrm)

            def norm_tokens(g):
                act.wait_ge(t_rs, g + 1)
                wait(act, n_tr, TT * g)
                wait(act, xn_out, 16 * TT * g)
                for t in range(TT):
                    norm(xn[:, t, :], x1[:, bass.ds(g % 2, 1), t, :].rearrange("p s l -> p (s l)"), t,
                         trs, tnb, t_nrm)

            def evacuate(dst, g, arrived, signal, free, free_at):
                for t in range(TT):
                    act.wait_ge(arrived, TT * g + t + 1)
                    wait(act, free, free_at)
                    tile = dst[:, bass.ds(g % 2, 1), :, t * P:(t + 1) * P].rearrange("p s c w -> p (s c) w")
                    act.activation(tile, mb[:, t, :].rearrange("p (c w) -> p c w", c=LB), ACT.Copy).then_inc(signal, 1)

            def round_kv(n, s):
                if isinstance(n, int) and n == 0:
                    act.wait_ge(kv0_m, 1)
                else:
                    act.wait_ge(kv_m, n)
                wait(act, conv, n - 1)
                act.activation(kvh[:, s, :, :], kv[:, s, :, :], ACT.Copy).then_inc(kv_h, 1)

            def silu(g, i):
                m = SK[ORDER[i]]
                act.wait_ge(gu_mm, SJ * g + i + 1)
                wait(act, mid_ok, SJ * g + max(i - 1, 0))
                act.activation(sil[0:m, i % 2, :], gu[0:m, i % 2, 0:GT], ACT.Silu).then_inc(sil_ok, 1)
                if i == 0:
                    wait(act, lg_tr, g)
                    act.activation(lgT[m:m + E, :], gu[m:m + E, 0, 0:GT], ACT.Copy).then_inc(lgT_ok, 1)

            def round_mid(g, i):
                j = ORDER[i]
                m = SK[j]
                act.wait_ge(mid_ok, SJ * g + i + 1)
                wait(act, dn_mm, TT * g)
                act.activation(midh[0:m, j, :], mid[0:m, i % 2, :], ACT.Copy).then_inc(mid_h, 1)

            def round_tokens(g):
                for t in range(TT):
                    act.wait_ge(n_tr, TT * g + t + 1)
                    wait(act, gu_mm, SJ * g)
                    act.activation(xT[:, :, 0, t * P:(t + 1) * P], mb[:, t, :].rearrange("p (c k) -> p c k", c=LB),
                                   ACT.Copy).then_inc(n_h, 1)

            def keep_scores(g):
                act.wait_ge(lg_tr, g + 1)
                act.activation(logits[:, bass.ds(g, 1), :].rearrange("p a e -> p (a e)"), mb[:, 1, 0:TT * E],
                               ACT.Copy).then_inc(lg_ok, 1)

            def exponents(i):
                tiles = ROUND[i]
                act.wait_ge(rt, i + 1)
                act.activation(scp[:, tiles, 0:E], rep[:, tiles, 0:E], ACT.Exp).then_inc(rt_exp, 1)

            def steps(g, prep, post, extra=()):
                for piece in extra[0:1]:
                    split_shared(piece)
                early = isinstance(g, int) and g == 1
                if not early:
                    round_kv(GH * g + 2, 0)
                if post:
                    norm_tokens(g - 1)
                    round_tokens(g - 1)
                if early:
                    round_kv(GH * g + 2, 0)
                if isinstance(g, int) and g == 0:
                    act.wait_ge(gate_t, 1)
                    act.activation(sw[:, :, 0, IS:UP], mb[:, 0, 0:LB * E].rearrange("p (c e) -> p c e", c=LB),
                                   ACT.Copy).then_inc(gate_h, 1)
                if not prep:
                    exponents(0)
                for piece in extra[1:2]:
                    split_shared(piece)
                if not early:
                    round_kv(GH * g + 3, 1)
                if prep:
                    evacuate(kT, g + 1, c_tr, k_ev, kv_m, GH * g - 1)
                if post:
                    for i in range(2):
                        silu(g - 1, i)
                        round_mid(g - 1, i)
                if early:
                    round_kv(GH * g + 3, 1)
                if prep and not early:
                    round_kv(GH * g + 4, 0)
                if prep:
                    norm_q(g + 1)
                if post:
                    keep_scores(g - 1)
                for piece in extra[2:3]:
                    if piece:
                        split_shared(piece)
                if post:
                    for i in range(2, 4):
                        silu(g - 1, i)
                        round_mid(g - 1, i)
                        if early and i == 2:
                            round_kv(GH * g + 4, 0)
                if prep:
                    evacuate(qT, g + 1, q_tr, q_ev, d_mul, GH * g)
                    round_kv(GH * g + 5, 1)
                for piece in extra[3:4]:
                    split_shared(piece)
                if post:
                    for i in range(4, 6):
                        silu(g - 1, i)
                        round_mid(g - 1, i)

            evacuate(kT, 0, c_tr, k_ev, c_tr, 0)
            norm_q(0, [0])
            round_kv(0, 0)
            norm_q(0, [1])
            evacuate(qT, 0, q_tr, q_ev, q_tr, 0)
            round_kv(1, 1)
            steps(0, True, False, (0, 1, 2, 3))
            steps(1, True, True, (4, 5, None, 6))
            steps(2, True, True)
            with act.Fori(3, NG - 1) as g:
                steps(g, True, True)
            steps(NG - 1, False, True)
            norm_tokens(NG - 1)
            round_tokens(NG - 1)
            silu(NG - 1, 0)
            keep_scores(NG - 1)
            exponents(1)

            def split_w(e, k, c):
                act.wait_ge(raw_in[k], 32 * ((e - k) // 2) + 32 if isinstance(e, int) else e * 16 + (32 - 16 * k))
                wait(act, e_mm, EJ * e - EJ)
                act.activation(ew[k][:, c, 0, :], raw_w[k][:, c, :], ACT.Copy).then_inc(ew_h, 1)

            def split_d(e, k):
                act.wait_ge(rawd_in[k], 32 * ((e - k) // 2) + 32 if isinstance(e, int) else e * 16 + (32 - 16 * k))
                wait(act, e_dn, HALVES * e - HALVES)
                act.activation(ed[k][:, 0:2, 0, :], raw_d[k][:, 0:2, :], ACT.Copy)
                act.activation(ed[k][0:EK[2], 2, 0, :], raw_d[k][0:EK[2], 2, :], ACT.Copy).then_inc(ed_h, 1)

            def weigh(e, k):
                if isinstance(e, int) and e == 0:
                    act.wait_ge(out_out, 16 * TT * NG)
                    act.wait_ge(xn_out, 16 * TT * NG)
                act.wait_ge(kept, e + 1)
                for h in range(HALVES):
                    act.wait_ge(e_dn, HALVES * e + h + 1)
                    wait(act, added, 16 * HALVES * (e - 1))
                    act.activation(weighed[k][:, h, :], mb[:, h, :], ACT.Copy, scale=wts_s[k][:, h:h + 1]).then_inc(e_ok, 1)

            def round_rows(e, k):
                for h in range(HALVES):
                    act.wait_ge(g_tr, HALVES * e + h + 1)
                    wait(act, e_mm, EJ * e - EJ)
                    act.activation(xgT[k][:, :, 0, h * P:(h + 1) * P],
                                   yb[:, h, :].rearrange("p (c n) -> p c n", c=LB), ACT.Copy).then_inc(g_h, 1)

            def e_silu(e, k, j):
                m, s = EK[j], (EJ * k + j) % 2
                act.wait_ge(e_mm, EJ * e + j + 1)
                wait(act, e_mid, EJ * e + j - 1)
                act.activation(sil[0:m, s, :], egu[j][0:m, 0:CAP], ACT.Silu).then_inc(e_sil, 1)

            def e_round(e, k, j):
                m, s = EK[j], (EJ * k + j) % 2
                act.wait_ge(e_mid, EJ * e + j + 1)
                wait(act, e_dn, HALVES * e - HALVES)
                act.activation(midh[0:m, EJ * k + j, :], mid[0:m, s, :], ACT.Copy).then_inc(e_midh, 1)

            def unit(e, k, before, next1):
                if before:
                    e_round(e - 1, 1 - k, 2)
                split_d(e, k)
                if next1 and not (isinstance(e, int) and e == 0):
                    for c in range(LB):
                        split_w(e + 1, 1 - k, c)
                e_silu(e, k, 0)
                e_round(e, k, 0)
                e_silu(e, k, 1)
                e_round(e, k, 1)
                if next1:
                    round_rows(e + 1, 1 - k)
                else:
                    e_silu(e, k, 2)
                    e_round(e, k, 2)
                if before:
                    weigh(e - 1, 1 - k)
                if next1:
                    e_silu(e, k, 2)

            for i in range(SJ):
                if i:
                    silu(NG - 1, i)
                round_mid(NG - 1, i)
                if i in (2, 3):
                    split_w(0, 0, i - 2)
            split_w(0, 0, 2)
            split_w(0, 0, 3)
            for c in range(LB):
                split_w(1, 1, c)
            act.wait_ge(gu_mm, SJ * NG)
            round_rows(0, 0)
            act.wait_ge(dn_mm, TT * NG)
            unit(0, 0, False, True)
            unit(1, 1, True, True)
            with act.Fori(1, E // 2 - 1) as i:
                unit(2 * i, 0, True, True)
                unit(2 * i + 1, 1, True, True)
            unit(E - 2, 0, True, True)
            unit(E - 1, 1, True, False)
            weigh(E - 1, 1)

        @block.gpsimd
        def _(pool):
            made = [0]

            def const(ins, after=True):
                ins.then_inc(consts, 1)
                made[0] += 1
                pool.wait_ge(consts, made[0])

            pool.memset(pad[:], 0.0).then_inc(pad_ok, 1)
            const(pool.memset(ident[:], 0.0))
            const(pool.affine_select(out=ident[:], in_=ident[:], compare_op=ALU.not_equal, fill=1.0, base=0,
                                     pattern=[[-1, P]], channel_multiplier=1))
            const(pool.memset(half_neg[:], -0.5))
            const(pool.iota(col_i[:], [[1, P]], base=0, channel_multiplier=0))
            const(pool.iota(colmod_i[:], [[0, TR], [1, B]], base=0, channel_multiplier=0))
            const(pool.iota(row_i[:, 0:1], [[0, 1]], base=0, channel_multiplier=1))
            const(pool.tensor_copy(iota_c[:], col_i[:]))
            const(pool.iota(tok_i[:], [[0, E], [TR, NT]], base=0, channel_multiplier=0))
            const(pool.memset(carrier[:], 0.0))
            assert made[0] == N_CONST

            def inverse(rs, nb, ve, nm, steps, ready, count, used, signal):
                pool.wait_ge(ready, count)
                wait(pool, used, TT * (count - 1))
                pool.tensor_tensor(rs[:], ve[:], half_neg[:], ALU.pow).then_inc(steps, 1)
                pool.wait_ge(steps, count)
                pool.tensor_tensor(nb[:], nm[:], rs[:], ALU.mult).then_inc(signal, 1)

            def inverse_x(g):
                inverse(xrs, xnb, xve, xnm, x_pow, x_stat, g + 1, x_nrm, x_rs)

            def inverse_t(g):
                inverse(trs, tnb, tve, tnm, t_pow, t_stat, g + 1, t_nrm, t_rs)

            def pairs(n, g, hl):
                s = hl % 2
                pool.wait_ge(k_ev, TT * g + TT)
                wait(pool, kv_h, n - 1)
                if isinstance(n, int) and n == 2:
                    pool.wait_ge(kv0_l, 1)
                else:
                    wait(pool, kv_l, n - 2)
                src = kT[:, bass.ds(g % 2, 1), :, hl * HD * B:(hl + 1) * HD * B].rearrange("p s c w -> p (s c) w")
                for d in range(HD):
                    w = (HD - d) * B
                    last = pool.tensor_tensor(kv[:, s, :, POFF[d]:POFF[d] + w], src[:, :, 0:w],
                                              src[:, :, d * B:HD * B], ALU.mult)
                last.then_inc(kv_m, 1)

            def low_kv(n, s):
                pool.wait_ge(kv_h, n + 1)
                wait(pool, conv, n - 1)
                pool.wait_ge(kv_m, n)
                pool.tensor_tensor(kvl[:, s, :, :], kv[:, s, :, :], kvh[:, s, :, :].bitcast(fp32), ALU.subtract)\
                    .then_inc(kv_l, 1)

            def low_mid(g, i):
                j = ORDER[i]
                m = SK[j]
                pool.wait_ge(mid_h, SJ * g + i + 1)
                wait(pool, dn_mm, TT * g)
                pool.tensor_tensor(midl[0:m, j, :], mid[0:m, i % 2, :], midh[0:m, j, :].bitcast(fp32), ALU.subtract)\
                    .then_inc(mid_l, 1)

            def split_shared(piece):
                pool.wait_ge(sw_h, piece + 1)
                for to, at in ((0, 0), (UP, IS)):
                    last = pool.tensor_tensor(sw[:, piece, 1, to:to + IS], sw_raw[:, piece % 2, at:at + IS],
                                              sw[:, piece, 0, to:to + IS].bitcast(fp32), ALU.subtract)
                last.then_inc(sw_lp, 1)

            def steps(g, prep, post, chunk):
                if chunk:
                    low_mid(g - 2, 4)
                    low_mid(g - 2, 5)
                if post and not chunk:
                    split_shared(3)
                    inverse_t(g - 1)
                pairs(GH * g + 2, g, 2)
                if post and chunk:
                    inverse_t(g - 1)
                low_kv(GH * g + 2, 0)
                pairs(GH * g + 3, g, 3)
                low_kv(GH * g + 3, 1)
                if isinstance(g, int) and g == 0:
                    split_shared(0)
                if prep and not (post and not chunk):
                    pairs(GH * g + 4, g + 1, 0)
                if post:
                    low_mid(g - 1, 1)
                if prep:
                    inverse_x(g + 1)
                    if post and not chunk:
                        pairs(GH * g + 4, g + 1, 0)
                    low_kv(GH * g + 4, 0)
                    pairs(GH * g + 5, g + 1, 1)
                if post:
                    low_mid(g - 1, 2)
                    low_mid(g - 1, 3)
                if prep:
                    low_kv(GH * g + 5, 1)

            inverse_x(0)
            pairs(1, 0, 1)
            low_kv(1, 1)
            steps(0, True, False, False)
            steps(1, True, True, False)
            steps(2, True, True, True)
            with pool.Fori(3, NG - 1) as g:
                steps(g, True, True, True)
            steps(NG - 1, False, True, True)
            low_mid(NG - 2, 4)
            low_mid(NG - 2, 5)
            inverse_t(NG - 1)
            pool.wait_ge(conv, H)
            pool.wait_ge(d_sum, H)
            pool.wait_ge(o_tr, TT * NG)
            pool.wait_ge(n_l, TT * NG)
            for k in range(2):
                pool.memset(xg[k][:], 0.0).then_inc(xg_zero, 1)
            pool.wait_ge(xg_zero, 2)

            def gather(e, k):
                pool.wait_ge(sl_ok, e + 1)
                wait(pool, g_tr, HALVES * e - HALVES)
                wait(pool, carried[0], e)
                pool.tensor_tensor(carrier[:, 0:1], carrier[:, 2:3], carrier[:, 2:3], ALU.mult)\
                    .then_inc(carried[0], 1)
                for h in range(HALVES):
                    pool.indirect_dma_start(xg[k][:, h, :], None, xn_dram,
                                            bass.IndirectOffsetOnAxis(idx_g[k][:, h:h + 1], 0),
                                            bounds_check=T - 1, oob_is_err=False).then_inc(rows_in[k], 16)

            def scatter(e, k):
                wait(pool, added, 16 * HALVES * e)
                if isinstance(e, int) and e == 0:
                    pool.wait_ge(out_out, 16 * TT * NG)
                for h in range(HALVES):
                    if isinstance(e, int):
                        pool.wait_ge(e_ok, HALVES * e + h + 1)
                    elif h == 0:
                        pool.wait_ge(e_ok, HALVES * e + HALVES)
                    if h == 0:
                        wait(pool, carried[1], e)
                        pool.tensor_tensor(carrier[:, 1:2], carrier[:, 2:3], carrier[:, 2:3], ALU.mult)\
                            .then_inc(carried[1], 1)
                    pool.indirect_dma_start(out_rows, bass.IndirectOffsetOnAxis(idx_s[k][:, h:h + 1], 0),
                                            weighed[k][:, h, :], None, bounds_check=T - 1, oob_is_err=False,
                                            compute_op=ALU.add).then_inc(added, 16)

            def low_d(e, k):
                pool.wait_ge(ed_h, e + 1)
                wait(pool, e_dn, HALVES * e - HALVES)
                pool.tensor_tensor(ed[k][:, 0:2, 1, :], raw_d[k][:, 0:2, :], ed[k][:, 0:2, 0, :].bitcast(fp32),
                                   ALU.subtract)
                pool.tensor_tensor(ed[k][0:EK[2], 2, 1, :], raw_d[k][0:EK[2], 2, :],
                                   ed[k][0:EK[2], 2, 0, :].bitcast(fp32), ALU.subtract).then_inc(ed_l, 1)

            def e_low(e, k, j):
                m, s = EK[j], (EJ * k + j) % 2
                pool.wait_ge(e_midh, EJ * e + j + 1)
                wait(pool, e_dn, HALVES * e - HALVES)
                pool.tensor_tensor(midl[0:m, EJ * k + j, :], mid[0:m, s, :],
                                   midh[0:m, EJ * k + j, :].bitcast(fp32), ALU.subtract).then_inc(e_midl, 1)

            def unit(e, k, before, next2):
                if before:
                    e_low(e - 1, 1 - k, 2)
                low_d(e, k)
                e_low(e, k, 0)
                e_low(e, k, 1)
                if next2:
                    gather(e + 2, k)
                if isinstance(e, int) and e == E - 1:
                    e_low(e, k, 2)
                if before:
                    scatter(e - 1, 1 - k)

            for i in range(1, SJ):
                low_mid(NG - 1, i)
            pool.wait_ge(xn_out, 16 * TT * NG)
            gather(0, 0)
            gather(1, 1)
            unit(0, 0, False, True)
            unit(1, 1, True, True)
            with pool.Fori(1, E // 2 - 1) as i:
                unit(2 * i, 0, True, True)
                unit(2 * i + 1, 1, True, True)
            unit(E - 2, 0, True, False)
            unit(E - 1, 1, True, False)
            scatter(E - 1, 1)
            pool.wait_ge(added, 16 * HALVES * E)

        @block.vector
        def _(dve):
            links = [0]

            def link(ins):
                links[0] += 1
                ins.then_inc(chain, 1)
                dve.wait_ge(chain, links[0])

            def split_shared(piece):
                s = piece % 2
                dve.wait_ge(sw_h, piece + 1)
                if piece < LB:
                    for to, at in ((0, 0), (UP, IS)):
                        last = dve.tensor_tensor(sw[:, piece, 1, to:to + IS], sw_raw[:, s, at:at + IS],
                                                 sw[:, piece, 0, to:to + IS].bitcast(fp32), ALU.subtract)
                    last.then_inc(sw_l, 1)
                else:
                    for h in range(2):
                        j = 2 * (piece - LB) + h
                        last = dve.tensor_tensor(sd[0:SK[j], j, 1, :], raw_down(piece)[0:SK[j], h, :],
                                                 sd[0:SK[j], j, 0, :].bitcast(fp32), ALU.subtract)
                    last.then_inc(sw_l, 1)

            def stats(tile, st, mv, ve, nm, signal):
                for t in range(TT):
                    dve.bn_stats(st[:, t, :], tile(t))
                dve.drain()
                for t in range(TT):
                    dve.bn_aggr(mv[:, t, :], st[:, t, :])
                dve.drain()
                dve.tensor_scalar(nm[:], mv[:, :, 0:1].rearrange("p t a -> p (t a)"), -1.0, None, ALU.mult)
                dve.tensor_scalar(ve[:], mv[:, :, 1:2].rearrange("p t a -> p (t a)"), EPS, None, ALU.add)\
                    .then_inc(signal, 1)

            def x_tile(g, t):
                return x_t[:, bass.ds(g % 3, 1), t, :].rearrange("p s l -> p (s l)")

            def x1_tile(g, t):
                return x1[:, bass.ds(g % 2, 1), t, :].rearrange("p s l -> p (s l)")

            def prep_stats(g):
                dve.wait_ge(x_in, 32 * g + 32)
                wait(dve, x_rs, g)
                dve.tensor_copy(carrier_d[:, 0:1], carrier_d[:, 1:2])
                stats(lambda t: x_tile(g, t), xstat, xmv, xve, xnm, x_stat)

            def multiply(n, g, hl):
                s = hl % 2
                dve.wait_ge(conv_half if by_halves(n) else conv, n + 1)
                dve.wait_ge(q_ev, TT * g + TT)
                wait(dve, d_sum, n - 1)
                q = qT[:, bass.ds(g % 2, 1), :, hl * HD * B:(hl + 1) * HD * B].rearrange("p s c w -> p (s c) w")

                def blocks(lo, hi):
                    for d in range(HD):
                        w = (HD - d) * B
                        last = dve.tensor_tensor(prod[:, s, lo:hi, d, d * B:HD * B],
                                                 yb[:, lo:hi, POFF[d]:POFF[d] + w], q[:, lo:hi, 0:w], ALU.mult)
                        if d:
                            last = dve.tensor_tensor(prod[:, s, lo:hi, HD - d, 0:w],
                                                     yb[:, lo:hi, POFF[d]:POFF[d] + w], q[:, lo:hi, d * B:HD * B],
                                                     ALU.mult)
                    return last

                if by_halves(n):
                    blocks(0, LB // 2).then_inc(d_half, 1)
                    dve.wait_ge(conv, n + 1)
                    blocks(LB // 2, LB).then_inc(d_mul, 1)
                else:
                    blocks(0, LB).then_inc(d_mul, 1)

            def add_up(n, g, hl):
                s = hl % 2
                dve.wait_ge(d_mul, n + 1)
                wait(dve, o_tr, TT * g)
                dve.tensor_reduce(oT[:, :, hl * HD * B:(hl + 1) * HD * B],
                                  prod[:, s, :, :, :].rearrange("p c i w -> p c w i"), AX.X, ALU.add)\
                    .then_inc(d_sum, 1)

            def add_x(g):
                for t in range(TT):
                    dve.wait_ge(o_tr, TT * g + t + 1)
                    wait(dve, dn_ok, TT * (g - 1))
                    dve.tensor_tensor(x1_tile(g, t), mb[:, t, ::-1], x_tile(g, t), ALU.add).then_inc(x1_ok, 1)
                dve.wait_ge(x1_ok, TT * g + TT)
                wait(dve, t_rs, g)
                dve.tensor_copy(carrier_d[:, 0:1], carrier_d[:, 1:2])
                stats(lambda t: x1_tile(g, t), tstat, tmv, tve, tnm, t_stat)

            def low_tokens(g):
                for t in range(TT):
                    dve.wait_ge(n_h, TT * g + t + 1)
                    wait(dve, gu_mm, SJ * g)
                    cols = slice(t * P, (t + 1) * P)
                    dve.tensor_tensor(xT[:, :, 1, cols], mb[:, t, :].rearrange("p (c n) -> p c n", c=LB),
                                      xT[:, :, 0, cols].bitcast(fp32), ALU.subtract).then_inc(n_l, 1)

            def middle(g, i):
                m = SK[ORDER[i]]
                dve.wait_ge(sil_ok, SJ * g + i + 1)
                wait(dve, mid_h, SJ * g + max(i - 1, 0))
                wait(dve, mid_l, (SJ - 1) * g + max(i - 2, 0))
                if i == 2:
                    dve.wait_ge(rest_l, g + 1)
                dve.tensor_tensor(mid[0:m, i % 2, :], sil[0:m, i % 2, :], gu[0:m, i % 2, GT:2 * GT], ALU.mult)\
                    .then_inc(mid_ok, 1)

            def low_rest(g):
                dve.wait_ge(mid_h, SJ * g + 1)
                wait(dve, dn_mm, TT * g)
                dve.tensor_tensor(midh[REST:2 * REST, SJ - 1, :], mid[0:REST, 0, :],
                                  midh[0:REST, SJ - 1, :].bitcast(fp32), ALU.subtract).then_inc(rest_l, 1)

            def chunk_sum(g, tiles=range(TT)):
                for t in tiles:
                    dve.wait_ge(dn_mm, TT * g + t + 1)
                    wait(dve, out_out, 16 * TT * g)
                    dve.tensor_tensor(yo[:, t, :], gu[:, t, :], x1_tile(g, t), ALU.add).then_inc(dn_ok, 1)

            def by_tile(t, tiles):
                return t[:].rearrange("p (e n) -> p n e", n=NT)[:, tiles, :]

            def width(tiles):
                return tiles.stop - tiles.start

            def scores(i):
                tiles = ROUND[i]
                dve.wait_ge(lg_ok, tiles.stop // TT)
                src = logits[:].rearrange("p g (t e) -> p (g t) e", e=E)[:, tiles, :]
                link(dve.tensor_reduce(r_max[:, tiles], src, AX.X, ALU.max))
                dve.tensor_tensor(rep[:, tiles, 0:E], src,
                                  r_max[:, tiles].unsqueeze(2).broadcast_to([P, width(tiles), E]),
                                  ALU.subtract).then_inc(rt, 1)

            def start_round_one():
                dve.wait_ge(c_tr, TT * NG)
                dve.wait_ge(q_tr, TT * NG)
                dve.wait_ge(kv_m, GH * (NG - 1) - 1)
                dve.memset(scp[:, :, E:PADW], -1.0)
                dve.memset(reset[:], 1.0)
                scores(0)

            def softmax(i):
                tiles = ROUND[i]
                dve.wait_ge(rt_exp, i + 1)
                link(dve.tensor_reduce(r_sum[:, tiles], scp[:, tiles, 0:E], AX.X, ALU.add))
                link(dve.reciprocal(r_rec[:, tiles], r_sum[:, tiles]))
                link(dve.tensor_tensor(rep[:, tiles, 0:E], scp[:, tiles, 0:E],
                                       r_rec[:, tiles].unsqueeze(2).broadcast_to([P, width(tiles), E]), ALU.mult))
                link(dve.tensor_copy(scp[:, tiles, 0:E], rep[:, tiles, 0:E]))

            def find(i):
                tiles = ROUND[i]
                for t in range(tiles.start, tiles.stop):
                    last = dve.max(top8[:, t, :], scp[:, t, :])
                link(last)

            def top(i):
                tiles = ROUND[i]
                link(dve.tensor_reduce(r_sum[:, tiles], top8[:, tiles, 0:TOPK], AX.X, ALU.add))
                dve.memset(top8[:, tiles, TOPK:8], -1.0)
                link(dve.tensor_scalar(r_sum[:, tiles], r_sum[:, tiles], 1e-20, None, ALU.add))
                for t in range(tiles.start, tiles.stop):
                    last = dve.match_replace(rep[:, t, :], top8[:, t, :], scp[:, t, :], -2.0)
                link(dve.reciprocal(r_rec[:, tiles], r_sum[:, tiles]))

            def choose(i):
                tiles = ROUND[i]
                link(dve.tensor_tensor(by_tile(chosen, tiles), rep[:, tiles, 0:E], scp[:, tiles, 0:E],
                                       ALU.not_equal))

            def weights(i):
                tiles = ROUND[i]
                w = by_tile(wt, tiles)
                part = lambda c: V[:, :, c:c + 1].rearrange("p (e n) a -> p n (e a)", n=NT)[:, tiles, :]
                link(dve.tensor_tensor(w, scp[:, tiles, 0:E],
                                       r_rec[:, tiles].unsqueeze(2).broadcast_to([P, width(tiles), E]), ALU.mult))
                if i == 0:
                    col = lambda c: V[:, :, c:c + 1].rearrange("p c a -> p (c a)")
                    dve.tensor_scalar(col(0), reset[:], 0.0, row_f[:, 1:2], ALU.mult, ALU.add)
                    dve.tensor_scalar(col(1), tok_i[:], row_f[:, 2:3], None, ALU.add)
                    dve.memset(col(2), 1.0)
                for c in range(3):
                    link(dve.tensor_copy(part(3 + c), w))
                    if c < 2:
                        link(dve.tensor_tensor(by_tile(wtmp, tiles), w, part(3 + c), ALU.subtract))
                        link(dve.tensor_copy(w, by_tile(wtmp, tiles)))

            def ranks():
                link(dve.memset(reset[:].rearrange("p (e n) -> p e n", n=NT)[:, :, 0:1], 0.0))
                dve.tensor_copy(chosen_b[:], chosen[:])
                link(dve.tensor_tensor_scan(run[:], reset[:], chosen[:], 0.0, ALU.mult, ALU.add))
                dve.tensor_tensor(excl_b[:], run[:], chosen[:], ALU.subtract)
                dve.tensor_copy(tot_b[:].rearrange("p (e n) -> p e n", n=NT),
                                run[:].rearrange("p (e n) -> p e n", n=NT)[:, :, NT - 1:NT]
                                .broadcast_to([P, E, NT])).then_inc(rt_c, 1)

            def places():
                dve.wait_ge(rt_mm, 1)
                link(dve.scalar_tensor_tensor(out=rank[:], in0=yb[:, 0, 0:TE], scalar=1.0, in1=chosen[:],
                                              op0=ALU.add, op1=ALU.mult))
                link(dve.tensor_scalar(rank[:], rank[:], -1.0, None, ALU.add))
                link(dve.tensor_scalar(wtmp[:], rank[:], float(P), None, ALU.is_ge))
                dve.scalar_tensor_tensor(out=rank_in[:], in0=wtmp[:], scalar=-float(P), in1=rank[:],
                                         op0=ALU.mult, op1=ALU.add)
                dve.scalar_tensor_tensor(out=in_half[:, 0, :], in0=rank[:], scalar=0.0, in1=wtmp[:],
                                         op0=ALU.is_ge, op1=ALU.subtract)
                link(dve.scalar_tensor_tensor(out=in_half[:, 1, :], in0=rank[:], scalar=float(CAP), in1=wtmp[:],
                                              op0=ALU.is_lt, op1=ALU.mult))

            def values(first, last):
                cols = slice(first * NT, last * NT)
                for h in range(HALVES):
                    end = dve.tensor_tensor(VH[:, cols, h, :], V[:, cols, :],
                                            in_half[:, h, cols].unsqueeze(2)
                                            .broadcast_to([P, cols.stop - cols.start, 6]), ALU.mult)
                link(end)

            def steps(g, prep, post, chunk, extra=()):
                if chunk:
                    add_x(g - 1)
                if not prep:
                    start_round_one()
                multiply(GH * g, g, 0)
                if post and not chunk:
                    add_x(g - 1)
                if chunk:
                    chunk_sum(g - 2, [0])
                add_up(GH * g, g, 0)
                if chunk:
                    chunk_sum(g - 2, [1])
                if isinstance(g, int) and g == 0:
                    dve.wait_ge(gate_h, 1)
                    dve.tensor_tensor(sw[:, :, 1, IS:UP], mb[:, 0, 0:LB * E].rearrange("p (c e) -> p c e", c=LB),
                                      sw[:, :, 0, IS:UP].bitcast(fp32), ALU.subtract).then_inc(gate_l, 1)
                if post:
                    low_tokens(g - 1)
                for piece in extra[0:1]:
                    if piece:
                        split_shared(piece)
                stats_at = 2 if isinstance(g, int) and g == 0 else 1
                for hl in range(1, GH):
                    multiply(GH * g + hl, g, hl)
                    if post:
                        middle(g - 1, 2 * hl - 2)
                    add_up(GH * g + hl, g, hl)
                    if post and hl == 1:
                        low_rest(g - 1)
                    if post:
                        middle(g - 1, 2 * hl - 1)
                    if prep and hl == stats_at:
                        prep_stats(g + 1)
                    for piece in extra[hl:hl + 1]:
                        if piece:
                            split_shared(piece)
                    if not prep and hl == 1:
                        softmax(0)
                        find(0)

            dve.memset(carrier_d[:], 0.0)
            dve.wait_ge(taps_in, 32)
            dve.wait_ge(pad_ok, 1)
            link(dve.tensor_copy(pad[:, 0:L], tap_rows[:, ::-1]))
            link(dve.tensor_tensor(pad[:, L - 1:L], pad[:, L - 1:L], skip_t[:], ALU.add))
            link(dve.tensor_copy(padhl[:, 0, :], pad[:]))
            dve.tensor_tensor(padhl[:, 1, :], pad[:], padhl[:, 0, :].bitcast(fp32), ALU.subtract).then_inc(taps_hl, 1)
            prep_stats(0)
            dve.wait_ge(k_ev, TT)
            for d in range(HD):
                w = (HD - d) * B
                last = dve.tensor_tensor(kv[:, 0, :, POFF[d]:POFF[d] + w], kT[:, 0, :, 0:w],
                                         kT[:, 0, :, d * B:HD * B], ALU.mult)
            last.then_inc(kv0_m, 1)
            dve.wait_ge(kv_h, 1)
            dve.tensor_tensor(kvl[:, 0, :, :], kv[:, 0, :, :], kvh[:, 0, :, :].bitcast(fp32), ALU.subtract)\
                .then_inc(kv0_l, 1)
            dve.wait_ge(consts, N_CONST)
            dve.tensor_scalar(row_i[:, 1:2], row_i[:, 0:1], B - 1, None, ALU.bitwise_and)
            link(dve.tensor_scalar(row_i[:, 2:3], row_i[:, 0:1], B.bit_length() - 1, None, ALU.logical_shift_right))
            link(dve.tensor_copy(row_f[:], row_i[:]))
            dve.tensor_scalar(later_row[:], col_i[:], row_f[:, 0:1], None, ALU.is_gt)
            dve.tensor_scalar(earlier_b[:], colmod_i[:], row_f[:, 1:2], None, ALU.is_gt)
            link(dve.tensor_scalar(same_b[:], colmod_i[:], row_f[:, 1:2], None, ALU.is_equal))
            link(dve.tensor_tensor(before_in_b[:], same_b[:], later_row[:], ALU.mult))
            steps(0, True, False, False, (None, None, None, 1))
            split_shared(2)
            steps(1, True, True, False, (4, 5, None, 6))
            steps(2, True, True, True)
            with dve.Fori(3, NG - 1) as g:
                steps(g, True, True, True)
            steps(NG - 1, False, True, True)
            add_x(NG - 1)
            top(0)
            choose(0)
            chunk_sum(NG - 2, [0])
            weights(0)
            low_tokens(NG - 1)
            chunk_sum(NG - 2, [1])

            def one_hot(e):
                wait(dve, sl_mm, e)
                for t in range(NT):
                    col = e * NT + t
                    last = dve.tensor_scalar(onehot[:, t, :], iota_c[:], rank_in[:, bass.ds(col, 1)], None,
                                             ALU.is_equal)
                last.then_inc(oh_ok, 1)

            def decode(e, k):
                dve.wait_ge(sl_mm, e + 1)
                wait(dve, rows_in[k], 16 * HALVES * ((e - k) // 2) if isinstance(e, int)
                     else e * (8 * HALVES) - 8 * k * HALVES)
                wait(dve, dec[2], e)
                dve.tensor_copy(slot_f[:], yb[:, 2, 0:6 * HALVES].rearrange("p (h c) -> p h c", c=6))\
                    .then_inc(sl_cp, 1)
                dve.wait_ge(sl_cp, e + 1)
                col = lambda i: slot_f[:, :, i:i + 1].rearrange("p h a -> p (h a)")
                dve.scalar_tensor_tensor(out=slot_a[:], in0=col(0), scalar=float(ROWS), in1=col(1),
                                         op0=ALU.mult, op1=ALU.add).then_inc(dec[0], 1)
                dve.tensor_reduce(wts_g[k][:], slot_f[:, :, 3:6], AX.X, ALU.add)
                dve.wait_ge(dec[0], e + 1)
                dve.scalar_tensor_tensor(out=slot_b[:], in0=col(2), scalar=-FAR, in1=slot_a[:],
                                         op0=ALU.mult, op1=ALU.add).then_inc(dec[1], 1)
                dve.wait_ge(dec[1], e + 1)
                dve.tensor_scalar(idx_g[k][:], slot_b[:], FAR, None, ALU.add).then_inc(sl_ok, 1)
                dve.engine_nop().then_inc(dec[2], 1)

            def keep_slots(e, k):
                wait(dve, added, 16 * HALVES * (e - 1) if isinstance(e, int) else e * (16 * HALVES) - 16 * HALVES)
                dve.wait_ge(sl_ok, e + 1)
                wait(dve, e_ok, HALVES * e - HALVES)
                dve.tensor_copy(idx_s[k][:], idx_g[k][:])
                dve.tensor_copy(wts_s[k][:], wts_g[k][:]).then_inc(kept, 1)

            def low_w(e, k, c):
                dve.wait_ge(ew_h, LB * e + c + 1)
                wait(dve, e_mm, EJ * e - EJ)
                dve.tensor_tensor(ew[k][:, c, 1, :], raw_w[k][:, c, :], ew[k][:, c, 0, :].bitcast(fp32),
                                  ALU.subtract).then_inc(ew_l, 1)

            def low_rows(e, k):
                for h in range(HALVES):
                    dve.wait_ge(g_h, HALVES * e + h + 1)
                    wait(dve, e_mm, EJ * e - EJ)
                    cols = slice(h * P, (h + 1) * P)
                    dve.tensor_tensor(xgT[k][:, :, 1, cols], yb[:, h, :].rearrange("p (c n) -> p c n", c=LB),
                                      xgT[k][:, :, 0, cols].bitcast(fp32), ALU.subtract).then_inc(g_l, 1)

            def e_middle(e, k, j):
                m, s = EK[j], (EJ * k + j) % 2
                dve.wait_ge(e_sil, EJ * e + j + 1)
                wait(dve, e_midh, EJ * e + j - 1)
                wait(dve, e_midl, EJ * e + j - 1)
                dve.tensor_tensor(mid[0:m, s, :], sil[0:m, s, :], egu[j][0:m, CAP:2 * CAP], ALU.mult)\
                    .then_inc(e_mid, 1)

            def unit(e, k, before, next1, next2):
                if before:
                    e_middle(e - 1, 1 - k, 2)
                if next2:
                    one_hot(e + 2)
                e_middle(e, k, 0)
                if next1 and not (isinstance(e, int) and e == 0):
                    low_w(e + 1, 1 - k, 0)
                    low_w(e + 1, 1 - k, 1)
                e_middle(e, k, 1)
                keep_slots(e, k)
                if next2:
                    decode(e + 2, k)
                if next1:
                    low_w(e + 1, 1 - k, 2)
                    low_rows(e + 1, 1 - k)
                    low_w(e + 1, 1 - k, 3)
                else:
                    e_middle(e, k, 2)
                if isinstance(e, int) and e == 0:
                    values(4, E)

            scores(1)
            middle(NG - 1, 0)
            softmax(1)
            low_rest(NG - 1)
            find(1)
            top(1)
            choose(1)
            middle(NG - 1, 1)
            ranks()
            middle(NG - 1, 2)
            weights(1)
            places()
            values(0, 2)
            middle(NG - 1, 3)
            one_hot(0)
            middle(NG - 1, 4)
            decode(0, 0)
            middle(NG - 1, 5)
            one_hot(1)
            for c in range(LB):
                low_w(0, 0, c)
            chunk_sum(NG - 1, [0])
            decode(1, 1)
            low_w(1, 1, 0)
            low_w(1, 1, 1)
            low_rows(0, 0)
            chunk_sum(NG - 1, [1])
            values(2, 4)
            unit(0, 0, False, True, True)
            unit(1, 1, True, True, True)
            with dve.Fori(1, E // 2 - 1) as i:
                unit(2 * i, 0, True, True, True)
                unit(2 * i + 1, 1, True, True, True)
            unit(E - 2, 0, True, True, False)
            unit(E - 1, 1, True, False, False)
            dve.wait_ge(e_ok, HALVES * E)


_INS = ['x', 'ctx_2048', 'L0_xattn_ssm_kernel', 'L0_xattn_D', 'L0_ffn_gate_w', 'L0_ffn_w_gate', 'L0_ffn_w_up',
        'L0_ffn_w_down', 'L0_ffn_sw_gate', 'L0_ffn_sw_up', 'L0_ffn_sw_down']
_OUTS = [((8, 256, 512), 'float32')]


def kernel(**inputs):
    import numpy as _np
    import concourse.bacc as _bacc
    from concourse import mybir as _mybir
    from concourse.bass_utils import run_bass_kernel_spmd as _run

    nc = _bacc.Bacc("TRN2", target_bir_lowering=False, num_devices=1)
    arrays, args = {}, []
    for name in _INS:
        a = _np.ascontiguousarray(inputs[name])
        arrays[f"in_{name}_dram"] = a
        args.append(nc.dram_tensor(f"in_{name}_dram", a.shape, _mybir.dt.from_np(a.dtype), kind="ExternalInput").ap())
    for i, (shape, dtype) in enumerate(_OUTS):
        dt = _mybir.dt.from_np(_np.dtype(dtype))
        args.append(nc.dram_tensor(f"out_{i}_dram", shape, dt, kind="ExternalOutput").ap())
    xattn_moe_kernel(nc, *args)
    r = _run(nc, [arrays], core_ids=[0])
    got = tuple(r.results[0][f"out_{i}_dram"] for i in range(len(_OUTS)))
    return got[0]
```
